# Optimizing a Trainium2 kernel written in Bass

```python
import numpy as np
import jax
import jax.numpy as jnp

def _softmax(x, axis=-1):
    return jax.nn.softmax(x, axis=axis)

def _gelu(x):
    return jax.nn.gelu(x, approximate=True)

def _silu(x):
    return jax.nn.silu(x)

def _sigmoid(x):
    return jax.nn.sigmoid(x)

def _layernorm(x, axis=-1, eps=1e-05):
    m = jnp.mean(x, axis=axis, keepdims=True)
    v = jnp.var(x, axis=axis, keepdims=True)
    return (x - m) / jnp.sqrt(v + eps)

def _scatter_add(tgt, idx, src, axis=0):
    return tgt.at[idx].add(src)

def _segment_sum(src, seg, n):
    return jax.ops.segment_sum(src, seg, n)
kernel_name = 'mk_xattn_ffn_d4_seqx_r4_4eba3b'

def setup_inputs(seed: int=0):
    np.random.seed(seed)
    _w = jnp.asarray

    def _rec_inputs():
        import jax
        import jax.numpy as jnp
        _rk = jax.random.key(seed)
        x = 7.22e-05 + 1 * jax.random.normal(jax.random.fold_in(_rk, 1), (4, 1024, 256), jnp.float32)
        _lenS = 1024 - jax.random.randint(jax.random.fold_in(_rk, 7), (4,), 0, max(1, 1024 // 4) + 1, jnp.int32)
        _lenS2 = 77 - jax.random.randint(jax.random.fold_in(_rk, 8), (4,), 0, max(1, 77 // 4) + 1, jnp.int32)
        _ctx_1024P = jax.random.normal(jax.random.fold_in(_rk, 11), (4, 16, 256), jnp.float32)
        _ctx_1024c = jax.random.dirichlet(jax.random.fold_in(_rk, 511), 0.3 * jnp.ones((16,), jnp.float32), (4, 77))
        _ctx_1024t = jnp.einsum('bsk,bkd->bsd', _ctx_1024c, _ctx_1024P)
        _ctx_1024t = _ctx_1024t * jax.lax.rsqrt(jnp.mean(jnp.square(_ctx_1024t)) + 1e-12) * 0.953939
        ctx_1024 = 4.13588e-05 + 0.999923 * (_ctx_1024t + 0.3 * jax.random.normal(jax.random.fold_in(_rk, 611), (4, 77, 256), jnp.float32))
        _validS = jnp.arange(1024)[None, :] < _lenS[:, None]
        _validS2 = jnp.arange(77)[None, :] < _lenS2[:, None]
        _causal = jnp.tril(jnp.ones((1024, 1024), dtype=bool))
        mask_BxS2_if0 = jnp.where(jnp.ones((4, 77), dtype=bool), 0, 1).astype(jnp.int32)
        mask_BxS2_ik0 = jnp.where(jnp.broadcast_to(_validS2[:, :], (4, 77)), 0, 1).astype(jnp.int32)
        return (x, ctx_1024, mask_BxS2_if0, mask_BxS2_ik0)
    x, ctx_1024, mask_BxS2_if0, mask_BxS2_ik0 = _rec_inputs()

    def _L0_xattn_setup():
        import jax, jax.numpy as jnp
        import numpy as np
        import math
        B, T, D = (2, 1024, 256)
        HD = D // 2
        DEPTH = 12
        LAMBDA_INIT = 0.8 - 0.6 * math.exp(-0.3 * DEPTH)
        SCALING = HD ** (-0.5)
        EPS = 1e-05
        key = jax.random.key(seed)
        ks = jax.random.split(key, 11)
        f32 = jnp.float32
        return {'q': jax.random.normal(ks[0], (B, T, D), f32), 'k': jax.random.normal(ks[1], (B, T, D), f32), 'v': jax.random.normal(ks[2], (B, T, D), f32), 'Wq': jax.random.normal(ks[3], (D, D), f32) * 0.02, 'Wk': jax.random.normal(ks[4], (HD, D), f32) * 0.02, 'Wv': jax.random.normal(ks[5], (D, D), f32) * 0.02, 'Wo': jax.random.normal(ks[6], (D, D), f32) * 0.02, 'lambda_q1': jax.random.normal(ks[7], (HD,), f32) * 0.1, 'lambda_k1': jax.random.normal(ks[8], (HD,), f32) * 0.1, 'lambda_q2': jax.random.normal(ks[9], (HD,), f32) * 0.1, 'lambda_k2': jax.random.normal(ks[10], (HD,), f32) * 0.1}
    _L0_xattn_all = _L0_xattn_setup()
    _L0_xattn_in = {k: v for k, v in _L0_xattn_all.items() if k in ('Wq', 'Wk', 'Wv', 'Wo', 'lambda_q1', 'lambda_k1', 'lambda_q2', 'lambda_k2')}
    del _L0_xattn_all

    def _L0_ffn_setup():
        import jax, jax.numpy as jnp
        import numpy as np
        N_HEAD = 16
        NUM_EXPERTS = 8
        TOP_K = 2
        LN_EPS = 1e-05

        def _layernorm(x, g, b):
            mu = jnp.mean(x, axis=-1, keepdims=True)
            var = jnp.mean(jnp.square(x - mu), axis=-1, keepdims=True)
            return (x - mu) * jax.lax.rsqrt(var + LN_EPS) * g + b

        def _attention(h, Wq, bq, Wk, bk, Wv, bv, Wp, bp):
            B, T, D = h.shape
            hd = D // N_HEAD

            def split(z):
                return z.reshape(B, T, N_HEAD, hd).transpose(0, 2, 1, 3)
            q = split(h @ Wq + bq)
            k = split(h @ Wk + bk)
            v = split(h @ Wv + bv)
            att = jnp.einsum('bhqd,bhkd->bhqk', q, k) / jnp.sqrt(jnp.float32(hd))
            causal = jnp.tril(jnp.ones((T, T), bool))
            att = jnp.where(causal, att, -jnp.inf)
            att = jax.nn.softmax(att, axis=-1)
            y = jnp.einsum('bhqk,bhkd->bhqd', att, v)
            y = y.transpose(0, 2, 1, 3).reshape(B, T, D)
            return y @ Wp + bp

        def _token_moe(h, gate_W, gate_b, exp_W1, exp_b1, exp_W2, exp_b2):
            B, T, D = h.shape
            flat = h.reshape(-1, D)
            N = flat.shape[0]
            logits = flat @ gate_W + gate_b
            top_v, top_i = jax.lax.top_k(logits, TOP_K)
            w = jax.nn.softmax(top_v, axis=-1)
            w_full = jnp.zeros((N, NUM_EXPERTS), flat.dtype)
            w_full = w_full.at[jnp.arange(N)[:, None], top_i].add(w)
            out = jnp.zeros_like(flat)
            for e in range(NUM_EXPERTS):
                mid = jax.nn.gelu(flat @ exp_W1[e] + exp_b1[e], approximate=False)
                y_e = mid @ exp_W2[e] + exp_b2[e]
                out = out + w_full[:, e:e + 1] * y_e
            return out.reshape(B, T, D)
        key = jax.random.key(seed)
        B, T, D = (8, 256, 256)
        H = 4 * D
        E = NUM_EXPERTS
        ks = jax.random.split(key, 24)
        s = 0.02
        inp = {'x': jax.random.normal(ks[0], (B, T, D), jnp.float32), 'ln1_g': jnp.ones((D,), jnp.float32), 'ln1_b': jnp.zeros((D,), jnp.float32), 'ln2_g': jnp.ones((D,), jnp.float32), 'ln2_b': jnp.zeros((D,), jnp.float32), 'Wq': jax.random.normal(ks[1], (D, D), jnp.float32) * s, 'bq': jnp.zeros((D,), jnp.float32), 'Wk': jax.random.normal(ks[2], (D, D), jnp.float32) * s, 'bk': jnp.zeros((D,), jnp.float32), 'Wv': jax.random.normal(ks[3], (D, D), jnp.float32) * s, 'bv': jnp.zeros((D,), jnp.float32), 'Wp': jax.random.normal(ks[4], (D, D), jnp.float32) * s, 'bp': jnp.zeros((D,), jnp.float32), 'gate_W': jax.random.normal(ks[5], (D, E), jnp.float32) * s, 'gate_b': jnp.zeros((E,), jnp.float32), 'exp_W1': jax.random.normal(ks[6], (E, D, H), jnp.float32) * s, 'exp_b1': jnp.zeros((E, H), jnp.float32), 'exp_W2': jax.random.normal(ks[7], (E, H, D), jnp.float32) * s, 'exp_b2': jnp.zeros((E, D), jnp.float32)}
        return inp
    _L0_ffn_all = _L0_ffn_setup()
    _L0_ffn_in = {k: v for k, v in _L0_ffn_all.items() if k in ('ln1_g', 'ln1_b', 'ln2_g', 'ln2_b', 'Wq', 'bq', 'Wk', 'bk', 'Wv', 'bv', 'Wp', 'bp', 'gate_W', 'gate_b', 'exp_W1', 'exp_b1', 'exp_W2', 'exp_b2')}
    del _L0_ffn_all

    def _L1_xattn_setup():
        import jax, jax.numpy as jnp
        import numpy as np
        DIM = 256
        HEADS = 16
        HEAD_DIM = DIM // HEADS
        B, NQ, NK = (2, 512, 512)
        key = jax.random.key(seed)
        ks = jax.random.split(key, 8)
        s = 1.0 / np.sqrt(DIM)
        return {'query': jax.random.normal(ks[0], (B, NQ, DIM), jnp.float32), 'key': jax.random.normal(ks[1], (B, NK, DIM), jnp.float32), 'value': jax.random.normal(ks[2], (B, NK, DIM), jnp.float32), 'qpos': jnp.zeros((B, NQ), jnp.int32), 'kpos': jnp.zeros((B, NK), jnp.int32), 'Wq': jax.random.normal(ks[3], (DIM, DIM), jnp.float32) * s, 'Wk': jax.random.normal(ks[4], (DIM, DIM), jnp.float32) * s, 'Wv': jax.random.normal(ks[5], (DIM, DIM), jnp.float32) * s, 'Wo': jax.random.normal(ks[6], (DIM, DIM), jnp.float32) * s, 'bo': jax.random.normal(ks[7], (DIM,), jnp.float32) * s}
    _L1_xattn_all = _L1_xattn_setup()
    _L1_xattn_in = {k: v for k, v in _L1_xattn_all.items() if k in ('Wq', 'Wk', 'Wv', 'Wo', 'bo')}
    del _L1_xattn_all

    def _L1_ffn_setup():
        import jax, jax.numpy as jnp
        import numpy as np
        QB = 127.0
        EPS = 1e-05

        def _ste(x, q):
            return x + jax.lax.stop_gradient(q - x)

        def bitlinear(x, W, b):
            w_scale = jnp.clip(jnp.mean(jnp.abs(W)), EPS, None)
            Wq = _ste(W, jnp.clip(jnp.round(W / w_scale), -1.0, 1.0) * w_scale)
            x_scale = jnp.clip(jnp.max(jnp.abs(x), axis=-1, keepdims=True), EPS, None)
            xq = _ste(x, jnp.clip(jnp.round(x * (QB / x_scale)), -QB - 1.0, QB) * (x_scale / QB))
            return jnp.einsum('bnd,hd->bnh', xq, Wq) + b
        key = jax.random.key(seed)
        k0, k1, k2 = jax.random.split(key, 3)
        B, N, D = (8, 1024, 256)
        H = int(D * 4.0)
        x = jax.random.normal(k0, (B, N, D), dtype=jnp.float32)
        W1 = jax.random.normal(k1, (H, D), dtype=jnp.float32) * 0.02
        b1 = jnp.zeros((H,), dtype=jnp.float32)
        W2 = jax.random.normal(k2, (D, H), dtype=jnp.float32) * 0.02
        b2 = jnp.zeros((D,), dtype=jnp.float32)
        return {'x': x, 'W1': W1, 'b1': b1, 'W2': W2, 'b2': b2}
    _L1_ffn_all = _L1_ffn_setup()
    _L1_ffn_in = {k: v for k, v in _L1_ffn_all.items() if k in ('W1', 'b1', 'W2', 'b2')}
    del _L1_ffn_all

    def _L2_xattn_setup():
        import jax, jax.numpy as jnp
        import numpy as np
        DIM = 256
        NUM_HEADS = 16
        HEAD_DIM = DIM // NUM_HEADS
        key = jax.random.key(seed)
        ks = jax.random.split(key, 11)
        B, N, C = (2, 512, DIM)
        s = 1.0 / np.sqrt(C)
        inp = {'q': jax.random.normal(ks[0], (B, N, C), jnp.float32), 'k': jax.random.normal(ks[1], (B, N, C), jnp.float32), 'v': jax.random.normal(ks[2], (B, N, C), jnp.float32), 'Wq': jax.random.normal(ks[3], (C, C), jnp.float32) * s, 'bq': jnp.zeros((C,), jnp.float32), 'Wk': jax.random.normal(ks[4], (C, C), jnp.float32) * s, 'bk': jnp.zeros((C,), jnp.float32), 'Wv': jax.random.normal(ks[5], (C, C), jnp.float32) * s, 'bv': jnp.zeros((C,), jnp.float32), 'Wo': jax.random.normal(ks[6], (C, C), jnp.float32) * s, 'bo': jnp.zeros((C,), jnp.float32)}
        return inp
    _L2_xattn_all = _L2_xattn_setup()
    _L2_xattn_in = {k: v for k, v in _L2_xattn_all.items() if k in ('Wq', 'bq', 'Wk', 'bk', 'Wv', 'bv', 'Wo', 'bo')}
    del _L2_xattn_all

    def _L2_ffn_setup():
        import jax, jax.numpy as jnp
        import numpy as np
        D_MODEL = 256
        EXPANSION = 4
        D_HIDDEN = D_MODEL * EXPANSION
        NUM_STAGES = int(np.log2(D_HIDDEN))

        def butterfly(y, weights, dim):
            lead = y.shape[:-1]
            for stage in range(weights.shape[0]):
                s = 2 ** stage
                nb = dim // (2 * s)
                yr = y.reshape(*lead, nb, 2, s)
                a = yr[..., 0, :]
                b = yr[..., 1, :]
                w = weights[stage].reshape(nb, s, 2, 2)
                na = w[..., 0, 0] * a + w[..., 0, 1] * b
                nb2 = w[..., 1, 0] * a + w[..., 1, 1] * b
                y = jnp.stack([na, nb2], axis=-2).reshape(*lead, dim)
            return y
        key = jax.random.key(seed)
        ks = jax.random.split(key, 6)
        B, S = (4, 512)
        x = jax.random.normal(ks[0], (B, S, D_MODEL), jnp.float32)
        W_exp = jax.random.normal(ks[1], (D_MODEL, D_HIDDEN), jnp.float32) * 0.02
        b_exp = jnp.zeros((D_HIDDEN,), jnp.float32)
        up_weights = jax.random.normal(ks[2], (NUM_STAGES, D_HIDDEN // 2, 2, 2), jnp.float32) * 0.02
        up_bias = jnp.zeros((D_HIDDEN,), jnp.float32)
        down_weights = jax.random.normal(ks[3], (NUM_STAGES, D_HIDDEN // 2, 2, 2), jnp.float32) * 0.02
        W_con = jax.random.normal(ks[4], (D_HIDDEN, D_MODEL), jnp.float32) * 0.02
        b_con = jnp.zeros((D_MODEL,), jnp.float32)
        down_bias = jnp.zeros((D_MODEL,), jnp.float32)
        return dict(x=x, W_exp=W_exp, b_exp=b_exp, up_weights=up_weights, up_bias=up_bias, down_weights=down_weights, W_con=W_con, b_con=b_con, down_bias=down_bias)
    _L2_ffn_all = _L2_ffn_setup()
    _L2_ffn_in = {k: v for k, v in _L2_ffn_all.items() if k in ('W_exp', 'b_exp', 'up_weights', 'up_bias', 'down_weights', 'W_con', 'b_con', 'down_bias')}
    del _L2_ffn_all

    def _L3_xattn_setup():
        import jax, jax.numpy as jnp
        import numpy as np
        B, LQ, LK, D = (4, 512, 512, 256)
        H = 16
        HD = D // H

        def _split_heads(x):
            b, l, _ = x.shape
            return x.reshape(b, l, H, HD).transpose(0, 2, 1, 3)
        key = jax.random.key(seed)
        ks = jax.random.split(key, 10)
        s = 0.02
        return {'hidden_states': jax.random.normal(ks[0], (B, LQ, D), jnp.float32), 'context': jax.random.normal(ks[1], (B, LK, D), jnp.float32), 'attention_mask': jax.random.randint(ks[2], (B, LK), 0, 2, jnp.int32), 'q_w': jax.random.normal(ks[3], (D, D), jnp.float32) * s, 'q_b': jnp.zeros((D,), jnp.float32), 'k_w': jax.random.normal(ks[4], (D, D), jnp.float32) * s, 'k_b': jnp.zeros((D,), jnp.float32), 'v_w': jax.random.normal(ks[5], (D, D), jnp.float32) * s, 'v_b': jnp.zeros((D,), jnp.float32)}
    _L3_xattn_all = _L3_xattn_setup()
    _L3_xattn_in = {k: v for k, v in _L3_xattn_all.items() if k in ('q_w', 'q_b', 'k_w', 'k_b', 'v_w', 'v_b')}
    del _L3_xattn_all

    def _L3_ffn_setup():
        import jax, jax.numpy as jnp
        import numpy as np
        N_HEAD, N_ACTIVE, D_MODEL, D_ATTN = (16, 4, 256, 64)
        key = jax.random.key(seed)
        ks = jax.random.split(key, 12)
        s = 0.02
        B, S = (2, 1024)
        return {'x': jax.random.normal(ks[0], (B, S, D_MODEL), dtype=jnp.float32), 'Wq': jax.random.normal(ks[1], (D_MODEL, N_HEAD * D_ATTN), dtype=jnp.float32) * s, 'bq': jnp.zeros((N_HEAD * D_ATTN,), dtype=jnp.float32), 'Wk': jax.random.normal(ks[2], (D_MODEL, N_HEAD * D_ATTN), dtype=jnp.float32) * s, 'bk': jnp.zeros((N_HEAD * D_ATTN,), dtype=jnp.float32), 'Wv': jax.random.normal(ks[3], (D_MODEL, N_HEAD * D_ATTN), dtype=jnp.float32) * s, 'bv': jnp.zeros((N_HEAD * D_ATTN,), dtype=jnp.float32), 'Wr': jax.random.normal(ks[4], (D_MODEL, N_HEAD), dtype=jnp.float32) * s, 'br': jnp.zeros((N_HEAD,), dtype=jnp.float32), 'Wo': jax.random.normal(ks[5], (N_ACTIVE * D_ATTN, D_MODEL), dtype=jnp.float32) * s, 'bo': jnp.zeros((D_MODEL,), dtype=jnp.float32)}
    _L3_ffn_all = _L3_ffn_setup()
    _L3_ffn_in = {k: v for k, v in _L3_ffn_all.items() if k in ('Wq', 'bq', 'Wk', 'bk', 'Wv', 'bv', 'Wr', 'br', 'Wo', 'bo')}
    del _L3_ffn_all
    return {'x': x, 'ctx_1024': ctx_1024, 'mask_BxS2_if0': mask_BxS2_if0, 'mask_BxS2_ik0': mask_BxS2_ik0, 'L0_xattn_Wq': _L0_xattn_in['Wq'], 'L0_xattn_Wk': _L0_xattn_in['Wk'], 'L0_xattn_Wv': _L0_xattn_in['Wv'], 'L0_xattn_Wo': _L0_xattn_in['Wo'], 'L0_xattn_lambda_q1': _L0_xattn_in['lambda_q1'], 'L0_xattn_lambda_k1': _L0_xattn_in['lambda_k1'], 'L0_xattn_lambda_q2': _L0_xattn_in['lambda_q2'], 'L0_xattn_lambda_k2': _L0_xattn_in['lambda_k2'], 'L0_ffn_ln1_g': _L0_ffn_in['ln1_g'], 'L0_ffn_ln1_b': _L0_ffn_in['ln1_b'], 'L0_ffn_ln2_g': _L0_ffn_in['ln2_g'], 'L0_ffn_ln2_b': _L0_ffn_in['ln2_b'], 'L0_ffn_Wq': _L0_ffn_in['Wq'], 'L0_ffn_bq': _L0_ffn_in['bq'], 'L0_ffn_Wk': _L0_ffn_in['Wk'], 'L0_ffn_bk': _L0_ffn_in['bk'], 'L0_ffn_Wv': _L0_ffn_in['Wv'], 'L0_ffn_bv': _L0_ffn_in['bv'], 'L0_ffn_Wp': _L0_ffn_in['Wp'], 'L0_ffn_bp': _L0_ffn_in['bp'], 'L0_ffn_gate_W': _L0_ffn_in['gate_W'], 'L0_ffn_gate_b': _L0_ffn_in['gate_b'], 'L0_ffn_exp_W1': _L0_ffn_in['exp_W1'], 'L0_ffn_exp_b1': _L0_ffn_in['exp_b1'], 'L0_ffn_exp_W2': _L0_ffn_in['exp_W2'], 'L0_ffn_exp_b2': _L0_ffn_in['exp_b2'], 'L1_xattn_Wq': _L1_xattn_in['Wq'], 'L1_xattn_Wk': _L1_xattn_in['Wk'], 'L1_xattn_Wv': _L1_xattn_in['Wv'], 'L1_xattn_Wo': _L1_xattn_in['Wo'], 'L1_xattn_bo': _L1_xattn_in['bo'], 'L1_ffn_W1': _L1_ffn_in['W1'], 'L1_ffn_b1': _L1_ffn_in['b1'], 'L1_ffn_W2': _L1_ffn_in['W2'], 'L1_ffn_b2': _L1_ffn_in['b2'], 'L2_xattn_Wq': _L2_xattn_in['Wq'], 'L2_xattn_bq': _L2_xattn_in['bq'], 'L2_xattn_Wk': _L2_xattn_in['Wk'], 'L2_xattn_bk': _L2_xattn_in['bk'], 'L2_xattn_Wv': _L2_xattn_in['Wv'], 'L2_xattn_bv': _L2_xattn_in['bv'], 'L2_xattn_Wo': _L2_xattn_in['Wo'], 'L2_xattn_bo': _L2_xattn_in['bo'], 'L2_ffn_W_exp': _L2_ffn_in['W_exp'], 'L2_ffn_b_exp': _L2_ffn_in['b_exp'], 'L2_ffn_up_weights': _L2_ffn_in['up_weights'], 'L2_ffn_up_bias': _L2_ffn_in['up_bias'], 'L2_ffn_down_weights': _L2_ffn_in['down_weights'], 'L2_ffn_W_con': _L2_ffn_in['W_con'], 'L2_ffn_b_con': _L2_ffn_in['b_con'], 'L2_ffn_down_bias': _L2_ffn_in['down_bias'], 'L3_xattn_q_w': _L3_xattn_in['q_w'], 'L3_xattn_q_b': _L3_xattn_in['q_b'], 'L3_xattn_k_w': _L3_xattn_in['k_w'], 'L3_xattn_k_b': _L3_xattn_in['k_b'], 'L3_xattn_v_w': _L3_xattn_in['v_w'], 'L3_xattn_v_b': _L3_xattn_in['v_b'], 'L3_ffn_Wq': _L3_ffn_in['Wq'], 'L3_ffn_bq': _L3_ffn_in['bq'], 'L3_ffn_Wk': _L3_ffn_in['Wk'], 'L3_ffn_bk': _L3_ffn_in['bk'], 'L3_ffn_Wv': _L3_ffn_in['Wv'], 'L3_ffn_bv': _L3_ffn_in['bv'], 'L3_ffn_Wr': _L3_ffn_in['Wr'], 'L3_ffn_br': _L3_ffn_in['br'], 'L3_ffn_Wo': _L3_ffn_in['Wo'], 'L3_ffn_bo': _L3_ffn_in['bo']}

def reference(x, ctx_1024, mask_BxS2_if0, mask_BxS2_ik0, L0_xattn_Wq, L0_xattn_Wk, L0_xattn_Wv, L0_xattn_Wo, L0_xattn_lambda_q1, L0_xattn_lambda_k1, L0_xattn_lambda_q2, L0_xattn_lambda_k2, L0_ffn_ln1_g, L0_ffn_ln1_b, L0_ffn_ln2_g, L0_ffn_ln2_b, L0_ffn_Wq, L0_ffn_bq, L0_ffn_Wk, L0_ffn_bk, L0_ffn_Wv, L0_ffn_bv, L0_ffn_Wp, L0_ffn_bp, L0_ffn_gate_W, L0_ffn_gate_b, L0_ffn_exp_W1, L0_ffn_exp_b1, L0_ffn_exp_W2, L0_ffn_exp_b2, L1_xattn_Wq, L1_xattn_Wk, L1_xattn_Wv, L1_xattn_Wo, L1_xattn_bo, L1_ffn_W1, L1_ffn_b1, L1_ffn_W2, L1_ffn_b2, L2_xattn_Wq, L2_xattn_bq, L2_xattn_Wk, L2_xattn_bk, L2_xattn_Wv, L2_xattn_bv, L2_xattn_Wo, L2_xattn_bo, L2_ffn_W_exp, L2_ffn_b_exp, L2_ffn_up_weights, L2_ffn_up_bias, L2_ffn_down_weights, L2_ffn_W_con, L2_ffn_b_con, L2_ffn_down_bias, L3_xattn_q_w, L3_xattn_q_b, L3_xattn_k_w, L3_xattn_k_b, L3_xattn_v_w, L3_xattn_v_b, L3_ffn_Wq, L3_ffn_bq, L3_ffn_Wk, L3_ffn_bk, L3_ffn_Wv, L3_ffn_bv, L3_ffn_Wr, L3_ffn_br, L3_ffn_Wo, L3_ffn_bo):
    import jax
    import jax.numpy as jnp

    def _L0_xattn_ref(q, k, v, Wq, Wk, Wv, Wo, lambda_q1, lambda_k1, lambda_q2, lambda_k2):
        import jax, jax.numpy as jnp
        import numpy as np
        import math
        B, T, D = (2, 1024, 256)
        HD = D // 2
        DEPTH = 12
        LAMBDA_INIT = 0.8 - 0.6 * math.exp(-0.3 * DEPTH)
        SCALING = HD ** (-0.5)
        EPS = 1e-05
        b, t, d = q.shape
        s = k.shape[1]
        qp = (q @ Wq.T).reshape(b, t, 2, HD).transpose(0, 2, 1, 3) * SCALING
        kp = k @ Wk.T
        scores = jnp.einsum('bhtd,bsd->bhts', qp, kp)
        scores = jax.nn.softmax(scores.astype(jnp.float32), axis=-1).astype(qp.dtype)
        lam1 = jnp.exp(jnp.sum(lambda_q1 * lambda_k1))
        lam2 = jnp.exp(jnp.sum(lambda_q2 * lambda_k2))
        lam = lam1 - lam2 + LAMBDA_INIT
        attn_w = scores[:, 0] - lam * scores[:, 1]
        vp = v @ Wv.T
        attn = jnp.einsum('bts,bsd->btd', attn_w, vp)
        rms = jax.lax.rsqrt(jnp.mean(jnp.square(attn), axis=-1, keepdims=True) + EPS)
        attn = attn * rms * (1.0 - LAMBDA_INIT)
        return attn @ Wo.T

    def _L0_ffn_ref(x, ln1_g, ln1_b, ln2_g, ln2_b, Wq, bq, Wk, bk, Wv, bv, Wp, bp, gate_W, gate_b, exp_W1, exp_b1, exp_W2, exp_b2):
        import jax, jax.numpy as jnp
        import numpy as np
        N_HEAD = 16
        NUM_EXPERTS = 8
        TOP_K = 2
        LN_EPS = 1e-05

        def _layernorm(x, g, b):
            mu = jnp.mean(x, axis=-1, keepdims=True)
            var = jnp.mean(jnp.square(x - mu), axis=-1, keepdims=True)
            return (x - mu) * jax.lax.rsqrt(var + LN_EPS) * g + b

        def _attention(h, Wq, bq, Wk, bk, Wv, bv, Wp, bp):
            B, T, D = h.shape
            hd = D // N_HEAD

            def split(z):
                return z.reshape(B, T, N_HEAD, hd).transpose(0, 2, 1, 3)
            q = split(h @ Wq + bq)
            k = split(h @ Wk + bk)
            v = split(h @ Wv + bv)
            att = jnp.einsum('bhqd,bhkd->bhqk', q, k) / jnp.sqrt(jnp.float32(hd))
            causal = jnp.tril(jnp.ones((T, T), bool))
            att = jnp.where(causal, att, -jnp.inf)
            att = jax.nn.softmax(att, axis=-1)
            y = jnp.einsum('bhqk,bhkd->bhqd', att, v)
            y = y.transpose(0, 2, 1, 3).reshape(B, T, D)
            return y @ Wp + bp

        def _token_moe(h, gate_W, gate_b, exp_W1, exp_b1, exp_W2, exp_b2):
            B, T, D = h.shape
            flat = h.reshape(-1, D)
            N = flat.shape[0]
            logits = flat @ gate_W + gate_b
            top_v, top_i = jax.lax.top_k(logits, TOP_K)
            w = jax.nn.softmax(top_v, axis=-1)
            w_full = jnp.zeros((N, NUM_EXPERTS), flat.dtype)
            w_full = w_full.at[jnp.arange(N)[:, None], top_i].add(w)
            out = jnp.zeros_like(flat)
            for e in range(NUM_EXPERTS):
                mid = jax.nn.gelu(flat @ exp_W1[e] + exp_b1[e], approximate=False)
                y_e = mid @ exp_W2[e] + exp_b2[e]
                out = out + w_full[:, e:e + 1] * y_e
            return out.reshape(B, T, D)
        x = x + _attention(_layernorm(x, ln1_g, ln1_b), Wq, bq, Wk, bk, Wv, bv, Wp, bp)
        x = x + _token_moe(_layernorm(x, ln2_g, ln2_b), gate_W, gate_b, exp_W1, exp_b1, exp_W2, exp_b2)
        return x

    def _L1_xattn_ref(query, key, value, qpos, kpos, Wq, Wk, Wv, Wo, bo):
        import jax, jax.numpy as jnp
        import numpy as np
        DIM = 256
        HEADS = 16
        HEAD_DIM = DIM // HEADS
        B, NQ, NK = (2, 512, 512)
        Bq, Nq, C = query.shape
        Nk = key.shape[1]
        scale = HEAD_DIM ** (-0.5)
        q = (query @ Wq.T).reshape(Bq, Nq, HEADS, HEAD_DIM).transpose(0, 2, 1, 3)
        k = (key @ Wk.T).reshape(Bq, Nk, HEADS, HEAD_DIM).transpose(0, 2, 1, 3)
        v = (value @ Wv.T).reshape(Bq, Nk, HEADS, HEAD_DIM).transpose(0, 2, 1, 3)
        attn = jnp.einsum('bhqd,bhkd->bhqk', q, k) * scale
        attn = jax.nn.softmax(attn, axis=-1)
        x = jnp.einsum('bhqk,bhkd->bhqd', attn, v)
        x = x.transpose(0, 2, 1, 3).reshape(Bq, Nq, C)
        return x @ Wo.T + bo

    def _L1_ffn_ref(x, W1, b1, W2, b2):
        import jax, jax.numpy as jnp
        import numpy as np
        QB = 127.0
        EPS = 1e-05

        def _ste(x, q):
            return x + jax.lax.stop_gradient(q - x)

        def bitlinear(x, W, b):
            w_scale = jnp.clip(jnp.mean(jnp.abs(W)), EPS, None)
            Wq = _ste(W, jnp.clip(jnp.round(W / w_scale), -1.0, 1.0) * w_scale)
            x_scale = jnp.clip(jnp.max(jnp.abs(x), axis=-1, keepdims=True), EPS, None)
            xq = _ste(x, jnp.clip(jnp.round(x * (QB / x_scale)), -QB - 1.0, QB) * (x_scale / QB))
            return jnp.einsum('bnd,hd->bnh', xq, Wq) + b
        h = bitlinear(x, W1, b1)
        h = jax.nn.gelu(h, approximate=False)
        return bitlinear(h, W2, b2)

    def _L2_xattn_ref(q, k, v, Wq, bq, Wk, bk, Wv, bv, Wo, bo):
        import jax, jax.numpy as jnp
        import numpy as np
        DIM = 256
        NUM_HEADS = 16
        HEAD_DIM = DIM // NUM_HEADS
        B, Nq, C = q.shape
        Nkv = k.shape[1]
        H, D = (NUM_HEADS, HEAD_DIM)
        qh = (q @ Wq.T + bq).reshape(B, Nq, H, D).transpose(0, 2, 1, 3)
        kh = (k @ Wk.T + bk).reshape(B, Nkv, H, D).transpose(0, 2, 1, 3)
        vh = (v @ Wv.T + bv).reshape(B, Nkv, H, D).transpose(0, 2, 1, 3)
        scale = D ** (-0.5)
        attn = jax.nn.softmax(jnp.einsum('bhqd,bhkd->bhqk', qh, kh) * scale, axis=-1)
        out = jnp.einsum('bhqk,bhkd->bhqd', attn, vh)
        out = out.transpose(0, 2, 1, 3).reshape(B, Nq, C)
        return out @ Wo.T + bo

    def _L2_ffn_ref(x, W_exp, b_exp, up_weights, up_bias, down_weights, W_con, b_con, down_bias):
        import jax, jax.numpy as jnp
        import numpy as np
        D_MODEL = 256
        EXPANSION = 4
        D_HIDDEN = D_MODEL * EXPANSION
        NUM_STAGES = int(np.log2(D_HIDDEN))

        def butterfly(y, weights, dim):
            lead = y.shape[:-1]
            for stage in range(weights.shape[0]):
                s = 2 ** stage
                nb = dim // (2 * s)
                yr = y.reshape(*lead, nb, 2, s)
                a = yr[..., 0, :]
                b = yr[..., 1, :]
                w = weights[stage].reshape(nb, s, 2, 2)
                na = w[..., 0, 0] * a + w[..., 0, 1] * b
                nb2 = w[..., 1, 0] * a + w[..., 1, 1] * b
                y = jnp.stack([na, nb2], axis=-2).reshape(*lead, dim)
            return y
        h = jnp.einsum('bsd,dh->bsh', x, W_exp) + b_exp
        h = butterfly(h, up_weights, D_HIDDEN)
        h = jax.nn.gelu(h + up_bias, approximate=False)
        h = butterfly(h, down_weights, D_HIDDEN)
        y = jnp.einsum('bsh,hd->bsd', h, W_con) + b_con
        return y + down_bias

    def _L3_xattn_ref(hidden_states, context, attention_mask, q_w, q_b, k_w, k_b, v_w, v_b):
        import jax, jax.numpy as jnp
        import numpy as np
        B, LQ, LK, D = (4, 512, 512, 256)
        H = 16
        HD = D // H

        def _split_heads(x):
            b, l, _ = x.shape
            return x.reshape(b, l, H, HD).transpose(0, 2, 1, 3)
        q = _split_heads(hidden_states @ q_w.T + q_b)
        k = _split_heads(context @ k_w.T + k_b)
        v = _split_heads(context @ v_w.T + v_b)
        scores = jnp.einsum('bhqd,bhkd->bhqk', q, k) / jnp.sqrt(jnp.float32(HD))
        mask = (attention_mask > 0)[:, None, None, :]
        scores = jnp.where(mask, -jnp.inf, scores)
        probs = jax.nn.softmax(scores, axis=-1)
        ctx = jnp.einsum('bhqk,bhkd->bhqd', probs, v)
        ctx = ctx.transpose(0, 2, 1, 3).reshape(ctx.shape[0], ctx.shape[2], H * HD)
        return ctx

    def _L3_ffn_ref(x, Wq, bq, Wk, bk, Wv, bv, Wr, br, Wo, bo):
        import jax, jax.numpy as jnp
        import numpy as np
        N_HEAD, N_ACTIVE, D_MODEL, D_ATTN = (16, 4, 256, 64)
        B, S, D = x.shape
        H, K, dh = (N_HEAD, N_ACTIVE, D_ATTN)
        dist = jax.nn.softmax(jnp.mean(x @ Wr + br, axis=1), axis=-1)
        top_vals, top_idx = jax.lax.top_k(dist, K)
        sparse = jnp.zeros_like(dist).at[jnp.arange(B)[:, None], top_idx].set(top_vals)
        gates_all = jax.nn.softmax(sparse, axis=1)
        g = jnp.take_along_axis(gates_all, top_idx, axis=1)[:, :, None, None]

        def proj(W, b):
            return (x @ W + b).reshape(B, S, H, dh).transpose(0, 2, 1, 3)
        Q, Kt, V = (proj(Wq, bq), proj(Wk, bk), proj(Wv, bv))
        idx = top_idx[:, :, None, None]
        Qk = jnp.take_along_axis(Q, idx, axis=1) * g
        Kk = jnp.take_along_axis(Kt, idx, axis=1) * g
        Vk = jnp.take_along_axis(V, idx, axis=1) * g
        scores = jnp.einsum('bksd,bktd->bkst', Qk, Kk) / jnp.sqrt(jnp.float32(dh))
        attn = jax.nn.softmax(scores, axis=-1)
        out = jnp.einsum('bkst,bktd->bksd', attn, Vk)
        out = out.transpose(0, 2, 1, 3).reshape(B, S, K * dh)
        return out @ Wo + bo
    x = x + _L0_xattn_ref(_layernorm(x, axis=-1), ctx_1024, ctx_1024, L0_xattn_Wq, L0_xattn_Wk, L0_xattn_Wv, L0_xattn_Wo, L0_xattn_lambda_q1, L0_xattn_lambda_k1, L0_xattn_lambda_q2, L0_xattn_lambda_k2)
    x = x + _L0_ffn_ref(_layernorm(x, axis=-1), L0_ffn_ln1_g, L0_ffn_ln1_b, L0_ffn_ln2_g, L0_ffn_ln2_b, L0_ffn_Wq, L0_ffn_bq, L0_ffn_Wk, L0_ffn_bk, L0_ffn_Wv, L0_ffn_bv, L0_ffn_Wp, L0_ffn_bp, L0_ffn_gate_W, L0_ffn_gate_b, L0_ffn_exp_W1, L0_ffn_exp_b1, L0_ffn_exp_W2, L0_ffn_exp_b2)
    x = x + _L1_xattn_ref(_layernorm(x, axis=-1), ctx_1024, ctx_1024, mask_BxS2_if0, mask_BxS2_if0, L1_xattn_Wq, L1_xattn_Wk, L1_xattn_Wv, L1_xattn_Wo, L1_xattn_bo)
    x = x + _L1_ffn_ref(_layernorm(x, axis=-1), L1_ffn_W1, L1_ffn_b1, L1_ffn_W2, L1_ffn_b2)
    x = x + _L2_xattn_ref(_layernorm(x, axis=-1), ctx_1024, ctx_1024, L2_xattn_Wq, L2_xattn_bq, L2_xattn_Wk, L2_xattn_bk, L2_xattn_Wv, L2_xattn_bv, L2_xattn_Wo, L2_xattn_bo)
    x = x + _L2_ffn_ref(_layernorm(x, axis=-1), L2_ffn_W_exp, L2_ffn_b_exp, L2_ffn_up_weights, L2_ffn_up_bias, L2_ffn_down_weights, L2_ffn_W_con, L2_ffn_b_con, L2_ffn_down_bias)
    x = x + _L3_xattn_ref(_layernorm(x, axis=-1), ctx_1024, mask_BxS2_ik0, L3_xattn_q_w, L3_xattn_q_b, L3_xattn_k_w, L3_xattn_k_b, L3_xattn_v_w, L3_xattn_v_b)
    x = x + _L3_ffn_ref(_layernorm(x, axis=-1), L3_ffn_Wq, L3_ffn_bq, L3_ffn_Wk, L3_ffn_bk, L3_ffn_Wv, L3_ffn_bv, L3_ffn_Wr, L3_ffn_br, L3_ffn_Wo, L3_ffn_bo)
    return x

_drawn_inputs = setup_inputs


def setup_inputs(seed=0):
    import zlib

    import numpy as np

    out = dict(_drawn_inputs(seed))
    spreads = {'L0_ffn_ln1_g': (1.0, 0.6),
     'L0_ffn_ln1_b': (0.0, 0.8),
     'L0_ffn_ln2_g': (1.0, 0.6),
     'L0_ffn_ln2_b': (0.0, 0.536),
     'L0_ffn_bq': (0.0, 0.8),
     'L0_ffn_bk': (0.0, 0.8),
     'L0_ffn_bv': (0.0, 0.555),
     'L0_ffn_bp': (0.0, 0.1),
     'L0_ffn_gate_b': (0.0, 0.276),
     'L0_ffn_exp_b1': (0.0, 0.738),
     'L0_ffn_exp_b2': (0.0, 0.1),
     'L1_ffn_b1': (0.0, 0.8),
     'L1_ffn_b2': (0.0, 0.1),
     'L2_xattn_bq': (0.0, 0.8),
     'L2_xattn_bk': (0.0, 0.8),
     'L2_xattn_bv': (0.0, 0.1),
     'L2_xattn_bo': (0.0, 0.1),
     'L2_ffn_b_exp': (0.0, 0.1),
     'L2_ffn_up_bias': (0.0, 0.1),
     'L2_ffn_b_con': (0.0, 0.1),
     'L2_ffn_down_bias': (0.0, 0.1),
     'L3_xattn_q_b': (0.0, 0.8),
     'L3_xattn_k_b': (0.0, 0.8),
     'L3_xattn_v_b': (0.0, 0.1),
     'L3_ffn_bq': (0.0, 0.8),
     'L3_ffn_bk': (0.0, 0.1),
     'L3_ffn_bv': (0.0, 0.8),
     'L3_ffn_br': (0.0, 0.8),
     'L3_ffn_bo': (0.0, 0.1)}
    factors = {'L0_xattn_Wq': 6.447,
     'L0_xattn_Wk': 6.351,
     'L0_xattn_lambda_q1': 5.937,
     'L0_xattn_lambda_k1': 8.0,
     'L0_xattn_lambda_q2': 8.0,
     'L0_xattn_lambda_k2': 8.0,
     'L0_ffn_Wq': 8.0,
     'L0_ffn_Wk': 8.0,
     'L0_ffn_Wv': 6.763,
     'L0_ffn_Wp': 3.314,
     'L1_ffn_W1': 2.798,
     'L3_xattn_q_w': 8.0,
     'L3_xattn_k_w': 8.0,
     'L3_ffn_Wq': 8.0,
     'L3_ffn_Wk': 8.0,
     'L3_ffn_Wv': 8.0,
     'L3_ffn_Wr': 8.0,
     'L3_ffn_Wo': 8.0}
    for name, (base, spread) in spreads.items():
        noise = np.random.default_rng([zlib.crc32(name.encode()), seed]).standard_normal(out[name].shape)
        drawn = base * np.exp(spread * noise) if base else spread * noise
        out[name] = jnp.asarray(drawn.astype(out[name].dtype))
    for name, factor in factors.items():
        out[name] = (out[name] * factor).astype(out[name].dtype)
    return out
```

```python
from contextlib import ExitStack

import concourse.bass as bass
from concourse import mybir
import numpy as np

P = 128
NB, T, D, TC = 4, 1024, 256, 77
NT = T // P
KD = D // P
CH = 512
HID = 4 * D
NM = HID // P
NE = 8
NH, DH = 16, 16
NG, GH = 4, 4
TX = 96
HS, DS = 4, 64
QUARTER = 32
EPS = 1e-5
LAM0 = 0.8 - 0.6 * float(np.exp(-0.3 * 12))
WS = 64.0
BIG = 60000.0
MAGIC = 1.5 * 2.0 ** 23
QB = 127.0
MROW = 96
NP = 5

F32, F16, I32, U32 = mybir.dt.float32, mybir.dt.float16, mybir.dt.int32, mybir.dt.uint32
ALU, ACT, AX = mybir.AluOpType, mybir.ActivationFunctionType, mybir.AxisListType.X

FLAT = ["A0q", "A0o", "B0q", "B0k", "B0v", "C1q", "D2q", "E3q"]
PADDED = ["B0p", "C1o", "D2o", "E3id", "F3o"]
CTXW = ["A0k", "A0v", "C1k", "C1v", "D2k", "D2v", "E3k", "E3v"]
BROW = ["B0v", "B0p", "C1o", "D2v", "D2o", "E3v", "F3o", "L2con", "L2down"] + [f"e{e}" for e in range(NE)]
BCOL = ["B0q", "B0k", "D2q", "D2k", "E3q", "E3k", "ln1_g", "ln1_b", "ln2_g", "ln2_b"]
BC_UP = 2 * len(BCOL)
BC_E1 = BC_UP + NM
NBC = BC_E1 + NE * NM
XL = ["C1", "D2", "E3"]
FLAT_N, PAD_N = KD * D, GH * D


class Ledger:

    def __init__(self, known):
        self.count, self.value, self.slot, self.freed = {}, {}, {}, {}
        self.known = known

    def mark(self, name, key, inc):
        self.count[name] = self.count.get(name, 0) + inc
        if (name, key) in self.value:
            raise KeyError(f"twice: {name} {key}")
        self.value[name, key] = self.count[name]
        return inc

    def at(self, name, key):
        return self.known.value[name, key] if self.known else 1


def attention_steps(own):
    steps = []
    if own:
        steps += [("S", 0, t) for t in range(NT)] + [("MT", 0)]
        for g in range(NG):
            for kt in range(NT):
                if kt:
                    steps += [("ST", g, kt, 0)]
                    steps += [("PVA", g, kt - 1)]
                    steps += [("ST", g, kt, j) for j in range(1, GH)]
                else:
                    steps += [("ST", g, kt, j) for j in range(GH)]
                if g + 1 < NG and kt < NT // 2:
                    steps += [("S", g + 1, kt), ("S", g + 1, NT - 1 - kt)]
                if g + 1 < NG and kt == NT // 2:
                    steps += [("MT", g + 1)]
                if g and kt == 5:
                    steps += [("NB", g - 1)]
            steps += [("PVA", g, NT - 1)]
        steps += [("NB", NG - 1)]
    else:
        for g in range(2):
            steps += [("S", g, t) for t in range(NT)] + [("MT", g)]
        for g in range(NG):
            steps += [("ST", g, 0, j) for j in range(GH)]
            if g + 2 < NG:
                steps += [("S", g + 2, t) for t in range(NT)] + [("MT", g + 2)]
            steps += [("PVA", g, 0)]
            if g >= 2:
                steps += [("NB", g - 2)]
        steps += [("NB", NG - 2), ("NB", NG - 1)]
    return steps


def last_attention_steps():
    steps = [("S", 0, t) for t in range(NT)] + [("MT", 0)]
    for h in range(HS):
        for kt in range(NT):
            steps += [("ST", h, kt)]
            if h + 1 < HS and kt < NT // 2:
                steps += [("S", h + 1, 2 * kt), ("S", h + 1, 2 * kt + 1)]
            if kt:
                steps += [("PV", h, kt - 1)]
            if h + 1 < HS and kt == NT // 2:
                steps += [("MT", h + 1)]
            if h and kt == 5:
                steps += [("NB", h - 1)]
        steps += [("PV", h, NT - 1)]
    steps += [("NB", HS - 1)]
    return steps


def build(nc, A, out, known, stages):
    led = Ledger(known)
    with ExitStack() as ctx:
        def sb(name, shape, dt):
            return ctx.enter_context(nc.sbuf_tensor(name, shape, dt))

        def dram(name, shape, dt):
            return nc.dram_tensor(name, shape, dt, kind="Internal").ap()

        Wf = sb("weights_flat", [P, len(FLAT), 2, KD, D], F16)
        Wp = sb("weights_padded", [P, len(PADDED), 2, GH, D], F16)
        Wq1 = sb("ternary_W1", [P, KD, HID], F16)
        Wq2 = sb("ternary_W2", [P, NM, D], F16)
        Wexp = sb("butterflied_W_exp", [P, KD, HID], F32)
        RT = sb("butterflied_W_con_turned", [P, NM, D], F32)
        X = sb("x_tokens", [P, NT, D], F32)
        H = sb("h_tokens", [P, NT, D], F32)
        XT = sb("x_channels_hi_lo", [P, 2, KD, T], F16)
        QS = sb("q_stack", [P, 2, GH, T], F16)
        KS = sb("k_stack", [P, 2, GH, T], F16)
        KX = sb("k_stack_context", [MROW + 2, len(XL), NH, TX], F16)
        VX = sb("v_context", [P, len(XL), NH, QUARTER], F32)
        KP0 = sb("k_context_0", [P, 2, TX], F16)
        VP0 = sb("v_context_0", [P, 2, D], F16)
        CTf = sb("context_f32", [P, KD, TC], F32)
        CT = sb("context_hi_lo", [P, 2, KD, TX], F16)
        identf = sb("identf", [P, P], F32)
        ident = sb("ident", [P, P], F16)
        big = sb("big_ident", [P, P], F16)
        small = sb("small_ident", [P, P], F16)
        causal = sb("causal", [P, 2, P], F16)
        E4 = sb("spread_sums", [P, P], F32)
        E64 = sb("spread_sums_last", [TX, TX], F32)
        onesf = sb("ones_f32", [P, P], F32)
        BR = sb("bias_rows", [P, 2, D], F16)
        BC = sb("bias_columns", [P, NBC], F32)
        upb = sb("up_bias_whole", [P, NM], F32)
        gateW = sb("gate_W", [P, 2, KD, NE], F16)
        gateb = sb("gate_b", [P, NE], F32)
        iota = sb("iota", [P, NE], F32)
        lamt = sb("lambda_work", [P, 8], F32)
        epsc = sb("eps_and_zero", [P, 2], F32)
        F3Wr = sb("router_W", [P, KD, NH], F32)
        F3br = sb("router_b", [1, NH], F32)
        wsc = sb("ternary_scales", [P, 8], F32)
        stats = sb("ln_stats", [P, NT, 6], F32)
        mv = sb("ln_mean_var", [P, NT, 2], F32)
        rstd = sb("ln_rstd", [P, NT], F32)
        sd = sb("ln_std", [P, NT], F32)
        mpart = sb("max_parts", [P, GH * NT, 2], F32)
        negm = sb("minus_max", [P, 2, GH * NT], F32)
        mrow = sb("minus_max_rows", [GH * NT, 2, 2, P], F16)
        rsum = sb("sums_by_token", [P, NG, QUARTER], F32)
        rinv = sb("inverse_sums_by_token", [P, NG, QUARTER], F32)
        sm = sb("small_work", [P, 160], F32)
        maxv = sb("top_values", [P, NT, NE], F32)
        maxi = sb("top_indices", [P, NT, NE], U32)
        wfull = sb("expert_weights", [P, NT, NE], F32)
        maskr = sb("mask_row", [1, TX], I32)
        rt = sb("router_row", [1, 96], F32)
        rti = sb("router_index", [1, NE], U32)
        xmean = sb("mean_x", [P, KD], F32)
        gcol = sb("gates_by_row", [P, 8], F32)
        arena = sb("arena", [P, 16 * 1024], F32)

        def area(kb, n, dt=F32, rows=P):
            v = arena[0:rows, int(kb * 256):int(kb * 256) + (n if dt == F32 else n // 2)]
            return v if dt == F32 else v.bitcast(dt)

        stage_flat = area(0, len(FLAT + CTXW) * FLAT_N)
        stage_pad = area(32, len(PADDED) * PAD_N)
        ctx_split = area(52, FLAT_N * 8, F16)
        lamr = area(60, 6 * P)
        gwf = area(63, KD * NE)
        brf = XT[:, :, :, :].rearrange("p s k c -> p (s k c)").bitcast(F32)[:, 0:D]
        KVW = area(0, len(CTXW) * 2 * FLAT_N, F16).rearrange("p (w s k d) -> p w s k d", s=2, k=KD, d=D)
        kxs = area(40, 2 * 3 * KD * TX, F16).rearrange("p (s l k c) -> p s l k c", s=2, l=3, k=KD)
        kxf = area(44, 3 * KD * TX).rearrange("p (l k c) -> p l k c", l=3, k=KD)
        maskb = area(57, NH * TX, F16, rows=1).rearrange("p (h c) -> p h c", h=NH)
        tmp = area(60, T)
        XN = {k: area(o, NT * D).rearrange("p (t d) -> p t d", d=D) for k, o in
              {"A": 48, "B": 16, "M": 48, "C": 16, "D": 16, "E": 16, "L1": 16, "L2": 16, "F": 28}.items()}
        VP = area(0, NT * NH * QUARTER).rearrange("p (t h d) -> p t h d", h=NH, d=QUARTER)
        PR = area(16, NP * T).rearrange("p (n c) -> p n c", c=T)
        OT = {True: [area(36 + 4 * (g % 2), T) for g in range(NG)],
              False: [area(36, T), area(40, T), area(0, T), area(4, T)]}
        ON = area(44, 2 * NG * T, F16).rearrange("p (s g c) -> p s g c", s=2, g=NG)
        qhl = area(44, 2 * KD * T, F16).rearrange("p (s k c) -> p s k c", s=2, k=KD)
        khl = area(52, 2 * KD * T, F16).rearrange("p (s k c) -> p s k c", s=2, k=KD)
        q0 = area(0, 2 * 2 * T, F16).rearrange("p (s h c) -> p s h c", s=2, h=2)
        E0 = area(8, 2 * 2 * TC).rearrange("p (n h c) -> p n h c", n=2, h=2)
        A0 = area(12, NT * TC).rearrange("p (t c) -> p t c", c=TC)
        AT0 = area(32, 2 * T, F16).rearrange("p (s c) -> p s c", s=2)
        AO0 = area(20, 2 * KD * T, F16).rearrange("p (s k c) -> p s k c", s=2, k=KD)
        sq0 = area(36, 2 * D).rearrange("p (n d) -> p n d", n=2)
        WSt = area(0, 2 * KD * HID).rearrange("p (w n) -> p w n", w=2)
        Wm = [area(16 + 16 * i, 2 * 2 * KD * HID, F16).rearrange("p (w s n) -> p w s n", w=2, s=2) for i in range(2)]
        midf = area(48, 3 * CH).rearrange("p (n c) -> p n c", n=3)
        mid = area(54, 4 * 2 * CH, F16).rearrange("p (n s c) -> p n s c", n=4, s=2)
        b1b = area(0, HID)
        hb = area(4, 3 * HID).rearrange("p (n c) -> p n c", n=3)
        xq = area(24, NT * D, F16).rearrange("p (t d) -> p t d", d=D)
        xqT = area(28, KD * T, F16).rearrange("p (k c) -> p k c", k=KD)
        hq = area(32, 2 * HID, F16).rearrange("p (n c) -> p n c", n=2)
        hqT = area(36, 2 * HID, F16).rearrange("p (n c) -> p n c", n=2)
        b2b = area(40, D)
        hr = area(44, 2 * HID).rearrange("p (n c) -> p n c", n=2)
        XTf = area(0, KD * T).rearrange("p (k c) -> p k c", k=KD)
        gT = area(24, 2 * NM * CH).rearrange("p (n m c) -> p n m c", n=2, m=NM)
        VP4 = area(0, NT * HS * TX).rearrange("p (t h d) -> p t h d", h=HS, d=TX)
        Wst = area(12, 3 * KD * D).rearrange("p (w k d) -> p w k d", w=3, k=KD)
        Wsel = area(18, 3 * 2 * KD * D, F16).rearrange("p (w s k d) -> p w s k d", w=3, s=2, k=KD)
        PR4 = area(16, NP * T).rearrange("p (n c) -> p n c", c=T)
        OT4 = [area(36, T, rows=TX), area(40, T, rows=TX)]
        ON4 = area(44, 2 * HS * T, F16, rows=TX).rearrange("p (s g c) -> p s g c", s=2, g=HS)
        bsel = sb("selected_biases", [P, 4], F32)
        bvr = area(24, D, rows=1)
        bvh = area(25, 2 * D, F16, rows=1).rearrange("p (s d) -> p s d", s=2)

        bE = area(0, 3 * HID).rearrange("p (k n) -> p k n", k=3)
        bC = area(12, 2 * HID).rearrange("p (k n) -> p k n", k=2)
        tE = area(20, 2 * 3 * CH).rearrange("p (n k c) -> p n k c", n=2, k=3)
        tC = area(32, 2 * 2 * CH).rearrange("p (n k c) -> p n k c", n=2, k=2)
        ringE = QS[:, :, :, :].rearrange("p b h c -> p (b h c)").bitcast(F32).rearrange("p (n c) -> p n c", n=2)
        ringC = KS[:, :, :, :].rearrange("p b h c -> p (b h c)").bitcast(F32).rearrange("p (n c) -> p n c", n=2)
        fW1 = X[:, :, :].rearrange("p t d -> p (t d)")
        fW2 = H[:, :, :].rearrange("p t d -> p (t d)")

        PS = ctx.enter_context(nc.psum_tensor("ps", [P, 8, CH], F32))
        flat = PS[:, :, :].rearrange("p b c -> p (b c)")
        SLOT = {"A0": flat[:, 0:1024], "A1": flat[:, 1024:2048], "B0": flat[:, 2048:2560], "B1": flat[:, 2560:3072],
                "S0": flat[:, 3072:3584], "S1": flat[:, 3584:4096]}

        d_ctxw = dram("scr_ctx_weights", [P, len(CTXW), 2 * FLAT_N], F16)
        d_kx = dram("scr_k_context", [2, len(XL), KD * P, TX], F16)
        d_q = dram("scr_q", [2, KD * P, T], F16)
        d_k = dram("scr_k", [2, KD * P, T], F16)
        d_m = dram("scr_max", [2, 2, GH * NT, P], F16)
        d_s = dram("scr_sums", [NG, GH, T], F32)
        d_r = dram("scr_inverse_sums", [NG, GH, T], F32)

        names = ["pe", "act", "dve", "pool", "ld_x", "ld_ctx", "ld_mask", "ld_kvw", "ld_const", "st_kx", "ld_kx", "st_q", "st_k",
                 "ld_stack0", "ld_stack1", "st_m0", "st_m1", "ld_m0", "ld_m1", "ld_wexp0", "ld_wexp1", "ld_b12",
                 "ld_sel", "st_out"] + [f"{n}{g}" for n in ("st_s", "ld_s", "st_r", "ld_r") for g in range(NG)]
        sems = {n: ctx.enter_context(nc.semaphore("s_" + n)) for n in names}
        first_num = min(s.num for s in sems.values())
        assert max(s.num for s in sems.values()) - first_num == len(sems) - 1
        once = {n: ctx.enter_context(nc.semaphore("u_" + n)) for n in (
            "load", "pe", "act", "dve", "pool", "ctxw", "staged", "bf_rows", "up", "down", "up_w0", "up_w1", "down_w0", "down_w1",
            "wsum", "store0", "store1", "store2", "store3")}
        arrived = ctx.enter_context(nc.semaphore("arrived"))
        go = {n: ctx.enter_context(nc.semaphore("go_" + n)) for n in ("pe", "act", "dve", "pool")}

        def did(name, *key):
            inc = 16 if name[:3] in ("ld_", "st_") else 1
            return sems[name], led.mark(name, key, inc)

        def of(name, *key):
            return sems[name], led.at(name, key)

        def slot(*key):
            return SLOT[led.slot[key]]

        def frees(name, *key):
            led.freed[key] = (name, ("free",) + key)
            return did(name, "free", *key)

        def back(e, c, m, n):
            i = (e * 2 + c) * NM + m - n
            return i // (2 * NM), i // NM % 2, i % NM

        def butterfly(eng, sem, y, t, w, s, i, turned):
            st, k = 2 ** s, y.shape[1]
            pair = y.rearrange("p k (n two s) -> p k n two s", two=2, s=st)
            wv = w.rearrange("p (n s rc) -> p n s rc", s=st, rc=4)
            a = [pair[:, kk, :, 0, :] for kk in range(k)]
            b_ = [pair[:, kk, :, 1, :] for kk in range(k)]
            t0 = [t[:, 0, kk].rearrange("p (n s) -> p n s", s=st) for kk in range(k)]
            t1 = [t[:, 1, kk].rearrange("p (n s) -> p n s", s=st) for kk in range(k)]
            c_ba, c_ab = (1, 2) if turned else (2, 1)
            n = 6 * i * k
            if n:
                eng.wait_ge(sem, n)
            for kk in range(k):
                eng.tensor_tensor(t0[kk], a[kk], wv[:, :, :, 0], ALU.mult).then_inc(sem, 1)
                eng.tensor_tensor(t1[kk], a[kk], wv[:, :, :, c_ba], ALU.mult).then_inc(sem, 1)
            eng.wait_ge(sem, n + 2 * k)
            for kk in range(k):
                eng.tensor_tensor(a[kk], b_[kk], wv[:, :, :, c_ab], ALU.mult).then_inc(sem, 1)
                eng.tensor_tensor(b_[kk], b_[kk], wv[:, :, :, 3], ALU.mult).then_inc(sem, 1)
            eng.wait_ge(sem, n + 4 * k)
            for kk in range(k):
                eng.tensor_tensor(a[kk], a[kk], t0[kk], ALU.add).then_inc(sem, 1)
                eng.tensor_tensor(b_[kk], b_[kk], t1[kk], ALU.add).then_inc(sem, 1)

        wi = {n: i for i, n in enumerate(FLAT)}
        pi = {n: i for i, n in enumerate(PADDED)}
        ci = {n: i for i, n in enumerate(CTXW)}
        bi = {n: i for i, n in enumerate(BROW)}
        bc = {n: 2 * i for i, n in enumerate(BCOL)}
        runs = [("B", "B0", True), ("C", "C1", False), ("D", "D2", False), ("E", "E3", False)]
        block = ctx.enter_context(nc.Block())

        def batch_end(eng, name):
            eng.drain().then_inc(arrived, 1)
            eng.wait_ge(go[name], 1)
            eng.sem_clear(go[name])

        @block.sync
        def _(sp):
            for dst, src in [(stage_flat, A["wflat"]), (stage_pad, A["wpad"]), (identf[:], A["c_ident"]), (ident[:], A["c_ident16"]),
                             (causal[:], A["c_causal"]), (E4[:], A["c_E4"]), (E64[:], A["c_E64"]), (iota[:], A["c_iota"]),
                             (BC[:, 0:NBC], A["bcol"]), (gateb[:], A["gate_b"].partition_broadcast(P)),
                             (epsc[:], A["c_eps"]), (KX[:MROW + 2], A["c_kx"]), (brf[0:len(BROW), :], A["brow"]),
                             (gwf[:], A["gate_W"]), (lamr[:, 0:4 * P], A["lam"].partition_broadcast(P)),
                             (F3Wr[:], A["F3_Wr"]), (F3br[:], A["F3_br"]),
                             (fW1, A["L1_W1"]), (fW2, A["L1_W2"])]:
                sp.dma_start(dst, src).then_inc(once["load"], 16)
            for w in range(len(CTXW)):
                sp.wait_ge(once["ctxw"], w + 1)
                sp.dma_start(d_ctxw[:, w, :], ctx_split[:, (w % 4) * 2 * FLAT_N:(w % 4 + 1) * 2 * FLAT_N]).then_inc(once[f"store{w % 4}"], 16)
            sp.wait_ge(once["staged"], 1)
            for i in range(4):
                sp.wait_ge(once[f"store{i}"], 16 * len(CTXW) // 4)
            sp.dma_start(bE, A["W_exp"]).then_inc(once["bf_rows"], 16)
            sp.dma_start(bC, A["W_con"]).then_inc(once["bf_rows"], 16)
            for s in range(10):
                if s >= 2:
                    sp.wait_ge(once["up"], 18 * (s - 1))
                sp.dma_start(ringE[:, s % 2], A["up_w"][s:s + 1, :].partition_broadcast(P)).then_inc(once[f"up_w{s % 2}"], 16)
                if s >= 2:
                    sp.wait_ge(once["down"], 12 * (s - 1))
                sp.dma_start(ringC[:, s % 2], A["down_w"][9 - s:10 - s, :].partition_broadcast(P)).then_inc(once[f"down_w{s % 2}"], 16)
            sp.wait_ge(arrived, 4)
            sp.sem_clear(arrived)
            for n in go:
                sp.sem_inc(go[n], 1)

            with sp.Fori(0, NB) as b:
                bs = bass.ds(b, 1)
                sp.dma_start(X[:], A["x"][bs].rearrange("o (t p) d -> p (o t) d", p=P)).then_inc(*did("ld_x"))
                sp.dma_start(CTf[:], A["ctxT"][bs].rearrange("o (k p) c -> p (o k) c", p=P)).then_inc(*did("ld_ctx"))
                sp.dma_start(maskr[:, 0:TC], A["mask"][bs]).then_inc(*did("ld_mask"))
                sp.dma_start(KVW.rearrange("p w s k d -> p w (s k d)"), d_ctxw).then_inc(*did("ld_kvw"))
                sp.dma_start(QS[48:MROW, :, :, :], A["c_qs"]).then_inc(*did("ld_const", 1))
                sp.dma_start(KS[48:MROW + 2, :, :, :], A["c_ks"]).then_inc(*did("ld_const", 2))
                sp.wait_ge(*of("dve", "kxs"))
                for s in range(2):
                    for l in range(len(XL)):
                        sp.dma_start(d_kx[s, l, :, 0:TC].rearrange("(k p) c -> p k c", p=P), kxs[:, s, l, :, 0:TC]).then_inc(*did("st_kx", s, l))
                sp.wait_ge(*of("st_kx", 1, 2))
                for n, s in enumerate((0, 1, 0)):
                    for l in range(len(XL)):
                        sp.dma_start(KX[16 * n:16 * n + 16, l, :, 0:TC],
                                     d_kx[s, l, :, 0:TC].rearrange("(h i) c -> i h c", i=DH)).then_inc(*did("ld_kx", n, l))
                sp.wait_ge(*of("dve", "mask"))
                sp.dma_start(KX[48:49, 2, :, 0:TC], maskb[:, :, 0:TC]).then_inc(*did("ld_kx", "mask"))

                def stacks(L, own, g):
                    buf = g % 2
                    if g >= 2:
                        sp.wait_ge(*of("pe", L, "ST", g - 2, NT - 1 if own else 0, GH - 1))
                    for n, s in enumerate((0, 0, 1)):
                        sp.dma_start(QS[16 * n:16 * n + 16, buf],
                                     d_q[s, g * GH * DH:(g + 1) * GH * DH].rearrange("(h i) c -> i h c", i=DH)).then_inc(*did(f"ld_stack{buf}", L, g, "q", n))
                    if own:
                        for n, s in enumerate((0, 1, 0)):
                            sp.dma_start(KS[16 * n:16 * n + 16, buf],
                                         d_k[s, g * GH * DH:(g + 1) * GH * DH].rearrange("(h i) c -> i h c", i=DH)).then_inc(*did(f"ld_stack{buf}", L, g, "k", n))

                def max_rows(L, g):
                    buf = g % 2
                    sp.wait_ge(*of("dve", L, "mrow", g))
                    n = NT if L == "F3" else GH * NT
                    sp.dma_start(d_m[buf, :, 0:n].rearrange("s n q -> n s q"), mrow[0:n, buf]).then_inc(*did(f"st_m{buf}", L, g))
                    sp.wait_ge(*of(f"st_m{buf}", L, g))
                    dst = QS[MROW:MROW + 2, 1, g, :] if L == "F3" else QS[MROW:MROW + 2, buf].rearrange("s h c -> s (h c)")
                    sp.dma_start(dst, d_m[buf, :, 0:n].rearrange("s n q -> s (n q)")).then_inc(*did(f"ld_m{buf}", L, g))

                def sums(L, ot, g, rows):
                    n = len(range(*rows.indices(P)))
                    w = n * T // P
                    sp.wait_ge(*of("act", L, "ot", g, 1))
                    sp.dma_start(d_s[g, 0:n], ot[rows, :]).then_inc(*did(f"st_s{g}", L))
                    sp.wait_ge(*of(f"st_s{g}", L))
                    sp.dma_start(rsum[:, g, 0:w], d_s[g, 0:n].rearrange("j (a b) -> (j a) b", b=w)).then_inc(*did(f"ld_s{g}", L))
                    sp.wait_ge(*of("dve", L, "rinv", g))
                    sp.dma_start(d_r[g, 0:n].rearrange("j (a b) -> (j a) b", b=w), rinv[:, g, 0:w]).then_inc(*did(f"st_r{g}", L))
                    sp.wait_ge(*of(f"st_r{g}", L))
                    sp.dma_start(ot[rows, :], d_r[g, 0:n]).then_inc(*did(f"ld_r{g}", L))

                def spill(L, own):
                    sp.wait_ge(*of("dve", L, "qlo", 1))
                    for s in range(2):
                        sp.dma_start(d_q[s].rearrange("(k p) c -> p k c", p=P), qhl[:, s]).then_inc(*did("st_q", L, s))
                    if own:
                        sp.wait_ge(*of("dve", L, "klo", 1))
                        for s in range(2):
                            sp.dma_start(d_k[s].rearrange("(k p) c -> p k c", p=P), khl[:, s]).then_inc(*did("st_k", L, s))
                        sp.wait_ge(*of("st_k", L, 1))
                    sp.wait_ge(*of("st_q", L, 1))

                def attention(L, own):
                    spill(L, own)
                    stacks(L, own, 0)
                    stacks(L, own, 1)
                    max_rows(L, 0)
                    if not own:
                        max_rows(L, 1)
                    for g in range(NG):
                        if own and g + 1 < NG:
                            max_rows(L, g + 1)
                        if g + 2 < NG:
                            stacks(L, own, g + 2)
                            if not own:
                                max_rows(L, g + 2)
                        sums(L, OT[own][g], g, slice(DH, P, QUARTER))

                if "B" in stages:
                    attention("B0", True)
                if "M" in stages:
                    sp.wait_ge(*of("pe", "B0", "PVA", NG - 1, NT - 1))
                    for e in range(NE):
                        if e:
                            sp.wait_ge(*of("dve", "M", "wlo", e - 1, 1))
                        sp.dma_start(WSt[:, 0], A["exp_W1"][e]).then_inc(*did("ld_wexp0", e))
                        sp.dma_start(WSt[:, 1], A["exp_W2"][e]).then_inc(*did("ld_wexp1", e))
                if "C" in stages:
                    attention("C1", False)
                if "L1" in stages:
                    sp.wait_ge(*of("dve", "L1", "xs"))
                    sp.dma_start(b1b, A["L1_b1"].partition_broadcast(P)).then_inc(*did("ld_b12", 0))
                    sp.dma_start(b2b, A["L1_b2"].partition_broadcast(P)).then_inc(*did("ld_b12", 1))
                if "D" in stages:
                    attention("D2", False)
                if "E" in stages:
                    attention("E3", False)
                if "F" in stages:
                    sp.wait_ge(*of("dve", "F", "index"))
                    for k in range(HS):
                        h = sp.value_load(rti[0:1, k:k + 1], min_val=0, max_val=15)
                        for w, n in enumerate(("Wq", "Wk", "Wv")):
                            sp.dma_start(Wst[:, w, :, k * DS:(k + 1) * DS],
                                         A["F3_" + n][:, :, bass.ds(h * DS, DS)]).then_inc(*did("ld_sel", k, w))
                        for w, n in enumerate(("bq", "bk")):
                            sp.dma_start(bsel[DS * (k % 2):DS * (k % 2) + DS, 2 * w + k // 2:2 * w + k // 2 + 1],
                                         A["F3_" + n][bass.ds(h * DS, DS)]).then_inc(*did("ld_sel", k, "b", w))
                        sp.dma_start(bvr[0:1, k * DS:(k + 1) * DS], A["F3_bv"][:, bass.ds(h * DS, DS)]).then_inc(*did("ld_sel", k, "bv"))
                    spill("F3", True)
                    for n, (dst, src) in enumerate([(QS[0:64, 0], d_q[0]), (QS[64:P, 0], d_q[1]), (KS[0:64, 0], d_k[0]),
                                                    (KS[64:P, 0], d_k[0]), (QS[0:64, 1], d_q[0]), (KS[0:64, 1], d_k[1])]):
                        sp.dma_start(dst, src.rearrange("(h i) c -> i h c", i=DS)).then_inc(*did("ld_stack0", "F3", n))
                    max_rows("F3", 0)
                    for h in range(HS):
                        if h + 1 < HS:
                            max_rows("F3", h + 1)
                        sums("F3", OT4[h % 2], h, slice(DS, DS + 1, 1))
                sp.wait_ge(*of("dve", "final"))
                sp.dma_start(out[bs].rearrange("o (t p) d -> p (o t) d", p=P), X[:]).then_inc(*did("st_out"))
                sp.wait_ge(*of("st_out"))
                for n in names:
                    if n in led.count:
                        sp.wait_ge(sems[n], led.count[n])
                sp.wait_ge(arrived, 4)
                sp.sem_clear(range(first_num, first_num + len(sems)))
                sp.sem_clear(arrived)
                for n in go:
                    sp.sem_inc(go[n], 1)

        @block.tensor
        def _(pe):
            holder, turn = {}, {"A": 0, "S": 0}

            def claim(kind, *key):
                name = kind
                if kind in turn:
                    name = f"{kind}{turn[kind] % 2}"
                    turn[kind] += 1
                led.slot[key] = name
                if name in holder:
                    reader = led.known.freed[holder[name]] if known else None
                    pe.wait_ge(sems[reader[0] if known else "act"], led.known.value[reader] if known else 1)
                holder[name] = key
                return SLOT[name]

            def split3(o, left, right, first, last, **kw):
                pe.matmul(o, left[0], right[0], start=first, stop=False, **kw)
                pe.matmul(o, left[0], right[1], start=False, stop=False, **kw)
                return pe.matmul(o, left[1], right[0], start=False, stop=last, **kw)

            def bias_rows(o, name, n, idt=None, last=True, **kw):
                row = (ident if idt is None else idt)[:, bi[name]:bi[name] + 1].to_broadcast([P, n])
                pe.matmul(o, row, BR[:, 0], start=False, stop=False, **kw)
                return pe.matmul(o, row, BR[:, 1], start=False, stop=last, **kw)

            def parts(t, *i):
                return t[(slice(None), 0) + i], t[(slice(None), 1) + i]

            pe.wait_ge(once["wsum"], 2)
            pe.wait_ge(once["pool"], 1)
            pe.matmul(SLOT["S0"][:, 0:2], onesf[:], wsc[:, 0:2], start=True, stop=True).then_inc(once["pe"], 1)
            pe.wait_ge(once["up"], 180)
            for m in range(NM):
                mm = pe.matmul(SLOT["S1"][:, m:m + 1], bE[0:1, KD, m * P:(m + 1) * P], onesf[0:1, 0:1], start=True, stop=True)
            mm.then_inc(once["pe"], 1)
            pe.wait_ge(once["down"], 120)
            for m in range(NM):
                for k in range(KD):
                    mm = pe.transpose(flat[:, m * D + k * P:m * D + (k + 1) * P], bC[:, k, m * P:(m + 1) * P], identf[:])
            mm.then_inc(once["pe"], 1)
            batch_end(pe, "pe")

            with pe.Fori(0, NB):
                def turn_x(N):
                    for k in range(KD):
                        s = claim("A", "T", N, k)
                        for t in range(NT):
                            pe.wait_ge(*of("dve", N, "xn", t))
                            mm = pe.transpose(s[:, t * P:(t + 1) * P], XN[N][:, t, k * P:(k + 1) * P], identf[:])
                        mm.then_inc(*did("pe", "T", N, k))

                def project(key, weight):
                    s = claim("A", *key)
                    for c in range(2):
                        for k in range(KD):
                            mm = split3(s[:, c * CH:(c + 1) * CH], weight(k), parts(XT, k, slice(c * CH, (c + 1) * CH)), k == 0, k == KD - 1)
                    mm.then_inc(*did("pe", *key))

                def wflat(name, m):
                    return lambda k: (Wf[:, wi[name], 0, k, m * P:(m + 1) * P], Wf[:, wi[name], 1, k, m * P:(m + 1) * P])

                pe.wait_ge(*of("dve", "ctlo"))
                pe.wait_ge(*of("ld_kvw"))

                def kvw(name, k, a, b):
                    return KVW[:, ci[name], 0, k, a:b], KVW[:, ci[name], 1, k, a:b]

                s = claim("S", "K0")
                for k in range(KD):
                    mm = split3(s[:, 0:TC], kvw("A0k", k, 0, P), parts(CT, k, slice(0, TC)), k == 0, k == KD - 1)
                mm.then_inc(*did("pe", "K0"))
                s = claim("S", "V0")
                for k in range(KD):
                    mm = split3(s[0:TC, 0:D], parts(CT, k, slice(0, TC)), kvw("A0v", k, 0, D), k == 0, k == KD - 1)
                mm.then_inc(*did("pe", "V0"))
                for l, L in enumerate(XL):
                    for m in range(KD):
                        s = claim("S", "KX", l, m)
                        for k in range(KD):
                            mm = split3(s[:, 0:TC], kvw(L + "k", k, m * P, (m + 1) * P), parts(CT, k, slice(0, TC)), k == 0, k == KD - 1)
                        mm.then_inc(*did("pe", "KX", l, m))
                    s = claim("S", "VX", l)
                    for k in range(KD):
                        mm = split3(s[0:TC, 0:D], parts(CT, k, slice(0, TC)), kvw(L + "v", k, 0, D), k == 0, k == KD - 1 and L == "C1")
                    if L != "C1":
                        mm = bias_rows(s[0:TC, 0:D], L + "v", TC)
                    mm.then_inc(*did("pe", "VX", l))

                if "A" in stages:
                    turn_x("A")
                    pe.wait_ge(*of("dve", "A", "xlo", 1))
                    for h in range(2):
                        project(("A", "Q", h), wflat("A0q", h))
                    pe.wait_ge(*of("dve", "A", "kp0"))
                    pe.wait_ge(*of("dve", "A", "qlo", 1))
                    for t in range(NT):
                        s = claim("S", "A", "S", t)
                        for h in range(2):
                            mm = split3(s[:, h * TC:(h + 1) * TC], (q0[:, 0, h, t * P:(t + 1) * P], q0[:, 1, h, t * P:(t + 1) * P]),
                                        parts(KP0, slice(0, TC)), True, True)
                        mm.then_inc(*did("pe", "A", "S", t))
                    s = claim("A", "A", "PT")
                    for t in range(NT):
                        pe.wait_ge(*of("dve", "A", "p", t))
                        mm = pe.transpose(s[0:TC, t * P:(t + 1) * P], A0[:, t, :], identf[:])
                    mm.then_inc(*did("pe", "A", "PT"))
                    pe.wait_ge(*of("dve", "A", "ptlo"))
                    pe.wait_ge(*of("dve", "A", "vp0"))
                    for m in range(KD):
                        s = claim("A", "A", "O", m)
                        for c in range(2):
                            mm = split3(s[:, c * CH:(c + 1) * CH], (VP0[0:TC, 0, m * P:(m + 1) * P], VP0[0:TC, 1, m * P:(m + 1) * P]),
                                        (AT0[0:TC, 0, c * CH:(c + 1) * CH], AT0[0:TC, 1, c * CH:(c + 1) * CH]), True, True)
                        mm.then_inc(*did("pe", "A", "O", m))
                    for t in range(NT):
                        s = claim("S", "A", "N", t)
                        split3(s[:, 0:D], (AT0[0:TC, 0, t * P:(t + 1) * P], AT0[0:TC, 1, t * P:(t + 1) * P]),
                               (VP0[0:TC, 0, :], VP0[0:TC, 1, :]), True, True).then_inc(*did("pe", "A", "N", t))
                    pe.wait_ge(*of("dve", "A", "olo", 1))
                    for t in range(NT):
                        s = claim("S", "A", "W", t)
                        for k in range(KD):
                            mm = split3(s[:, 0:D], parts(AO0, k, slice(t * P, (t + 1) * P)),
                                        (Wf[:, wi["A0o"], 0, k, :], Wf[:, wi["A0o"], 1, k, :]), k == 0, k == KD - 1)
                        mm.then_inc(*did("pe", "A", "W", t))

                def attention(L, own):
                    for m in range(KD):
                        project((L, "q", m), wflat(L + "q", m))
                    if own:
                        for m in range(KD):
                            project((L, "k", m), wflat(L + "k", m))
                        for t in range(NT):
                            s = claim("S", L, "v", t)
                            for k in range(KD):
                                split3(s[:, 0:D], parts(XT, k, slice(t * P, (t + 1) * P)),
                                       (Wf[:, wi[L + "v"], 0, k, :], Wf[:, wi[L + "v"], 1, k, :]), k == 0, False)
                            bias_rows(s[:, 0:D], L + "v", P).then_inc(*did("pe", L, "v", t))
                    l = None if own else XL.index(L)
                    steps = attention_steps(own)
                    ring = {s[1:]: n % NP for n, s in enumerate(s for s in steps if s[0] == "ST")}
                    for step in steps:
                        kind, g = step[:2]
                        buf = g % 2
                        if kind == "S":
                            t = step[2]
                            if t == 0 or (own and g and t == 0):
                                pe.wait_ge(*of(f"ld_stack{buf}", L, g, "k" if own else "q", 2))
                                pe.wait_ge(*of("ld_const", 2))
                                pe.wait_ge(*of("ld_kx", "mask"))
                            if own:
                                keys = (t + 1) * P
                                for j in range(GH):
                                    for c in range((keys + CH - 1) // CH):
                                        n = min(CH, keys - c * CH)
                                        s = claim("S", L, "S", g, t, j, c)
                                        on_edge = c * CH + n == keys
                                        mm = pe.matmul(s[:, 0:n], QS[0:MROW, buf, j, t * P:(t + 1) * P], KS[0:MROW, buf, j, c * CH:c * CH + n],
                                                       start=True, stop=not on_edge)
                                        if on_edge:
                                            mm = pe.matmul(s[:, n - P:n], big[:], causal[:, 0, :], start=False, stop=True)
                                        mm.then_inc(*did("pe", L, "S", g, t, j, c))
                            else:
                                s = claim("S", L, "S", g, t)
                                for j in range(GH):
                                    mm = pe.matmul(s[:, j * TX:(j + 1) * TX], QS[0:MROW, buf, j, t * P:(t + 1) * P],
                                                   KX[0:MROW, l, g * GH + j, :], start=True, stop=True)
                                mm.then_inc(*did("pe", L, "S", g, t))
                        elif kind == "MT":
                            pe.wait_ge(*(of("dve", L, "negm", g) if own else of("dve", "free", L, "S", g, NT - 1)))
                            s = claim("S", L, "MT", g)
                            pe.transpose(s[0:GH * NT, 0:P], negm[:, g % 2, :], identf[:]).then_inc(*did("pe", L, "MT", g))
                        elif kind == "ST":
                            kt, j = step[2:]
                            if kt == 0 and j == 0:
                                pe.wait_ge(*of(f"ld_m{buf}", L, g))
                            s = claim("A", L, "ST", g, kt, j)
                            q0_ = kt * P
                            for c in range(2):
                                a = max(q0_, c * CH)
                                if a >= (c + 1) * CH:
                                    continue
                                key_rows = KS[0:MROW + 2, buf, j, kt * P:(kt + 1) * P] if own else KX[0:MROW + 2, l, g * GH + j, :]
                                o = s[0:P if own else TX, a:(c + 1) * CH]
                                edge = own and a == q0_
                                mm = pe.matmul(o, key_rows, QS[0:MROW + 2, buf, j, a:(c + 1) * CH], start=True, stop=not edge)
                                if edge:
                                    mm = pe.matmul(s[:, a:a + P], big[:], causal[:, 1, :], start=False, stop=True)
                            mm.then_inc(*did("pe", L, "ST", g, kt, j))
                        elif kind == "PVA":
                            kt = step[2]
                            if kt == 0:
                                acc = [claim("B0", L, "PV", g, 0), claim("B1", L, "PV", g, 1)]
                            if g == 0 and kt == 0 and own:
                                pe.wait_ge(*of("act", L, "vp", NT - 1))
                            if g == 0 and kt == 0:
                                pe.wait_ge(*of("act", "free", "VX", len(XL) - 1))
                            pe.wait_ge(*of("act", L, "exp", g, kt, GH - 1))
                            nk = NT if own else 1
                            rows = P if own else TX
                            for c in range(2):
                                a = max(kt * P, c * CH)
                                if a >= (c + 1) * CH:
                                    continue
                                final = kt == (min(nk, 4 * (c + 1)) - 1)
                                for j in range(GH):
                                    v = VP[:, kt, g * GH + j, :] if own else VX[0:TX, l, g * GH + j, :]
                                    p = PR[0:rows, ring[g, kt, j], a:(c + 1) * CH]
                                    mm = pe.matmul(acc[c][QUARTER * j:QUARTER * (j + 1), a - c * CH:CH], v, p, start=kt == 0, stop=final,
                                                   tile_position=(0, QUARTER * j))
                            mm.then_inc(*did("pe", L, "PVA", g, kt))
                        elif kind == "NB":
                            s = claim("A", L, "NB", g)
                            pe.wait_ge(*of(f"ld_r{g}", L))
                            for c in range(2):
                                mm = pe.matmul(s[:, c * CH:(c + 1) * CH], E4[:], OT[own][g][:, c * CH:(c + 1) * CH], start=True, stop=True)
                            mm.then_inc(*did("pe", L, "NB", g))
                    pe.wait_ge(*of("dve", L, "onlo", NG - 1))
                    for t in range(NT):
                        s = claim("S", L, "W", t)
                        w = pi[{"B0": "B0p", "C1": "C1o", "D2": "D2o", "E3": "E3id"}[L]]
                        for g in range(NG):
                            mm = split3(s[:, 0:D], parts(ON, g, slice(t * P, (t + 1) * P)), (Wp[:, w, 0, g, :], Wp[:, w, 1, g, :]),
                                        g == 0, g == NG - 1 and L == "E3")
                        if L != "E3":
                            mm = bias_rows(s[:, 0:D], {"B0": "B0p", "C1": "C1o", "D2": "D2o"}[L], P)
                        mm.then_inc(*did("pe", L, "W", t))

                def block_of(N, L, own):
                    turn_x(N)
                    pe.wait_ge(*of("dve", N, "xlo", 1))
                    attention(L, own)

                if "B" in stages:
                    block_of("B", "B0", True)

                if "M" in stages:
                    turn_x("M")
                    pe.wait_ge(*of("dve", "M", "xlo", 1))
                    s = claim("S", "M", "gate")
                    for t in range(NT):
                        for k in range(KD):
                            mm = split3(s[:, t * NE:(t + 1) * NE], parts(XT, k, slice(t * P, (t + 1) * P)), parts(gateW, k), k == 0, k == KD - 1)
                    mm.then_inc(*did("pe", "M", "gate"))
                    order = [(e, c, m) for e in range(NE) for c in range(2) for m in range(NM)]

                    def up(e, c, m):
                        if c == 0 and m == 0:
                            pe.wait_ge(*of("dve", "M", "wlo", e, 1))
                        s = claim("A", "M", "U", e, c, m)
                        w1 = Wm[e % 2][:, 0].rearrange("p s (k n) -> p s k n", k=KD)
                        for k in range(KD):
                            mm = split3(s[:, 0:CH], parts(w1, k, slice(m * P, (m + 1) * P)), parts(XT, k, slice(c * CH, (c + 1) * CH)),
                                        k == 0, k == KD - 1)
                        mm.then_inc(*did("pe", "M", "U", e, c, m))

                    def down(e, c, m):
                        n = (e * 2 + c) * NM + m
                        if m == 0:
                            pair = ("B0", "B1") if (2 * e + c) % 2 == 0 else ("S0", "S1")
                            acc[:] = [claim(pair[0], "M", "D", e, c, 0), claim(pair[1], "M", "D", e, c, 1)]
                        pe.wait_ge(*of("dve", "M", "midlo", e, c, m))
                        w2 = Wm[e % 2][:, 1].rearrange("p s (m n) -> p s m n", m=NM)
                        for i in range(4):
                            o = acc[i // 2][:, (i % 2) * D:(i % 2 + 1) * D]
                            left = (mid[:, n % 4, 0, i * P:(i + 1) * P], mid[:, n % 4, 1, i * P:(i + 1) * P])
                            mm = split3(o, left, parts(w2, m), m == 0 and i % 2 == 0, False, skip_group_check=True)
                            if m == NM - 1:
                                mm = bias_rows(o, f"e{e}", P, last=True, skip_group_check=True)
                        mm.then_inc(*did("pe", "M", "D", e, c, m))

                    acc = [None, None]
                    for n in range(len(order) + 2):
                        if n < len(order):
                            up(*order[n])
                        if n >= 2:
                            down(*order[n - 2])

                if "C" in stages:
                    block_of("C", "C1", False)

                if "L1" in stages:
                    for k in range(KD):
                        s = claim("A", "L1", "XQ", k).bitcast(F16)
                        for t in range(NT):
                            pe.wait_ge(*of("dve", "L1", "xq", t))
                            mm = pe.transpose(s[:, t * P:(t + 1) * P], xq[:, t, k * P:(k + 1) * P], ident[:])
                        mm.then_inc(*did("pe", "L1", "XQ", k))
                    pe.wait_ge(*of("act", "L1", "xqT", 1))

                    def ternary_up(t):
                        s = claim("A", "L1", "H1", t)
                        for c in range(2):
                            for k in range(KD):
                                mm = pe.matmul(s[:, c * CH:(c + 1) * CH], xqT[:, k, t * P:(t + 1) * P], Wq1[:, k, c * CH:(c + 1) * CH],
                                               start=k == 0, stop=k == KD - 1)
                        mm.then_inc(*did("pe", "L1", "H1", t))

                    def ternary_down(t):
                        s = claim("S", "L1", "HQ", t).bitcast(F16)
                        pe.wait_ge(*of("dve", "L1", "hq", t))
                        for m in range(NM):
                            mm = pe.transpose(s[:, m * P:(m + 1) * P], hq[:, t % 2, m * P:(m + 1) * P], ident[:])
                        mm.then_inc(*did("pe", "L1", "HQ", t))
                        s = claim("S", "L1", "H2", t)
                        pe.wait_ge(*of("act", "L1", "hqT", t))
                        for m in range(NM):
                            mm = pe.matmul(s[:, 0:D], hqT[:, t % 2, m * P:(m + 1) * P], Wq2[:, m, :], start=m == 0, stop=m == NM - 1)
                        mm.then_inc(*did("pe", "L1", "H2", t))

                    for t in range(NT + 1):
                        if t < NT:
                            ternary_up(t)
                        if t:
                            ternary_down(t - 1)

                if "D" in stages:
                    block_of("D", "D2", False)

                if "L2" in stages:
                    turn_x("L2")
                    pe.wait_ge(*of("act", "L2", "xf", 1))

                    def butterfly_up(c):
                        for m in range(NM):
                            s = claim("A", "L2", "G", c, m)
                            for k in range(KD):
                                mm = pe.matmul(s[:, 0:CH], Wexp[:, k, m * P:(m + 1) * P], XTf[:, k, c * CH:(c + 1) * CH],
                                               start=k == 0, stop=k == KD - 1)
                            mm.then_inc(*did("pe", "L2", "G", c, m))

                    def butterfly_down(c):
                        for t in range(4 * c, 4 * c + 4):
                            s = claim("S", "L2", "Y", t)
                            pe.wait_ge(*of("act", "L2", "g", c, NM - 1))
                            for m in range(NM):
                                pe.matmul(s[:, 0:D], gT[:, c, m, (t % 4) * P:(t % 4 + 1) * P], RT[:, m, :], start=m == 0, stop=False)
                            bias_rows(s[:, 0:D], "L2con", P, idt=small, last=False)
                            bias_rows(s[:, 0:D], "L2down", P, idt=small).then_inc(*did("pe", "L2", "Y", t))

                    butterfly_up(0)
                    butterfly_up(1)
                    butterfly_down(0)
                    butterfly_down(1)

                if "E" in stages:
                    block_of("E", "E3", False)

                if "F" in stages:
                    turn_x("F")
                    s = claim("S", "F", "R")
                    pe.wait_ge(*of("dve", "F", "xmean", 1))
                    for k in range(KD):
                        mm = pe.matmul(s[0:1, 0:NH], xmean[:, k:k + 1], F3Wr[:, k, :], start=k == 0, stop=k == KD - 1)
                    mm.then_inc(*did("pe", "F", "R"))
                    s = claim("S", "F", "G")
                    pe.wait_ge(*of("dve", "F", "gates"))
                    pe.matmul(s[:, 0:HS], onesf[0:1, :], rt[0:1, 48:48 + HS], start=True, stop=True).then_inc(*did("pe", "F", "G"))
                    pe.wait_ge(*of("dve", "F", "xlo", 1))
                    pe.wait_ge(*of("dve", "F", "wsel_lo"))
                    for w, n in enumerate("qk"):
                        for m in range(KD):
                            project(("F3", n, m), lambda k: (Wsel[:, w, 0, k, m * P:(m + 1) * P], Wsel[:, w, 1, k, m * P:(m + 1) * P]))
                    pe.wait_ge(*of("dve", "F", "bv_lo"))
                    for t in range(NT):
                        s = claim("S", "F3", "v", t)
                        for k in range(KD):
                            split3(s[:, 0:D], parts(XT, k, slice(t * P, (t + 1) * P)), (Wsel[:, 2, 0, k, :], Wsel[:, 2, 1, k, :]), k == 0, False)
                        pe.matmul(s[:, 0:D], ident[0:1, 0:1].to_broadcast([1, P]), bvh[:, 0, :], start=False, stop=False)
                        pe.matmul(s[:, 0:D], ident[0:1, 0:1].to_broadcast([1, P]), bvh[:, 1, :], start=False, stop=True).then_inc(*did("pe", "F3", "v", t))
                    pe.wait_ge(*of("ld_stack0", "F3", 5))
                    for step in last_attention_steps():
                        kind, h = step[:2]
                        if kind == "S":
                            t = step[2]
                            for c in range(2):
                                s = claim("S", "F3", "S", h, t, c)
                                pe.matmul(s[:], QS[:, 0, h, t * P:(t + 1) * P], KS[:, 0, h, c * CH:(c + 1) * CH], start=True, stop=False)
                                pe.matmul(s[:], QS[0:MROW, 1, h, t * P:(t + 1) * P], KS[0:MROW, 1, h, c * CH:(c + 1) * CH],
                                          start=False, stop=True).then_inc(*did("pe", "F3", "S", h, t, c))
                        elif kind == "MT":
                            pe.wait_ge(*of("dve", "F3", "negm", h))
                            s = claim("S", "F3", "MT", h)
                            pe.transpose(s[0:NT, 0:P], negm[:, h % 2, 0:NT], identf[:]).then_inc(*did("pe", "F3", "MT", h))
                        elif kind == "ST":
                            kt = step[2]
                            if kt == 0:
                                pe.wait_ge(*of(f"ld_m{h % 2}", "F3", h))
                            s = claim("A", "F3", "ST", h, kt)
                            for c in range(2):
                                pe.matmul(s[:, c * CH:(c + 1) * CH], KS[:, 0, h, kt * P:(kt + 1) * P], QS[:, 0, h, c * CH:(c + 1) * CH],
                                          start=True, stop=False)
                                mm = pe.matmul(s[:, c * CH:(c + 1) * CH], KS[0:MROW + 2, 1, h, kt * P:(kt + 1) * P],
                                               QS[0:MROW + 2, 1, h, c * CH:(c + 1) * CH], start=False, stop=True)
                            mm.then_inc(*did("pe", "F3", "ST", h, kt))
                        elif kind == "PV":
                            kt = step[2]
                            if kt == 0:
                                acc = [claim("B0", "F3", "PV", h, 0), claim("B1", "F3", "PV", h, 1)]
                                if h == 0:
                                    pe.wait_ge(*of("act", "F3", "vp", NT - 1))
                            pe.wait_ge(*of("act", "F3", "exp", h, kt))
                            for c in range(2):
                                mm = pe.matmul(acc[c][0:TX], VP4[:, kt, h, :], PR4[:, (h * NT + kt) % NP, c * CH:(c + 1) * CH],
                                               start=kt == 0, stop=kt == NT - 1)
                            mm.then_inc(*did("pe", "F3", "PV", h, "k", kt))
                        elif kind == "NB":
                            s = claim("A", "F3", "NB", h)
                            pe.wait_ge(*of(f"ld_r{h}", "F3"))
                            for c in range(2):
                                mm = pe.matmul(s[0:TX, c * CH:(c + 1) * CH], E64[:], OT4[h % 2][:, c * CH:(c + 1) * CH], start=True, stop=True)
                            mm.then_inc(*did("pe", "F3", "NB", h))
                    pe.wait_ge(*of("dve", "F3", "onlo", HS - 1))
                    for t in range(NT):
                        s = claim("S", "F3", "W", t)
                        for h in range(HS):
                            split3(s[:, 0:D], (ON4[:, 0, h, t * P:(t + 1) * P], ON4[:, 1, h, t * P:(t + 1) * P]),
                                   (Wp[0:TX, pi["F3o"], 0, h, :], Wp[0:TX, pi["F3o"], 1, h, :]), h == 0, False)
                        bias_rows(s[:, 0:D], "F3o", P).then_inc(*did("pe", "F3", "W", t))
                batch_end(pe, "pe")

        @block.scalar
        def _(act):
            act.wait_ge(once["load"], 16 * 19)
            act.activation(Wf[:, :, 0].rearrange("p w k d -> p w (k d)"),
                           stage_flat[:, 0:len(FLAT) * FLAT_N].rearrange("p (w n) -> p w n", n=FLAT_N), ACT.Copy, scale=WS).then_inc(once["act"], 1)
            act.activation(Wp[:, :, 0].rearrange("p w k d -> p w (k d)"), stage_pad.rearrange("p (w n) -> p w n", n=PAD_N),
                           ACT.Copy, scale=WS).then_inc(once["act"], 1)
            act.wait_ge(once["dve"], 2)
            act.activation(lamt[:, 2:4], lamt[:, 0:2], ACT.Exp).then_inc(once["act"], 1)
            batch_end(act, "act")

            with act.Fori(0, NB):
                def norm_std(N):
                    act.wait_ge(*of("dve", N, "mv"))
                    act.activation(sd[:], mv[:, :, 1], ACT.Sqrt, bias=epsc[:, 0:1], scale=1.0).then_inc(*did("act", N, "sd"))

                def x_hi(N):
                    for k in range(KD):
                        act.wait_ge(*of("pe", "T", N, k))
                        act.activation(XT[:, 0, k], slot("T", N, k), ACT.Copy).then_inc(*did("act", N, "xhi", k))

                def x_affine(N, g_, b_):
                    for k in range(KD):
                        act.wait_ge(*of("pe", "T", N, k))
                        if k:
                            act.wait_ge(*of("dve", N, "xlo", k - 1))
                        act.activation(tmp, slot("T", N, k), ACT.Identity, bias=BC[:, bc[b_] + k:bc[b_] + k + 1],
                                       scale=BC[:, bc[g_] + k:bc[g_] + k + 1]).then_inc(*frees("act", "T", N, k))

                def q_f32(L, n, scale):
                    for m in range(KD):
                        act.wait_ge(*of("pe", L, n, m))
                        if (n, m) != ("q", 0):
                            act.wait_ge(*of("dve", L, *(("qlo", 0) if (n, m) == ("q", 1) else ("qlo", 1) if m == 0 else ("klo", 0))))
                        name = L + n
                        b = BC[:, bc[name] + m:bc[name] + m + 1] if name in bc else epsc[:, 1:2]
                        act.activation(tmp, slot(L, n, m), ACT.Identity, bias=b, scale=scale / WS).then_inc(*frees("act", L, n, m))

                act.wait_ge(*of("ld_ctx"))
                act.activation(CT[:, 0, :, 0:TC], CTf[:], ACT.Copy).then_inc(*did("act", "cthi"))
                act.wait_ge(*of("pe", "K0"))
                act.activation(KP0[:, 0, 0:TC], slot("K0")[:, 0:TC], ACT.Copy, scale=1.0 / WS).then_inc(*did("act", "kp0hi"))
                act.wait_ge(*of("pe", "V0"))
                act.activation(VP0[0:TC, 0, :], slot("V0")[0:TC, 0:D], ACT.Copy, scale=1.0 / WS).then_inc(*did("act", "vp0hi"))
                for l, L in enumerate(XL):
                    for m in range(KD):
                        act.wait_ge(*of("pe", "KX", l, m))
                        b = BC[:, bc[L + "k"] + m:bc[L + "k"] + m + 1] if L != "C1" else epsc[:, 1:2]
                        act.activation(kxf[:, l, m, 0:TC], slot("KX", l, m)[:, 0:TC], ACT.Identity, bias=b,
                                       scale=1.0 / WS).then_inc(*frees("act", "KX", l, m))
                    act.wait_ge(*of("pe", "VX", l))
                    act.activation(VX[0:TC, l, :, 0:DH], slot("VX", l)[0:TC, 0:D].rearrange("p (h d) -> p h d", d=DH), ACT.Copy,
                                   scale=1.0 / WS).then_inc(*frees("act", "VX", l))

                if "A" in stages:
                    norm_std("A")
                    x_hi("A")
                    for h in range(2):
                        act.wait_ge(*of("pe", "A", "Q", h))
                        act.activation(q0[:, 0, h], slot("A", "Q", h), ACT.Copy, scale=float(P) ** -0.5 / WS).then_inc(*did("act", "A", "qhi", h))
                    for t in range(NT):
                        act.wait_ge(*of("dve", "A", "m", t))
                        if t >= 2:
                            act.wait_ge(*of("dve", "A", "p", t - 2))
                        for h in range(2):
                            act.activation(E0[:, t % 2, h], slot("A", "S", t)[:, h * TC:(h + 1) * TC], ACT.Exp, bias=sm[:, 2 * t + h:2 * t + h + 1],
                                           scale=1.0, accum_out=sm[:, 16 + 2 * t + h:17 + 2 * t + h]
                                           ).then_inc(*(frees("act", "A", "S", t) if h else did("act", "A", "e0", t)))
                    act.wait_ge(*of("pe", "A", "PT"))
                    act.activation(AT0[0:TC, 0, :], slot("A", "PT")[0:TC], ACT.Copy).then_inc(*did("act", "A", "pthi"))
                    for m in range(KD):
                        act.wait_ge(*of("pe", "A", "O", m))
                        act.activation(AO0[:, 0, m], slot("A", "O", m), ACT.Copy).then_inc(*did("act", "A", "ohi", m))
                    for t in range(NT):
                        act.wait_ge(*of("pe", "A", "N", t))
                        if t >= 2:
                            act.wait_ge(*of("act", "free", "A", "N", t - 2))
                        act.activation(sq0[:, t % 2], slot("A", "N", t)[:, 0:D], ACT.Square,
                                       accum_out=sm[:, 64 + t:65 + t]).then_inc(*frees("act", "A", "N", t))
                    act.wait_ge(*of("act", "free", "A", "N", NT - 1))
                    act.activation(sm[:, 72:80], sm[:, 64:72], ACT.Sqrt, bias=epsc[:, 0:1], scale=1.0 / D).then_inc(*did("act", "A", "rms"))

                def exps(L, own, steps):
                    n = 0
                    for step in steps:
                        if step[0] == "ST":
                            _, g, kt, j = step
                            act.wait_ge(*of("pe", L, "ST", g, kt, j))
                            if n >= NP:
                                g0, k0, j0 = [s[1:] for s in steps if s[0] == "ST"][n - NP]
                                act.wait_ge(*of("pe", L, "PVA", g0, k0))
                            rows = P if own else TX
                            act.activation(PR[0:rows, n % NP, kt * P:T], slot(L, "ST", g, kt, j)[0:rows, kt * P:T],
                                           ACT.Exp).then_inc(*did("act", L, "exp", g, kt, j))
                            led.freed[(L, "ST", g, kt, j)] = ("act", (L, "exp", g, kt, j))
                            n += 1
                        elif step[0] == "PVA" and step[2] == (NT - 1 if own else 0):
                            g = step[1]
                            act.wait_ge(*of("pe", L, "PVA", g, step[2]))
                            if own and g >= 2:
                                act.wait_ge(*of("dve", L, "onf", g - 2))
                            for c in range(2):
                                act.activation(OT[own][g][:, c * CH:(c + 1) * CH], slot(L, "PV", g, c), ACT.Copy).then_inc(*did("act", L, "ot", g, c))
                                led.freed[(L, "PV", g, c)] = ("act", (L, "ot", g, c))

                def attention(L, own):
                    q_f32(L, "q", 0.25)
                    if own:
                        q_f32(L, "k", 1.0)
                        act.wait_ge(*of("dve", L, "ones"))
                        for t in range(NT):
                            act.wait_ge(*of("pe", L, "v", t))
                            act.activation(VP[:, t, :, 0:DH], slot(L, "v", t)[:, 0:D].rearrange("p (h d) -> p h d", d=DH), ACT.Copy,
                                           scale=1.0 / WS).then_inc(*did("act", L, "vp", t))
                            led.freed[(L, "v", t)] = ("act", (L, "vp", t))
                    exps(L, own, attention_steps(own))

                if "B" in stages:
                    norm_std("B1")
                    norm_std("B")
                    x_affine("B", "ln1_g", "ln1_b")
                    attention("B0", True)

                if "M" in stages:
                    norm_std("M")
                    x_affine("M", "ln2_g", "ln2_b")
                    act.wait_ge(*of("dve", "M", "d"))
                    act.activation(sm[:, 88:96], sm[:, 80:88], ACT.Exp).then_inc(*did("act", "M", "e"))

                    def weights_hi(e, w):
                        act.wait_ge(*of(f"ld_wexp{w}", e))
                        if e >= 2:
                            act.wait_ge(*of("pe", "M", "D", e - 2, 1, NM - 1))
                        act.activation(Wm[e % 2][:, w, 0], WSt[:, w], ACT.Copy, scale=WS).then_inc(*did("act", "M", "whi", e, w))

                    weights_hi(0, 0)
                    weights_hi(0, 1)
                    n = 0
                    for e in range(NE):
                        for c in range(2):
                            for m in range(NM):
                                act.wait_ge(*of("pe", "M", "U", e, c, m))
                                if n >= 3:
                                    act.wait_ge(*of("dve", "M", "midlo", *back(e, c, m, 3)))
                                act.activation(midf[:, n % 3], slot("M", "U", e, c, m)[:, 0:CH], ACT.Gelu,
                                               bias=BC[:, BC_E1 + e * NM + m:BC_E1 + e * NM + m + 1],
                                               scale=1.0 / WS).then_inc(*frees("act", "M", "U", e, c, m))
                                n += 1
                                if e + 1 < NE and (c, m) in ((0, 4), (1, 0)):
                                    weights_hi(e + 1, c)

                if "C" in stages:
                    norm_std("C")
                    x_hi("C")
                    attention("C1", False)

                if "L1" in stages:
                    norm_std("L1")
                    for k in range(KD):
                        act.wait_ge(*of("pe", "L1", "XQ", k))
                        act.activation(xqT[:, k], slot("L1", "XQ", k).bitcast(F16)[:, 0:T], ACT.Copy).then_inc(*did("act", "L1", "xqT", k))
                        led.freed[("L1", "XQ", k)] = ("act", ("L1", "xqT", k))
                    for t in range(NT + 1):
                        if t < NT:
                            act.wait_ge(*of("dve", "L1", "h", t))
                            act.activation(hb[:, t % 3], hb[:, t % 3], ACT.Gelu).then_inc(*did("act", "L1", "gelu", t))
                        if t:
                            act.wait_ge(*of("pe", "L1", "HQ", t - 1))
                            if t >= 3:
                                act.wait_ge(*of("pe", "L1", "H2", t - 3))
                            act.activation(hqT[:, (t - 1) % 2], slot("L1", "HQ", t - 1).bitcast(F16)[:, 0:HID], ACT.Copy
                                           ).then_inc(*did("act", "L1", "hqT", t - 1))
                            led.freed[("L1", "HQ", t - 1)] = ("act", ("L1", "hqT", t - 1))

                if "D" in stages:
                    norm_std("D")
                    x_hi("D")
                    attention("D2", False)

                if "L2" in stages:
                    norm_std("L2")
                    for k in range(KD):
                        act.wait_ge(*of("pe", "T", "L2", k))
                        act.activation(XTf[:, k], slot("T", "L2", k), ACT.Copy).then_inc(*did("act", "L2", "xf", k))
                        led.freed[("T", "L2", k)] = ("act", ("L2", "xf", k))
                    for c in range(2):
                        for m in range(NM):
                            act.wait_ge(*of("pe", "L2", "G", c, m))
                            act.activation(gT[:, c, m], slot("L2", "G", c, m)[:, 0:CH], ACT.Gelu, bias=upb[:, m:m + 1],
                                           scale=1.0).then_inc(*did("act", "L2", "g", c, m))
                            led.freed[("L2", "G", c, m)] = ("act", ("L2", "g", c, m))

                if "E" in stages:
                    norm_std("E")
                    x_hi("E")
                    attention("E3", False)

                if "F" in stages:
                    norm_std("F")
                    x_hi("F")
                    act.wait_ge(*of("dve", "F", "lmax"))
                    act.activation(rt[0:1, 0:NH], rt[0:1, 0:NH], ACT.Exp, bias=rt[0:1, 24:25], scale=1.0,
                                   accum_out=rt[0:1, 25:26]).then_inc(*did("act", "F", "e1"))
                    act.wait_ge(*of("dve", "F", "index"))
                    act.activation(rt[0:1, 40:44], rt[0:1, 28:32], ACT.Exp, bias=rt[0:1, 36:37], scale=1.0,
                                   accum_out=rt[0:1, 44:45]).then_inc(*did("act", "F", "e2"))
                    act.activation(rt[0:1, 45:46], rt[0:1, 36:37], ACT.Exp).then_inc(*did("act", "F", "e3"))
                    act.wait_ge(*of("dve", "F", "wscaled"))
                    act.activation(Wsel[:, :, 0], Wst, ACT.Copy).then_inc(*did("act", "F", "wsel_hi"))
                    act.wait_ge(*of("dve", "F", "qkscale"))
                    for w, n in enumerate("qk"):
                        for m in range(KD):
                            act.wait_ge(*of("pe", "F3", n, m))
                            if (n, m) != ("q", 0):
                                act.wait_ge(*of("dve", "F3", *(("qlo", 0) if (n, m) == ("q", 1) else ("qlo", 1) if m == 0 else ("klo", 0))))
                            act.activation(tmp, slot("F3", n, m), ACT.Identity, bias=bsel[:, 2 * w + m:2 * w + m + 1],
                                           scale=gcol[:, 4 + 2 * w + m:5 + 2 * w + m]).then_inc(*frees("act", "F3", n, m))
                    act.wait_ge(*of("dve", "F3", "ones"))
                    for t in range(NT):
                        act.wait_ge(*of("pe", "F3", "v", t))
                        act.activation(VP4[:, t, :, 0:DS], slot("F3", "v", t)[:, 0:D].rearrange("p (h d) -> p h d", d=DS), ACT.Copy,
                                       scale=1.0 / WS).then_inc(*did("act", "F3", "vp", t))
                        led.freed[("F3", "v", t)] = ("act", ("F3", "vp", t))
                    act.wait_ge(*of("pe", "F3", "v", NT - 1))
                    n = 0
                    for step in last_attention_steps():
                        if step[0] == "ST":
                            _, h, kt = step
                            act.wait_ge(*of("pe", "F3", "ST", h, kt))
                            if n >= NP:
                                act.wait_ge(*of("pe", "F3", "PV", (n - NP) // NT, "k", (n - NP) % NT))
                            act.activation(PR4[:, n % NP], slot("F3", "ST", h, kt), ACT.Exp).then_inc(*did("act", "F3", "exp", h, kt))
                            led.freed[("F3", "ST", h, kt)] = ("act", ("F3", "exp", h, kt))
                            n += 1
                        elif step[0] == "PV" and step[2] == NT - 1:
                            h = step[1]
                            act.wait_ge(*of("pe", "F3", "PV", h, "k", NT - 1))
                            if h >= 2:
                                act.wait_ge(*of("dve", "F3", "onf", h - 2))
                            for c in range(2):
                                act.activation(OT4[h % 2][:, c * CH:(c + 1) * CH], slot("F3", "PV", h, c)[0:TX], ACT.Copy
                                               ).then_inc(*did("act", "F3", "ot", h, c))
                                led.freed[("F3", "PV", h, c)] = ("act", ("F3", "ot", h, c))
                batch_end(act, "act")

        @block.gpsimd
        def _(pool):
            pool.memset(onesf[:], 1.0).then_inc(once["pool"], 1)
            pool.memset(VX[:], 0.0).then_inc(once["pool"], 1)
            pool.memset(mpart[:], -3.0e38).then_inc(once["pool"], 1)
            pool.wait_ge(once["pool"], 3)
            pool.memset(VX[0:TX, :, :, DH:QUARTER], 1.0).then_inc(once["pool"], 1)
            pool.wait_ge(once["bf_rows"], 32)
            for i in range(10):
                s = 9 - i
                pool.wait_ge(once[f"down_w{i % 2}"], 16 * (i // 2 + 1))
                butterfly(pool, once["down"], bC, tC, ringC[:, i % 2], s, i, True)
            batch_end(pool, "pool")
            with pool.Fori(0, NB):
                batch_end(pool, "pool")

        @block.vector
        def _(dve):
            dve.wait_ge(once["load"], 16 * 19)
            pr = lamr[:, 4 * P:6 * P].rearrange("p (a c) -> p a c", a=2)
            dve.tensor_tensor(pr, lamr[:, 0:4 * P].rearrange("p (a b c) -> p a b c", a=2, b=2)[:, :, 0],
                              lamr[:, 0:4 * P].rearrange("p (a b c) -> p a b c", a=2, b=2)[:, :, 1], ALU.mult).then_inc(once["dve"], 1)
            dve.wait_ge(once["dve"], 1)
            dve.tensor_reduce(lamt[:, 0:2], pr, AX, ALU.add).then_inc(once["dve"], 1)
            dve.tensor_reduce(wsc[:, 0:1], fW1, AX, ALU.add, apply_absolute_value=True).then_inc(once["wsum"], 1)
            dve.tensor_reduce(wsc[:, 1:2], fW2, AX, ALU.add, apply_absolute_value=True).then_inc(once["wsum"], 1)
            count = 2
            for w in range(len(CTXW)):
                if w >= 4:
                    dve.wait_ge(once[f"store{w % 4}"], 16)
                src = stage_flat[:, (len(FLAT) + w) * FLAT_N:(len(FLAT) + w + 1) * FLAT_N]
                dst = ctx_split[:, (w % 4) * 2 * FLAT_N:(w % 4 + 1) * 2 * FLAT_N]
                dve.tensor_scalar(dst[:, 0:FLAT_N], src, WS, None, ALU.mult).then_inc(once["dve"], 1)
                count += 1
                dve.wait_ge(once["dve"], count)
                dve.scalar_tensor_tensor(dst[:, FLAT_N:2 * FLAT_N], src, WS, dst[:, 0:FLAT_N], ALU.mult, ALU.subtract).then_inc(once["ctxw"], 1)
            dve.wait_ge(once["act"], 2)
            dve.scalar_tensor_tensor(Wf[:, :, 1].rearrange("p w k d -> p w (k d)"),
                                     stage_flat[:, 0:len(FLAT) * FLAT_N].rearrange("p (w n) -> p w n", n=FLAT_N), WS,
                                     Wf[:, :, 0].rearrange("p w k d -> p w (k d)"), ALU.mult, ALU.subtract).then_inc(once["dve"], 1)
            dve.scalar_tensor_tensor(Wp[:, :, 1].rearrange("p w k d -> p w (k d)"), stage_pad.rearrange("p (w n) -> p w n", n=PAD_N), WS,
                                     Wp[:, :, 0].rearrange("p w k d -> p w (k d)"), ALU.mult, ALU.subtract).then_inc(once["dve"], 1)
            count += 2
            dve.wait_ge(once["dve"], count)
            dve.memset(rt[0:1, 95:96], 0.0).then_inc(once["staged"], 1)

            def then(ins):
                nonlocal count
                ins.then_inc(once["dve"], 1)
                count += 1
                dve.wait_ge(once["dve"], count)

            then(dve.memset(BR[:], 0.0))
            nb = len(BROW)
            then(dve.tensor_scalar(BR[0:nb, 0], brf[0:nb], WS, None, ALU.mult))
            then(dve.scalar_tensor_tensor(BR[0:nb, 1], brf[0:nb], WS, BR[0:nb, 0], ALU.mult, ALU.subtract))
            gw = gwf[:, :].rearrange("p (k n) -> p k n", k=KD)
            then(dve.tensor_scalar(gateW[:, 0], gw, WS, None, ALU.mult))
            then(dve.scalar_tensor_tensor(gateW[:, 1], gw, WS, gateW[:, 0], ALU.mult, ALU.subtract))
            for n in ("B0q", "D2q", "E3q"):
                then(dve.tensor_scalar(BC[:, bc[n]:bc[n] + 2], BC[:, bc[n]:bc[n] + 2], 0.25, None, ALU.mult))
            then(dve.tensor_scalar(big[:], ident[:], BIG, None, ALU.mult))
            then(dve.tensor_scalar(small[:], ident[:], 1.0 / WS, None, ALU.mult))
            dve.wait_ge(once["act"], 3)
            then(dve.tensor_tensor(lamt[:, 4:5], lamt[:, 3:4], lamt[:, 2:3], ALU.subtract))
            then(dve.tensor_scalar(lamt[:, 5:6], lamt[:, 4:5], -LAM0, None, ALU.add))
            dve.wait_ge(once["pe"], 1)
            then(dve.tensor_scalar(wsc[:, 2:4], SLOT["S0"][:, 0:2], 1.0 / (HID * D), EPS, ALU.mult, ALU.max))
            then(dve.reciprocal(wsc[:, 4:6], wsc[:, 2:4]))
            for i, (f, w) in enumerate(((fW1, Wq1[:, :, :].rearrange("p k n -> p (k n)")), (fW2, Wq2[:, :, :].rearrange("p k n -> p (k n)")))):
                then(dve.tensor_scalar(f, f, wsc[:, 4 + i:5 + i], MAGIC, ALU.mult, ALU.add))
                then(dve.tensor_scalar(f, f, -MAGIC, 1.0, ALU.add, ALU.min))
                then(dve.tensor_scalar(w, f, -1.0, None, ALU.max))
            then(dve.tensor_scalar(wsc[:, 2:4], wsc[:, 2:4], 1.0 / QB, None, ALU.mult))
            dve.wait_ge(once["bf_rows"], 32)
            for s in range(10):
                dve.wait_ge(once[f"up_w{s % 2}"], 16 * (s // 2 + 1))
                butterfly(dve, once["up"], bE, tE, ringE[:, s % 2], s, s, False)
            dve.wait_ge(once["up"], 180)
            then(dve.tensor_copy(Wexp[:], bE[:, 0:KD]))
            dve.wait_ge(once["pe"], 2)
            then(dve.tensor_tensor(upb[:], SLOT["S1"][:, 0:NM], BC[:, BC_UP:BC_UP + NM], ALU.add))
            dve.wait_ge(once["pe"], 3)
            then(dve.tensor_copy(RT[:].rearrange("p m d -> p (m d)"), flat[:, 0:NM * D]))
            batch_end(dve, "dve")

            with dve.Fori(0, NB):
                def step(*key):
                    return did("dve", *key)

                def norm(N, src, dst):
                    for t in range(NT):
                        dve.bn_stats(stats[:, t], src[:, t]).then_inc(*step(N, "bn", t))
                    for t in range(NT):
                        dve.wait_ge(*of("dve", N, "bn", t))
                        dve.bn_aggr(mv[:, t], stats[:, t]).then_inc(*(step(N, "mv") if t == NT - 1 else step(N, "ag", t)))
                    dve.wait_ge(*of("act", N, "sd"))
                    dve.reciprocal(rstd[:], sd[:]).then_inc(*step(N, "rstd"))
                    dve.wait_ge(*of("dve", N, "rstd"))
                    for t in range(NT):
                        dve.tensor_scalar(dst[:, t], src[:, t], mv[:, t, 0:1], rstd[:, t:t + 1], ALU.subtract, ALU.mult).then_inc(*step(N, "xn", t))

                def x_lo(N):
                    for k in range(KD):
                        dve.wait_ge(*of("act", N, "xhi", k))
                        if N == "F":
                            dve.tensor_reduce(xmean[:, k:k + 1], slot("T", N, k), AX, ALU.add).then_inc(*step(N, "xmean", k))
                        dve.tensor_tensor(XT[:, 1, k], slot("T", N, k), XT[:, 0, k], ALU.subtract).then_inc(*step(N, "xlo", k))
                        led.freed[("T", N, k)] = ("dve", (N, "xlo", k))

                def halves(src, hi, lo, ready, key):
                    dve.wait_ge(*ready)
                    dve.tensor_copy(hi, src).then_inc(*step(*key, "hi"))
                    dve.wait_ge(*of("dve", *key, "hi"))
                    dve.tensor_tensor(lo, src, hi, ALU.subtract).then_inc(*step(*key))

                def x_affine(N):
                    for k in range(KD):
                        halves(tmp, XT[:, 0, k], XT[:, 1, k], of("act", "free", "T", N, k), (N, "xlo", k))

                dve.wait_ge(*of("ld_mask"))
                dve.tensor_scalar(maskb[:, :, 0:TC], maskr[:, 0:TC].unsqueeze(1).broadcast_to([1, NH, TC]), 0.0, -BIG, ALU.is_gt, ALU.mult).then_inc(*step("mask"))
                dve.wait_ge(*of("act", "cthi"))
                dve.tensor_tensor(CT[:, 1, :, 0:TC], CTf[:], CT[:, 0, :, 0:TC], ALU.subtract).then_inc(*step("ctlo"))
                dve.wait_ge(*of("act", "kp0hi"))
                dve.scalar_tensor_tensor(KP0[:, 1, 0:TC], slot("K0")[:, 0:TC], 1.0 / WS, KP0[:, 0, 0:TC], ALU.mult, ALU.subtract).then_inc(*step("A", "kp0"))
                led.freed[("K0",)] = ("dve", ("A", "kp0"))
                dve.wait_ge(*of("act", "vp0hi"))
                dve.scalar_tensor_tensor(VP0[0:TC, 1], slot("V0")[0:TC, 0:D], 1.0 / WS, VP0[0:TC, 0], ALU.mult, ALU.subtract).then_inc(*step("A", "vp0"))
                led.freed[("V0",)] = ("dve", ("A", "vp0"))
                dve.wait_ge(*of("act", "free", "KX", len(XL) - 1, KD - 1))
                for s in range(2):
                    if s:
                        dve.wait_ge(*of("dve", "kxhi"))
                        dve.tensor_tensor(kxs[:, 1, :, :, 0:TC], kxf[:, :, :, 0:TC], kxs[:, 0, :, :, 0:TC], ALU.subtract).then_inc(*step("kxs"))
                    else:
                        dve.tensor_copy(kxs[:, 0, :, :, 0:TC], kxf[:, :, :, 0:TC]).then_inc(*step("kxhi"))
                dve.wait_ge(*of("ld_x"))
                if "A" not in stages:
                    dve.wait_ge(*of("ld_kx", "mask"))

                if "A" in stages:
                    norm("A", X, XN["A"])
                    x_lo("A")
                    for h in range(2):
                        dve.wait_ge(*of("act", "A", "qhi", h))
                        dve.scalar_tensor_tensor(q0[:, 1, h], slot("A", "Q", h), float(P) ** -0.5 / WS, q0[:, 0, h], ALU.mult,
                                                 ALU.subtract).then_inc(*step("A", "qlo", h))
                        led.freed[("A", "Q", h)] = ("dve", ("A", "qlo", h))
                    for t in range(NT + 1):
                        if t < NT:
                            dve.wait_ge(*of("pe", "A", "S", t))
                            dve.tensor_reduce(sm[:, 2 * t:2 * t + 2], slot("A", "S", t)[:, 0:2 * TC].rearrange("p (h c) -> p h c", h=2), AX, ALU.max,
                                              negate=True).then_inc(*step("A", "m", t))
                        if t:
                            u = t - 1
                            dve.wait_ge(*of("act", "free", "A", "S", u))
                            dve.reciprocal(sm[:, 32 + 2 * u:34 + 2 * u], sm[:, 16 + 2 * u:18 + 2 * u]).then_inc(*step("A", "r", u))
                            dve.wait_ge(*of("dve", "A", "r", u))
                            dve.tensor_tensor(sm[:, 48 + u:49 + u], sm[:, 33 + 2 * u:34 + 2 * u], lamt[:, 5:6], ALU.mult).then_inc(*step("A", "r1", u))
                            dve.wait_ge(*of("dve", "A", "r1", u))
                            dve.tensor_scalar(A0[:, u], E0[:, u % 2, 1], sm[:, 48 + u:49 + u], None, ALU.mult).then_inc(*step("A", "p1", u))
                            dve.wait_ge(*of("dve", "A", "p1", u))
                            dve.scalar_tensor_tensor(A0[:, u], E0[:, u % 2, 0], sm[:, 32 + 2 * u:33 + 2 * u], A0[:, u], ALU.mult,
                                                     ALU.add).then_inc(*step("A", "p", u))
                    dve.wait_ge(*of("act", "A", "pthi"))
                    dve.tensor_tensor(AT0[0:TC, 1], slot("A", "PT")[0:TC], AT0[0:TC, 0], ALU.subtract).then_inc(*step("A", "ptlo"))
                    led.freed[("A", "PT")] = ("dve", ("A", "ptlo"))
                    for m in range(KD):
                        dve.wait_ge(*of("act", "A", "ohi", m))
                        dve.tensor_tensor(AO0[:, 1, m], slot("A", "O", m), AO0[:, 0, m], ALU.subtract).then_inc(*step("A", "olo", m))
                        led.freed[("A", "O", m)] = ("dve", ("A", "olo", m))
                    dve.wait_ge(*of("act", "A", "rms"))
                    dve.reciprocal(sm[:, 120:128], sm[:, 72:80]).then_inc(*step("A", "rr"))
                    dve.wait_ge(*of("dve", "A", "rr"))
                    dve.tensor_scalar(sm[:, 128:136], sm[:, 120:128], (1.0 - LAM0) / WS, None, ALU.mult).then_inc(*step("A", "rw"))
                    dve.wait_ge(*of("dve", "A", "rw"))
                    for t in range(NT):
                        dve.wait_ge(*of("pe", "A", "W", t))
                        dve.scalar_tensor_tensor(X[:, t], slot("A", "W", t)[:, 0:D], sm[:, 128 + t:129 + t], X[:, t], ALU.mult,
                                                 ALU.add).then_inc(*step("A", "x", t))
                        led.freed[("A", "W", t)] = ("dve", ("A", "x", t))
                    dve.wait_ge(*of("dve", "A", "x", NT - 1))

                def maxima(L, own, step_):
                    _, g, t = step_
                    last = None
                    if own:
                        for j in range(GH):
                            for c in range(((t + 1) * P + CH - 1) // CH):
                                n = min(CH, (t + 1) * P - c * CH)
                                dve.wait_ge(*of("pe", L, "S", g, t, j, c))
                                dve.tensor_reduce(mpart[:, j * NT + t, c:c + 1], slot(L, "S", g, t, j, c)[:, 0:n], AX,
                                                  ALU.max).then_inc(*frees("dve", L, "S", g, t, j, c))
                                last = (L, "S", g, t, j, c)
                    else:
                        dve.wait_ge(*of("pe", L, "S", g, t))
                        if g >= 2:
                            dve.wait_ge(*of("pe", L, "MT", g - 2))
                        dve.tensor_reduce(negm[:, g % 2].rearrange("p (j t) -> p j t", t=NT)[:, :, t],
                                          slot(L, "S", g, t)[:, 0:GH * TX].rearrange("p (j c) -> p j c", c=TX), AX, ALU.max,
                                          negate=True).then_inc(*frees("dve", L, "S", g, t))
                        last = (L, "S", g, t)
                    return last

                def minus_max_rows(L, g, last, n):
                    if n:
                        dve.wait_ge(*of("dve", "free", *last))
                        dve.tensor_reduce(negm[:, g % 2, 0:n], mpart[:, 0:n], AX, ALU.max, negate=True).then_inc(*step(L, "negm", g))

                def minus_max_parts(L, g, n):
                    dve.wait_ge(*of("pe", L, "MT", g))
                    if g >= 2:
                        dve.wait_ge(*of(f"st_m{g % 2}", L, g - 2))
                    dve.tensor_copy(mrow[0:n, g % 2, 0], slot(L, "MT", g)[0:n, 0:P]).then_inc(*step(L, "mhi", g))
                    dve.wait_ge(*of("dve", L, "mhi", g))
                    dve.tensor_tensor(mrow[0:n, g % 2, 1], slot(L, "MT", g)[0:n, 0:P], mrow[0:n, g % 2, 0], ALU.subtract).then_inc(*step(L, "mrow", g))
                    led.freed[(L, "MT", g)] = ("dve", (L, "mrow", g))

                def inverse_sums(L, g, w):
                    dve.wait_ge(*of(f"ld_s{g}", L))
                    dve.reciprocal(rinv[:, g, 0:w], rsum[:, g, 0:w]).then_inc(*step(L, "rinv", g))

                def normalised(L, own, g):
                    dve.wait_ge(*of("pe", L, "NB", g))
                    dve.tensor_tensor(tmp, OT[own][g], slot(L, "NB", g), ALU.mult).then_inc(*step(L, "onf", g))
                    led.freed[(L, "NB", g)] = ("dve", (L, "onf", g))
                    halves(tmp, ON[:, 0, g], ON[:, 1, g], of("dve", L, "onf", g), (L, "onlo", g))
                    dve.wait_ge(*of("dve", L, "onlo", g))

                def attention(L, own, dst):
                    for m in range(KD):
                        halves(tmp, qhl[:, 0, m], qhl[:, 1, m], of("act", "free", L, "q", m), (L, "qlo", m))
                    if own:
                        for m in range(KD):
                            halves(tmp, khl[:, 0, m], khl[:, 1, m], of("act", "free", L, "k", m), (L, "klo", m))
                        dve.memset(VP[:, :, :, DH:QUARTER], 1.0).then_inc(*step(L, "ones"))
                    steps = attention_steps(own)
                    last = None
                    for i, s in enumerate(steps):
                        if s[0] == "S":
                            last = maxima(L, own, s)
                        elif s[0] == "MT":
                            minus_max_rows(L, s[1], last, GH * NT if own else 0)
                            minus_max_parts(L, s[1], GH * NT)
                        elif s[0] == "ST" and own and s[1] and s[2:] == (2, 0):
                            inverse_sums(L, s[1] - 1, QUARTER)
                        elif s[0] == "PVA" and (not own or s[1:] == (NG - 1, NT - 1)):
                            inverse_sums(L, s[1], QUARTER)
                        elif s[0] == "NB":
                            normalised(L, own, s[1])
                    for t in range(NT):
                        dve.wait_ge(*of("pe", L, "W", t))
                        dve.scalar_tensor_tensor(dst[:, t], slot(L, "W", t)[:, 0:D], 1.0 / WS, dst[:, t], ALU.mult, ALU.add).then_inc(*step(L, "x", t))
                        led.freed[(L, "W", t)] = ("dve", (L, "x", t))
                    dve.wait_ge(*of("dve", L, "x", NT - 1))

                if "B" in stages:
                    dve.wait_ge(*of("ld_kx", "mask"))
                    norm("B1", X, H)
                    dve.wait_ge(*of("dve", "B1", "xn", NT - 1))
                    norm("B", H, XN["B"])
                    x_affine("B")
                    attention("B0", True, H)

                if "M" in stages:
                    norm("M", H, XN["M"])
                    x_affine("M")
                    dve.wait_ge(*of("pe", "M", "gate"))
                    lg = sm[:, 0:64].rearrange("p (t e) -> p t e", e=NE)
                    dve.scalar_tensor_tensor(lg, slot("M", "gate")[:, 0:NT * NE].rearrange("p (t e) -> p t e", e=NE), 1.0 / WS,
                                             gateb[:].unsqueeze(1).broadcast_to([P, NT, NE]), ALU.mult, ALU.add).then_inc(*frees("dve", "M", "gate"))
                    dve.wait_ge(*of("dve", "free", "M", "gate"))
                    for t in range(NT):
                        dve.max(maxv[:, t], lg[:, t]).then_inc(*step("M", "top", t))
                    for t in range(NT):
                        dve.wait_ge(*of("dve", "M", "top", t))
                        dve.max_index(maxi[:, t], maxv[:, t], lg[:, t]).then_inc(*step("M", "idx", t))
                    dve.tensor_tensor(sm[:, 80:88], maxv[:, :, 1], maxv[:, :, 0], ALU.subtract).then_inc(*step("M", "d"))
                    dve.wait_ge(*of("act", "M", "e"))
                    dve.tensor_scalar(sm[:, 96:104], sm[:, 88:96], WS, WS, ALU.mult, ALU.add).then_inc(*step("M", "den"))
                    dve.wait_ge(*of("dve", "M", "den"))
                    dve.reciprocal(sm[:, 104:112], sm[:, 96:104]).then_inc(*step("M", "w1"))
                    dve.wait_ge(*of("dve", "M", "w1"))
                    dve.tensor_tensor(sm[:, 112:120], sm[:, 88:96], sm[:, 104:112], ALU.mult).then_inc(*step("M", "w2"))
                    dve.tensor_copy(sm[:, 64:80].rearrange("p (t i) -> p t i", i=2), maxi[:, :, 0:2]).then_inc(*step("M", "idxf"))
                    dve.wait_ge(*of("dve", "M", "idxf"))
                    io = iota[:].unsqueeze(1).broadcast_to([P, NT, NE])
                    ix = sm[:, 64:80].rearrange("p (t i) -> p t i", i=2)
                    for i, dst in enumerate((wfull[:], lg)):
                        dve.tensor_tensor(dst, io, ix[:, :, i:i + 1].broadcast_to([P, NT, NE]), ALU.is_equal).then_inc(*step("M", "eq", i))
                        dve.wait_ge(*of("dve", "M", "eq", i))
                        dve.tensor_tensor(dst, dst, sm[:, 104 + 8 * i:112 + 8 * i].unsqueeze(2).broadcast_to([P, NT, NE]), ALU.mult).then_inc(*step("M", "wm", i))
                        dve.wait_ge(*of("dve", "M", "wm", i))
                    dve.tensor_tensor(wfull[:], wfull[:], lg, ALU.add).then_inc(*step("M", "wfull"))
                    dve.wait_ge(*of("dve", "M", "wfull"))

                    def weights_lo(e, w):
                        dve.wait_ge(*of("act", "M", "whi", e, w))
                        dve.scalar_tensor_tensor(Wm[e % 2][:, w, 1], WSt[:, w], WS, Wm[e % 2][:, w, 0], ALU.mult, ALU.subtract).then_inc(*step("M", "wlo", e, w))

                    def expert_out(e, c):
                        for i in range(4):
                            dve.wait_ge(*of("pe", "M", "D", e, c, NM - 1))
                            t = 4 * c + i
                            if e:
                                dve.wait_ge(*of("dve", "M", "h", e - 1, t))
                            key = ("M", "h", e, t)
                            dve.scalar_tensor_tensor(H[:, t], slot("M", "D", e, c, i // 2)[:, (i % 2) * D:(i % 2 + 1) * D], wfull[:, t, e:e + 1],
                                                     H[:, t], ALU.mult, ALU.add).then_inc(*step(*key))
                            if i % 2:
                                led.freed[("M", "D", e, c, i // 2)] = ("dve", key)

                    weights_lo(0, 0)
                    weights_lo(0, 1)
                    n = 0
                    for e in range(NE):
                        for c in range(2):
                            for m in range(NM):
                                if n >= 4:
                                    dve.wait_ge(*of("pe", "M", "D", *back(e, c, m, 4)))
                                halves(midf[:, n % 3], mid[:, n % 4, 0], mid[:, n % 4, 1], of("act", "free", "M", "U", e, c, m), ("M", "midlo", e, c, m))
                                n += 1
                                if e + 1 < NE and (c, m) in ((0, 5), (1, 1)):
                                    weights_lo(e + 1, c)
                                if m == 3 and (e, c) != (0, 0):
                                    expert_out(*back(e, c, 0, 1)[:2])
                    expert_out(NE - 1, 1)
                    for t in range(NT):
                        dve.wait_ge(*of("dve", "M", "h", NE - 1, t))
                        dve.tensor_tensor(X[:, t], X[:, t], H[:, t], ALU.add).then_inc(*step("M", "x", t))
                    dve.wait_ge(*of("dve", "M", "x", NT - 1))

                if "C" in stages:
                    norm("C", X, XN["C"])
                    x_lo("C")
                    attention("C1", False, X)

                if "L1" in stages:
                    norm("L1", X, XN["L1"])
                    dve.wait_ge(*of("dve", "L1", "xn", NT - 1))
                    dve.tensor_reduce(sm[:, 0:8], XN["L1"], AX, ALU.max, apply_absolute_value=True).then_inc(*step("L1", "amax"))
                    dve.wait_ge(*of("dve", "L1", "amax"))
                    dve.tensor_scalar(sm[:, 0:8], sm[:, 0:8], EPS, None, ALU.max).then_inc(*step("L1", "xs"))
                    dve.wait_ge(*of("dve", "L1", "xs"))
                    dve.reciprocal(sm[:, 8:16], sm[:, 0:8]).then_inc(*step("L1", "xr"))
                    dve.wait_ge(*of("dve", "L1", "xr"))
                    dve.tensor_scalar(sm[:, 16:24], sm[:, 8:16], QB, None, ALU.mult).then_inc(*step("L1", "xm"))
                    dve.tensor_scalar(sm[:, 24:32], sm[:, 0:8], wsc[:, 2:3], None, ALU.mult).then_inc(*step("L1", "xsc"))
                    dve.wait_ge(*of("dve", "L1", "xsc"))
                    for t in range(NT):
                        dve.tensor_scalar(XN["L1"][:, t], XN["L1"][:, t], sm[:, 16 + t:17 + t], MAGIC, ALU.mult, ALU.add).then_inc(*step("L1", "xr1", t))
                    for t in range(NT):
                        dve.wait_ge(*of("dve", "L1", "xr1", t))
                        dve.tensor_scalar(XN["L1"][:, t], XN["L1"][:, t], -MAGIC, QB, ALU.add, ALU.min).then_inc(*step("L1", "xr2", t))
                    for t in range(NT):
                        dve.wait_ge(*of("dve", "L1", "xr2", t))
                        dve.tensor_scalar(xq[:, t], XN["L1"][:, t], -QB - 1.0, None, ALU.max).then_inc(*step("L1", "xq", t))
                    dve.wait_ge(*of("ld_b12", 1))

                    def hidden(t):
                        dve.wait_ge(*of("pe", "L1", "H1", t))
                        if t >= 3:
                            dve.wait_ge(*of("dve", "L1", "hr1", t - 3))
                        dve.scalar_tensor_tensor(hb[:, t % 3], slot("L1", "H1", t), sm[:, 24 + t:25 + t], b1b, ALU.mult, ALU.add).then_inc(*step("L1", "h", t))
                        led.freed[("L1", "H1", t)] = ("dve", ("L1", "h", t))

                    def quantise(t):
                        a, b_, c_ = 32 + t, 40 + t, 48 + t
                        dve.wait_ge(*of("act", "L1", "gelu", t))
                        dve.tensor_reduce(sm[:, a:a + 1], hb[:, t % 3], AX, ALU.max, apply_absolute_value=True).then_inc(*step("L1", "ha", t))
                        dve.wait_ge(*of("dve", "L1", "ha", t))
                        dve.tensor_scalar(sm[:, a:a + 1], sm[:, a:a + 1], EPS, None, ALU.max).then_inc(*step("L1", "hs", t))
                        dve.wait_ge(*of("dve", "L1", "hs", t))
                        dve.reciprocal(sm[:, b_:b_ + 1], sm[:, a:a + 1]).then_inc(*step("L1", "hrc", t))
                        dve.tensor_scalar(sm[:, c_:c_ + 1], sm[:, a:a + 1], wsc[:, 3:4], None, ALU.mult).then_inc(*step("L1", "hsc", t))
                        dve.wait_ge(*of("dve", "L1", "hrc", t))
                        dve.tensor_scalar(sm[:, 56 + t:57 + t], sm[:, b_:b_ + 1], QB, None, ALU.mult).then_inc(*step("L1", "hm", t))
                        dve.wait_ge(*of("dve", "L1", "hm", t))
                        if t >= 2:
                            dve.wait_ge(*of("dve", "L1", "hq", t - 2))
                            dve.wait_ge(*of("pe", "L1", "HQ", t - 2))
                        dve.tensor_scalar(hr[:, t % 2], hb[:, t % 3], sm[:, 56 + t:57 + t], MAGIC, ALU.mult, ALU.add).then_inc(*step("L1", "hr1", t))
                        dve.wait_ge(*of("dve", "L1", "hr1", t))
                        dve.tensor_scalar(hr[:, t % 2], hr[:, t % 2], MAGIC - QB - 1.0, MAGIC + QB, ALU.max, ALU.min).then_inc(*step("L1", "hr2", t))
                        dve.wait_ge(*of("dve", "L1", "hr2", t))
                        dve.tensor_scalar(hq[:, t % 2], hr[:, t % 2], -MAGIC, None, ALU.add).then_inc(*step("L1", "hq", t))

                    def ternary_out(t):
                        dve.wait_ge(*of("pe", "L1", "H2", t))
                        dve.scalar_tensor_tensor(X[:, t], slot("L1", "H2", t)[:, 0:D], sm[:, 48 + t:49 + t], X[:, t], ALU.mult, ALU.add).then_inc(*step("L1", "x1", t))
                        led.freed[("L1", "H2", t)] = ("dve", ("L1", "x1", t))
                        dve.wait_ge(*of("dve", "L1", "x1", t))
                        dve.tensor_tensor(X[:, t], X[:, t], b2b, ALU.add).then_inc(*step("L1", "x", t))

                    hidden(0)
                    for t in range(NT):
                        if t + 1 < NT:
                            hidden(t + 1)
                        quantise(t)
                        if t:
                            ternary_out(t - 1)
                    ternary_out(NT - 1)
                    dve.wait_ge(*of("dve", "L1", "x", NT - 1))

                if "D" in stages:
                    norm("D", X, XN["D"])
                    x_lo("D")
                    attention("D2", False, X)

                if "L2" in stages:
                    norm("L2", X, XN["L2"])
                    for t in range(NT):
                        dve.wait_ge(*of("pe", "L2", "Y", t))
                        dve.tensor_tensor(X[:, t], X[:, t], slot("L2", "Y", t)[:, 0:D], ALU.add).then_inc(*step("L2", "x", t))
                        led.freed[("L2", "Y", t)] = ("dve", ("L2", "x", t))
                    dve.wait_ge(*of("dve", "L2", "x", NT - 1))

                if "E" in stages:
                    norm("E", X, XN["E"])
                    x_lo("E")
                    attention("E3", False, X)

                if "F" in stages:
                    norm("F", X, XN["F"])
                    x_lo("F")

                    def small_step(key, ins):
                        ins.then_inc(*step("F", key))
                        dve.wait_ge(*of("dve", "F", key))

                    dve.wait_ge(*of("pe", "F", "R"))
                    small_step("lg", dve.scalar_tensor_tensor(rt[0:1, 0:NH], slot("F", "R")[0:1, 0:NH], 1.0 / T, F3br[:], ALU.mult, ALU.add))
                    led.freed[("F", "R")] = ("dve", ("F", "lg"))
                    small_step("l8", dve.max(rt[0:1, 16:24], rt[0:1, 0:NH]))
                    small_step("lmax", dve.tensor_scalar(rt[0:1, 24:25], rt[0:1, 16:17], -1.0, None, ALU.mult))
                    dve.wait_ge(*of("act", "F", "e1"))
                    small_step("r1", dve.reciprocal(rt[0:1, 26:27], rt[0:1, 25:26]))
                    small_step("dist", dve.tensor_scalar(rt[0:1, 64:80], rt[0:1, 0:NH], rt[0:1, 26:27], None, ALU.mult))
                    small_step("top", dve.max(rt[0:1, 28:36], rt[0:1, 64:80]))
                    small_step("neg", dve.tensor_scalar(rt[0:1, 36:37], rt[0:1, 28:29], -1.0, None, ALU.mult))
                    small_step("index", dve.max_index(rti[:], rt[0:1, 28:36], rt[0:1, 64:80]))
                    dve.wait_ge(*of("act", "F", "e3"))
                    small_step("den", dve.scalar_tensor_tensor(rt[0:1, 46:47], rt[0:1, 45:46], float(NH - HS), rt[0:1, 44:45], ALU.mult, ALU.add))
                    small_step("rden", dve.reciprocal(rt[0:1, 47:48], rt[0:1, 46:47]))
                    small_step("gates", dve.tensor_scalar(rt[0:1, 48:52], rt[0:1, 40:44], rt[0:1, 47:48], None, ALU.mult))
                    dve.wait_ge(*of("pe", "F", "G"))
                    small_step("gcol", dve.tensor_copy(gcol[:, 0:4], slot("F", "G")[:, 0:4]))
                    led.freed[("F", "G")] = ("dve", ("F", "gcol"))
                    for m in range(KD):
                        for i in range(2):
                            r = slice(DS * i, DS * (i + 1))
                            g_ = gcol[r, 2 * m + i:2 * m + i + 1]
                            small_step(("gq", m, i), dve.tensor_scalar(gcol[r, 4 + m:5 + m], g_, float(DS) ** -0.5 / WS, None, ALU.mult))
                            small_step(("gk", m, i), dve.tensor_scalar(gcol[r, 6 + m:7 + m], g_, 1.0 / WS, None, ALU.mult))
                    dve.wait_ge(*of("ld_sel", HS - 1, "bv"))
                    small_step("bs", dve.tensor_scalar(bsel[:], bsel[:], WS, None, ALU.mult))
                    small_step("qkscale", dve.tensor_tensor(bsel[:], bsel[:], gcol[:, 4:8], ALU.mult))
                    small_step("bv_hi", dve.tensor_scalar(bvh[:, 0], bvr[:], WS, None, ALU.mult))
                    small_step("bv_lo", dve.scalar_tensor_tensor(bvh[:, 1], bvr[:], WS, bvh[:, 0], ALU.mult, ALU.subtract))
                    small_step("wscaled", dve.tensor_scalar(Wst, Wst, WS, None, ALU.mult))
                    dve.wait_ge(*of("act", "F", "wsel_hi"))
                    dve.tensor_tensor(Wsel[:, :, 1], Wst, Wsel[:, :, 0], ALU.subtract).then_inc(*step("F", "wsel_lo"))
                    for n, hl in (("q", qhl), ("k", khl)):
                        for m in range(KD):
                            halves(tmp, hl[:, 0, m], hl[:, 1, m], of("act", "free", "F3", n, m), ("F3", n + "lo", m))
                    dve.memset(VP4[:, :, :, DS:TX], 1.0).then_inc(*step("F3", "ones"))
                    for s in last_attention_steps():
                        if s[0] == "S":
                            _, h, t = s
                            for c in range(2):
                                dve.wait_ge(*of("pe", "F3", "S", h, t, c))
                                dve.tensor_reduce(mpart[:, t, c:c + 1], slot("F3", "S", h, t, c), AX, ALU.max).then_inc(*frees("dve", "F3", "S", h, t, c))
                        elif s[0] == "MT":
                            h = s[1]
                            minus_max_rows("F3", h, ("F3", "S", h, NT - 1, 1), NT)
                            minus_max_parts("F3", h, NT)
                        elif s[0] == "ST" and s[1] and s[2] == 3:
                            inverse_sums("F3", s[1] - 1, NT)
                        elif s[0] == "NB":
                            h = s[1]
                            if h == HS - 1:
                                inverse_sums("F3", h, NT)
                            dve.wait_ge(*of("pe", "F3", "NB", h))
                            dve.scalar_tensor_tensor(tmp[0:TX], OT4[h % 2], gcol[0:TX, h:h + 1], slot("F3", "NB", h)[0:TX], ALU.mult,
                                                     ALU.mult).then_inc(*step("F3", "onf", h))
                            led.freed[("F3", "NB", h)] = ("dve", ("F3", "onf", h))
                            halves(tmp[0:TX], ON4[:, 0, h], ON4[:, 1, h], of("dve", "F3", "onf", h), ("F3", "onlo", h))
                            dve.wait_ge(*of("dve", "F3", "onlo", h))
                    dve.memset(mpart[:], -3.0e38).then_inc(*step("F3", "mpart"))
                    for t in range(NT):
                        dve.wait_ge(*of("pe", "F3", "W", t))
                        dve.scalar_tensor_tensor(X[:, t], slot("F3", "W", t)[:, 0:D], 1.0 / WS, X[:, t], ALU.mult, ALU.add).then_inc(*step("F3", "x", t))
                        led.freed[("F3", "W", t)] = ("dve", ("F3", "x", t))
                    dve.wait_ge(*of("dve", "F3", "x", NT - 1))
                dve.memset(rt[0:1, 95:96], 0.0).then_inc(*step("final"))
                batch_end(dve, "dve")
        return led


def halves_of(w):
    return w.reshape(KD, P, -1).transpose(1, 0, 2).reshape(P, -1)


def by_heads(w, heads, width, tall, groups):
    out = np.zeros((heads, tall, w.shape[1]), np.float32)
    out[:, :width] = w.reshape(heads, width, -1)
    return out.reshape(groups, -1, w.shape[1])


def layouts(i):
    f = {k: np.asarray(v) for k, v in i.items()}
    z = np.zeros
    pad_k = z((D, D), np.float32)
    pad_k[:, :P] = f["L0_xattn_Wk"].T
    mats = {"A0q": f["L0_xattn_Wq"].T, "A0o": f["L0_xattn_Wo"].T, "A0k": pad_k, "A0v": f["L0_xattn_Wv"].T,
            "B0q": f["L0_ffn_Wq"], "B0k": f["L0_ffn_Wk"], "B0v": f["L0_ffn_Wv"],
            "C1q": f["L1_xattn_Wq"].T, "C1k": f["L1_xattn_Wk"].T, "C1v": f["L1_xattn_Wv"].T,
            "D2q": f["L2_xattn_Wq"].T, "D2k": f["L2_xattn_Wk"].T, "D2v": f["L2_xattn_Wv"].T,
            "E3q": f["L3_xattn_q_w"].T, "E3k": f["L3_xattn_k_w"].T, "E3v": f["L3_xattn_v_w"].T}
    padded = {"B0p": f["L0_ffn_Wp"], "C1o": f["L1_xattn_Wo"].T, "D2o": f["L2_xattn_Wo"].T, "E3id": np.eye(D, dtype=np.float32)}
    pads = [by_heads(padded[n], NH, DH, QUARTER, NG) for n in PADDED[:-1]]
    pads.append(by_heads(f["L3_ffn_Wo"], HS, DS, P, HS))
    rows = {"B0v": f["L0_ffn_bv"], "B0p": f["L0_ffn_bp"], "C1o": f["L1_xattn_bo"], "D2v": f["L2_xattn_bv"], "D2o": f["L2_xattn_bo"],
            "E3v": f["L3_xattn_v_b"], "F3o": f["L3_ffn_bo"], "L2con": f["L2_ffn_b_con"], "L2down": f["L2_ffn_down_bias"]}
    rows.update({f"e{e}": f["L0_ffn_exp_b2"][e] for e in range(NE)})
    cols = {"B0q": f["L0_ffn_bq"], "B0k": f["L0_ffn_bk"], "D2q": f["L2_xattn_bq"], "D2k": f["L2_xattn_bk"], "E3q": f["L3_xattn_q_b"],
            "E3k": f["L3_xattn_k_b"], "ln1_g": f["L0_ffn_ln1_g"], "ln1_b": f["L0_ffn_ln1_b"], "ln2_g": f["L0_ffn_ln2_g"], "ln2_b": f["L0_ffn_ln2_b"]}
    w_exp = z((3, P, HID), np.float32)
    w_exp[:KD] = f["L2_ffn_W_exp"].reshape(KD, P, HID)
    w_exp[KD, 0] = f["L2_ffn_b_exp"]
    eye = np.eye(P, dtype=np.float32)
    k_, q_ = np.arange(P)[:, None], np.arange(P)[None, :]
    causal = np.stack([np.where(q_ > k_, -BIG, 0.0), np.where(k_ > q_, -BIG, 0.0)], 1).astype(np.float16)
    e4 = z((P, P), np.float32)
    for j in range(GH):
        e4[QUARTER * j + DH, QUARTER * j:QUARTER * (j + 1)] = 1.0
    e64 = z((TX, TX), np.float32)
    e64[DS] = 1.0
    kx = z((MROW + 2, len(XL), NH, TX), np.float16)
    kx[48, :, :, TC:] = -BIG
    kx[MROW:] = 1.0
    qs = z((MROW - 48, 2, GH, T), np.float16)
    qs[0] = BIG
    ks = z((MROW + 2 - 48, 2, GH, T), np.float16)
    ks[MROW - 48:] = 1.0
    eps = z((P, 2), np.float32)
    eps[:, 0] = EPS
    a = {
        "x": f["x"], "ctxT": f["ctx_1024"].transpose(0, 2, 1), "mask": f["mask_BxS2_ik0"],
        "wflat": np.concatenate([halves_of(mats[n]) for n in FLAT + CTXW], 1),
        "wpad": np.concatenate([p.transpose(1, 0, 2).reshape(P, -1) for p in pads], 1),
        "bcol": np.concatenate([cols[n].reshape(KD, P).T for n in BCOL] + [f["L2_ffn_up_bias"].reshape(NM, P).T,
                               f["L0_ffn_exp_b1"].reshape(NE * NM, P).T], 1),
        "brow": np.stack([rows[n] for n in BROW]),
        "gate_W": halves_of(f["L0_ffn_gate_W"]), "gate_b": f["L0_ffn_gate_b"].reshape(1, NE),
        "lam": np.concatenate([f["L0_xattn_lambda_" + n] for n in ("q1", "k1", "q2", "k2")]).reshape(1, -1),
        "exp_W1": f["L0_ffn_exp_W1"].reshape(NE, KD, P, HID).transpose(0, 2, 1, 3).reshape(NE, P, -1),
        "exp_W2": f["L0_ffn_exp_W2"].reshape(NE, NM, P, D).transpose(0, 2, 1, 3).reshape(NE, P, -1),
        "L1_W1": halves_of(f["L1_ffn_W1"].T), "L1_W2": f["L1_ffn_W2"].T.reshape(NM, P, D).transpose(1, 0, 2).reshape(P, -1),
        "L1_b1": f["L1_ffn_b1"].reshape(1, -1), "L1_b2": f["L1_ffn_b2"].reshape(1, -1),
        "W_exp": w_exp.transpose(1, 0, 2), "W_con": f["L2_ffn_W_con"].T.reshape(KD, P, HID).transpose(1, 0, 2),
        "up_w": f["L2_ffn_up_weights"].reshape(10, -1), "down_w": f["L2_ffn_down_weights"].reshape(10, -1),
        "F3_Wq": f["L3_ffn_Wq"].reshape(KD, P, HID).transpose(1, 0, 2), "F3_Wk": f["L3_ffn_Wk"].reshape(KD, P, HID).transpose(1, 0, 2),
        "F3_Wv": f["L3_ffn_Wv"].reshape(KD, P, HID).transpose(1, 0, 2),
        "F3_bq": f["L3_ffn_bq"].reshape(-1, 1), "F3_bk": f["L3_ffn_bk"].reshape(-1, 1), "F3_bv": f["L3_ffn_bv"].reshape(1, -1),
        "F3_Wr": f["L3_ffn_Wr"].reshape(KD, P, NH).transpose(1, 0, 2), "F3_br": f["L3_ffn_br"].reshape(1, -1),
        "c_ident": eye, "c_ident16": eye.astype(np.float16), "c_causal": causal, "c_E4": e4, "c_E64": e64,
        "c_iota": np.tile(np.arange(NE, dtype=np.float32), (P, 1)), "c_eps": eps, "c_kx": kx, "c_qs": qs, "c_ks": ks,
    }
    return {k: np.ascontiguousarray(v) for k, v in a.items()}


STAGES = ("A", "B", "M", "C", "L1", "D", "L2", "E", "F")


def program(nc, arrays, known, stages):
    args = {k: nc.dram_tensor(f"in_{k}", v.shape, mybir.dt.from_np(v.dtype), kind="ExternalInput").ap() for k, v in arrays.items()}
    out = nc.dram_tensor("out_0", (NB, T, D), F32, kind="ExternalOutput").ap()
    return build(nc, args, out, known, stages)


def kernel(**inputs):
    import concourse.bacc as _bacc
    from concourse.bass_utils import run_bass_kernel_spmd as _run

    arrays = layouts(inputs)
    counted = program(_bacc.Bacc("TRN2", target_bir_lowering=False, num_devices=1), arrays, None, STAGES)
    nc = _bacc.Bacc("TRN2", target_bir_lowering=False, num_devices=1)
    program(nc, arrays, counted, STAGES)
    r = _run(nc, [{f"in_{k}": v for k, v in arrays.items()}], core_ids=[0])
    return r.results[0]["out_0"]
```

```python
from contextlib import ExitStack

import concourse.bass as bass
from concourse import mybir
import numpy as np

P = 128
NB, T, D, TC = 4, 1024, 256, 77
NT = T // P
KD = D // P
CH = 512
HID = 4 * D
NM = HID // P
NE = 8
NH, DH = 16, 16
NG, GH = 4, 4
TX = 96
HS, DS = 4, 64
QUARTER = 32
EPS = 1e-5
LAM0 = 0.8 - 0.6 * float(np.exp(-0.3 * 12))
WS = 64.0
BIG = 60000.0
MAGIC = 1.5 * 2.0 ** 23
QB = 127.0
MROW = 96
NP, NPX = 5, 7

F32, F16, I32, U32 = mybir.dt.float32, mybir.dt.float16, mybir.dt.int32, mybir.dt.uint32
ALU, ACT, AX = mybir.AluOpType, mybir.ActivationFunctionType, mybir.AxisListType.X

FLAT = ["A0q", "A0o", "B0q", "B0k", "B0v", "C1q", "D2q", "E3q"]
PADDED = ["B0p", "C1o", "D2o", "E3id", "F3o"]
CTXW = ["A0k", "A0v", "C1k", "C1v", "D2k", "D2v", "E3k", "E3v"]
BROW = ["B0v", "B0p", "C1o", "D2v", "D2o", "E3v", "F3o", "L2con", "L2down"] + [f"e{e}" for e in range(NE)]
BCOL = ["B0q", "B0k", "D2q", "D2k", "E3q", "E3k", "ln1_g", "ln1_b", "ln2_g", "ln2_b"]
BC_UP = 2 * len(BCOL)
BC_E1 = BC_UP + NM
NBC = BC_E1 + NE * NM
LOW, HIGH = 7, 3
XL = ["C1", "D2", "E3"]
FLAT_N, PAD_N = KD * D, GH * D


N_LOADS = 19


class Ledger:

    def __init__(self, known):
        self.count, self.value, self.slot, self.freed = {}, {}, {}, {}
        self.known = known

    def mark(self, name, key, inc):
        self.count[name] = self.count.get(name, 0) + inc
        if (name, key) in self.value:
            raise KeyError(f"twice: {name} {key}")
        self.value[name, key] = self.count[name]
        return inc

    def at(self, name, key):
        return self.known.value[name, key] if self.known else 1


def own_attention_steps():
    order = [(t, j) for pair in ((0, 7), (1, 6), (2, 5), (3, 4)) for j in range(GH) for t in pair]
    spread = [4, 6, 6, 6, 5, 5, 0, 0]
    steps = [("S", 0, t, j) for t in range(NT) for j in range(GH)] + [("MT", 0)]
    for g in range(NG):
        ahead = [("S", g + 1) + o for o in order] if g + 1 < NG else []
        for kt in range(NT):
            mine = [("ST", g, kt, 0)] + ([("PV", g, kt - 1, c) for c in range(2) if kt <= 4 * (c + 1)] if kt else [])
            mine += [("ST", g, kt, j) for j in range(1, GH)]
            for i, step in enumerate(mine):
                late = 2 if kt == 0 else 0
                n = spread[kt] * max(i + 1 - late, 0) // (len(mine) - late) - spread[kt] * max(i - late, 0) // (len(mine) - late)
                steps += [step] + ahead[:n]
                del ahead[:n]
            if g + 1 < NG and kt == 5:
                steps += [("MT", g + 1)]
            if g and kt == 3:
                steps += [("NB", g - 1)]
        steps += [("PV", g, NT - 1, 1)]
    return steps + output_steps()


def output_steps():
    return [("WS", 0), ("WS", 1), ("WB", 0), ("WB", 1), ("WS", 2), ("WB", 2), ("NB", NG - 1), ("WL",)]


def context_attention_steps():
    def S(g, a, b):
        return [("S", g, t) for t in range(a, b)]

    def ST(g, a, b):
        return [("ST", g, 0, j) for j in range(a, b)]

    steps = S(0, 0, NT) + S(1, 0, NT) + [("MT", 0)] + S(2, 0, NT)
    steps += ST(0, 0, 2) + S(3, 0, NT // 2) + ST(0, 2, GH) + S(3, NT // 2, NT) + [("MT", 1)]
    for g in range(NG):
        if g + 1 < NG:
            steps += ST(g + 1, 0, 3)
        steps += [("PV", g, 0, 0), ("PV", g, 0, 1)]
        if g + 1 < NG:
            steps += ST(g + 1, 3, GH)
        if g:
            steps += [("NB", g - 1)]
    return steps + output_steps()


def attention_steps(own):
    return own_attention_steps() if own else context_attention_steps()


def last_attention_steps():
    steps = [("S", 0, t, c) for t in range(NT) for c in range(2)] + [("MT", 0)]
    for h in range(HS):
        ahead = [("S", h + 1, t, c) for t in range(NT) for c in range(2)] if h + 1 < HS else []
        for kt in range(NT):
            steps += [("ST", h, kt)] + ahead[:1]
            if kt:
                steps += [("PV", h, kt - 1, 0)] + ahead[1:2] + [("PV", h, kt - 1, 1)] + ahead[2:3]
            else:
                steps += ahead[1:3]
            del ahead[:3]
            if h + 1 < HS and kt == 5:
                steps += [("MT", h + 1)]
            if h and kt == 4:
                steps += [("NB", h - 1)]
        steps += [("PV", h, NT - 1, 0), ("PV", h, NT - 1, 1)]
    return steps + output_steps()


def build(nc, A, out, known, stages):
    led = Ledger(known)
    with ExitStack() as ctx:
        def sb(name, shape, dt):
            return ctx.enter_context(nc.sbuf_tensor(name, shape, dt))

        def dram(name, shape, dt):
            return nc.dram_tensor(name, shape, dt, kind="Internal").ap()

        Wf = sb("weights_flat", [P, len(FLAT), 2, KD, D], F16)
        Wp = sb("weights_padded", [P, len(PADDED), 2, GH, D], F16)
        Wq1 = sb("ternary_W1", [P, KD, HID], F16)
        Wq2 = sb("ternary_W2", [P, NM, D], F16)
        Wexp = sb("butterflied_W_exp", [P, KD, HID], F32)
        RT = sb("butterflied_W_con_turned", [P, NM, D], F32)
        X = sb("x_tokens", [P, NT, D], F32)
        H = sb("h_tokens", [P, NT, D], F32)
        XT = sb("x_channels_hi_lo", [P, 2, KD, T], F16)
        QS = sb("q_stack", [P, 2, GH, T], F16)
        KS = sb("k_stack", [P, 2, GH, T], F16)
        KX = sb("k_stack_context", [MROW + 2, len(XL), NH, TX], F16)
        VX = sb("v_context", [P, len(XL), NH, QUARTER], F32)
        KP0 = sb("k_context_0", [P, 2, TX], F16)
        VP0 = sb("v_context_0", [P, 2, D], F16)
        CTf = sb("context_f32", [P, KD, TC], F32)
        CT = sb("context_hi_lo", [P, 2, KD, TX], F16)
        identf = sb("identf", [P, P], F32)
        ident = sb("ident", [P, P], F16)
        big = sb("big_ident", [P, P], F16)
        small = sb("small_ident", [P, P], F16)
        causal = sb("causal", [P, 2, P], F16)
        E4 = sb("spread_sums", [P, P], F32)
        E64 = sb("spread_sums_last", [TX, TX], F32)
        onesf = sb("ones_f32", [P, P], F32)
        BR = sb("bias_rows", [P, 2, D], F16)
        BC = sb("bias_columns", [P, NBC], F32)
        upb = sb("up_bias_whole", [P, NM], F32)
        gateW = sb("gate_W", [P, 2, KD, NE], F16)
        gateb = sb("gate_b", [P, NE], F32)
        iota = sb("iota", [P, NE], F32)
        lamt = sb("lambda_work", [P, 8], F32)
        epsc = sb("eps_and_zero", [P, 2], F32)
        F3Wr = sb("router_W", [P, KD, NH], F32)
        F3br = sb("router_b", [1, NH], F32)
        wsc = sb("ternary_scales", [P, 8], F32)
        stats = sb("ln_stats", [P, NT, 6], F32)
        mv = sb("ln_mean_var", [P, NT, 2], F32)
        rstd = sb("ln_rstd", [P, NT], F32)
        sd = sb("ln_std", [P, NT], F32)
        mpart = sb("max_parts", [P, GH * NT, 2], F32)
        negm = sb("minus_max", [P, 2, GH * NT], F32)
        mrow = sb("minus_max_rows", [2 * GH * NT, 2, 2, P], F16)
        rsum = sb("sums_by_token", [P, NG, QUARTER], F32)
        rinv = sb("inverse_sums_by_token", [P, NG, QUARTER], F32)
        sm = sb("small_work", [P, 160], F32)
        maxv = sb("top_values", [P, NT, NE], F32)
        maxi = sb("top_indices", [P, NT, NE], U32)
        wfull = sb("expert_weights", [P, NT, NE], F32)
        maskr = sb("mask_row", [1, TX], I32)
        rt = sb("router_row", [1, 96], F32)
        rti = sb("router_index", [1, NE], U32)
        xmean = sb("mean_x", [P, KD], F32)
        gcol = sb("gates_by_row", [P, 8], F32)
        arena = sb("arena", [P, 16 * 1024], F32)

        def area(kb, n, dt=F32, rows=P):
            v = arena[0:rows, int(kb * 256):int(kb * 256) + (n if dt == F32 else n // 2)]
            return v if dt == F32 else v.bitcast(dt)

        stage_flat = area(0, len(FLAT + CTXW) * FLAT_N)
        stage_pad = area(32, len(PADDED) * PAD_N)
        ctx_split = area(52, FLAT_N * 8, F16)
        lamr = area(60, 6 * P)
        gwf = area(63, KD * NE)
        spare = KX[:, :, :, :].rearrange("p l h c -> p (l h c)").bitcast(F32)
        low_w = spare[:, 0:2 * HID]
        brf = spare[:, 2 * HID:2 * HID + D]
        KVW = area(0, len(CTXW) * 2 * FLAT_N, F16).rearrange("p (w s k d) -> p w s k d", s=2, k=KD, d=D)
        kxs = area(40, 2 * 3 * KD * TX, F16).rearrange("p (s l k c) -> p s l k c", s=2, l=3, k=KD)
        kxf = area(44, 3 * KD * TX).rearrange("p (l k c) -> p l k c", l=3, k=KD)
        maskb = area(57, NH * TX, F16, rows=1).rearrange("p (h c) -> p h c", h=NH)
        tmp = area(60, T)
        XN = {k: area(o, NT * D).rearrange("p (t d) -> p t d", d=D) for k, o in
              {"A": 48, "B": 16, "M": 48, "C": 16, "D": 16, "E": 16, "L1": 16, "L2": 16, "F": 28}.items()}
        VP = area(0, NT * NH * QUARTER).rearrange("p (t h d) -> p t h d", h=NH, d=QUARTER)
        PR = area(16, NP * T).rearrange("p (n c) -> p n c", c=T)
        PRX = area(8, NPX * T).rearrange("p (n c) -> p n c", c=T)
        OT = {True: [area(36 + 4 * (g % 2), T) for g in range(NG)],
              False: [area(36, T), area(40, T), area(0, T), area(4, T)]}
        ON = area(44, 2 * NG * T, F16).rearrange("p (s g c) -> p s g c", s=2, g=NG)
        qhl = area(44, 2 * KD * T, F16).rearrange("p (s k c) -> p s k c", s=2, k=KD)
        khl = area(52, 2 * KD * T, F16).rearrange("p (s k c) -> p s k c", s=2, k=KD)
        q0 = area(0, 2 * 2 * T, F16).rearrange("p (s h c) -> p s h c", s=2, h=2)
        E0 = area(8, 2 * 2 * TC).rearrange("p (n h c) -> p n h c", n=2, h=2)
        A0 = area(12, NT * TC).rearrange("p (t c) -> p t c", c=TC)
        AT0 = area(32, 2 * T, F16).rearrange("p (s c) -> p s c", s=2)
        AO0 = area(20, 2 * KD * T, F16).rearrange("p (s k c) -> p s k c", s=2, k=KD)
        sq0 = area(36, 2 * D).rearrange("p (n d) -> p n d", n=2)
        WSt = area(0, 2 * KD * HID).rearrange("p (w n) -> p w n", w=2)
        Wm = [area(16 + 16 * i, 2 * 2 * KD * HID, F16).rearrange("p (w s n) -> p w s n", w=2, s=2) for i in range(2)]
        midf = area(48, 3 * CH).rearrange("p (n c) -> p n c", n=3)
        mid = area(54, 4 * 2 * CH, F16).rearrange("p (n s c) -> p n s c", n=4, s=2)
        b1b = area(0, HID)
        hb = area(4, 3 * HID).rearrange("p (n c) -> p n c", n=3)
        xq = area(24, NT * D, F16).rearrange("p (t d) -> p t d", d=D)
        xqT = area(28, KD * T, F16).rearrange("p (k c) -> p k c", k=KD)
        hq = area(32, 2 * HID, F16).rearrange("p (n c) -> p n c", n=2)
        hqT = area(36, 2 * HID, F16).rearrange("p (n c) -> p n c", n=2)
        b2b = area(40, D)
        hr = area(44, 2 * HID).rearrange("p (n c) -> p n c", n=2)
        XTf = area(0, KD * T).rearrange("p (k c) -> p k c", k=KD)
        gT = area(24, 2 * NM * CH).rearrange("p (n m c) -> p n m c", n=2, m=NM)
        VP4 = area(0, NT * HS * TX).rearrange("p (t h d) -> p t h d", h=HS, d=TX)
        Wst = area(12, 3 * KD * D).rearrange("p (w k d) -> p w k d", w=3, k=KD)
        Wsel = area(18, 3 * 2 * KD * D, F16).rearrange("p (w s k d) -> p w s k d", w=3, s=2, k=KD)
        PR4 = area(16, NP * T).rearrange("p (n c) -> p n c", c=T)
        OT4 = [area(36, T, rows=TX), area(40, T, rows=TX)]
        ON4 = area(44, 2 * HS * T, F16, rows=TX).rearrange("p (s g c) -> p s g c", s=2, g=HS)
        bsel = sb("selected_biases", [P, 4], F32)
        bvr = area(24, D, rows=1)
        bvh = area(25, 2 * D, F16, rows=1).rearrange("p (s d) -> p s d", s=2)

        low_up = RT[:, :, :].rearrange("p m d -> p (m d)")[:, 0:HID].unsqueeze(1)
        low_up_t = RT[:, :, :].rearrange("p m d -> p (m d)")[:, HID:2 * HID].rearrange("p (n k c) -> p n k c", n=2, k=1)
        low_down = Wexp[:, 0:1, :]
        low_down_t = Wexp[:, 1, :].rearrange("p (n k c) -> p n k c", n=2, k=1)
        ring_up = QS[:, :, :, :].rearrange("p b h c -> p (b h c)").bitcast(F32).rearrange("p (n c) -> p n c", n=2)
        ring_down = KS[:, :, :, :].rearrange("p b h c -> p (b h c)").bitcast(F32).rearrange("p (n c) -> p n c", n=2)
        rows_e = area(33, NM * (D + 1)).rearrange("p (m d) -> p m d", d=D + 1)
        rows_c = XT[:, :, :, :].rearrange("p s k c -> p (s k c)").bitcast(F32).rearrange("p (m d) -> p m d", d=D)
        high_t = area(42, NM * (D + 1)).rearrange("p (n q d) -> p n q d", n=2, q=NM // 2)
        high_w = sm[:, 0:2 * HIGH * 2 * NM].rearrange("p (e s q rc) -> p e s q rc", e=2, s=HIGH, rc=4)
        fW1 = X[:, :, :].rearrange("p t d -> p (t d)")
        fW2 = H[:, :, :].rearrange("p t d -> p (t d)")

        PS = ctx.enter_context(nc.psum_tensor("ps", [P, 8, CH], F32))
        flat = PS[:, :, :].rearrange("p b c -> p (b c)")
        SLOT = {"A0": flat[:, 0:1024], "A1": flat[:, 1024:2048], "B0": flat[:, 2048:2560], "B1": flat[:, 2560:3072],
                "S0": flat[:, 3072:3584], "S1": flat[:, 3584:4096]}

        d_ctxw = dram("scr_ctx_weights", [P, len(CTXW), 2 * FLAT_N], F16)
        d_kx = dram("scr_k_context", [2, len(XL), KD * P, TX], F16)
        d_q = dram("scr_q", [2, KD * P, T], F16)
        d_k = dram("scr_k", [2, KD * P, T], F16)

        negp = [negm[:, :, :].rearrange("p b n -> p (b n)"), mpart[:, :, :].rearrange("p n c -> p (n c)")]

        names = ["pe", "act", "dve", "pool", "ld_next", "ld_kvw", "ld_const", "st_kx", "ld_kx", "st_q0", "st_q1", "st_k0", "st_k1",
                 "ld_stack0", "ld_stack1", "ld_m0", "ld_m1", "ld_wexp0", "ld_wexp1", "ld_b12",
                 "ld_sel", "st_out"] + [f"{n}{g}" for n in ("ld_s", "ld_r") for g in range(NG)]
        sems = {n: ctx.enter_context(nc.semaphore("s_" + n)) for n in names}
        first_num = min(s.num for s in sems.values())
        assert max(s.num for s in sems.values()) - first_num == len(sems) - 1
        once = {n: ctx.enter_context(nc.semaphore("u_" + n)) for n in (
            "load", "lambda", "ternary", "first", "kvw", "pe", "act", "dve", "pool", "ctxw", "staged", "low_w", "rows_e", "spread_up", "spread_down", "ring_up", "ring_down",
            "up", "down", "high", "wsum", "store0", "store1", "store2", "store3")}
        arrived = ctx.enter_context(nc.semaphore("arrived"))
        go = {n: ctx.enter_context(nc.semaphore("go_" + n)) for n in ("pe", "act", "dve", "pool")}

        def did(name, *key):
            inc = 16 if name[:3] in ("ld_", "st_") else 1
            return sems[name], led.mark(name, key, inc)

        def of(name, *key):
            return sems[name], led.at(name, key)

        def slot(*key):
            return SLOT[led.slot[key]]

        def frees(name, *key):
            led.freed[key] = (name, ("free",) + key)
            return did(name, "free", *key)

        def back(e, c, m, n):
            i = (e * 2 + c) * NM + m - n
            return i // (2 * NM), i // NM % 2, i % NM

        def butterfly(eng, sem, y, t, w, s, i, turned):
            st, k = 2 ** s, y.shape[1]
            pair = y.rearrange("p k (n two s) -> p k n two s", two=2, s=st)
            wv = w.rearrange("p (n s rc) -> p n s rc", s=st, rc=4)
            a = [pair[:, kk, :, 0, :] for kk in range(k)]
            b_ = [pair[:, kk, :, 1, :] for kk in range(k)]
            t0 = [t[:, 0, kk].rearrange("p (n s) -> p n s", s=st) for kk in range(k)]
            t1 = [t[:, 1, kk].rearrange("p (n s) -> p n s", s=st) for kk in range(k)]
            c_ba, c_ab = (1, 2) if turned else (2, 1)
            n = 6 * i * k
            if n:
                eng.wait_ge(sem, n)
            for kk in range(k):
                eng.tensor_tensor(t0[kk], a[kk], wv[:, :, :, 0], ALU.mult).then_inc(sem, 1)
                eng.tensor_tensor(t1[kk], a[kk], wv[:, :, :, c_ba], ALU.mult).then_inc(sem, 1)
            eng.wait_ge(sem, n + 2 * k)
            for kk in range(k):
                eng.tensor_tensor(a[kk], b_[kk], wv[:, :, :, c_ab], ALU.mult).then_inc(sem, 1)
                eng.tensor_tensor(b_[kk], b_[kk], wv[:, :, :, 3], ALU.mult).then_inc(sem, 1)
            eng.wait_ge(sem, n + 4 * k)
            for kk in range(k):
                eng.tensor_tensor(a[kk], a[kk], t0[kk], ALU.add).then_inc(sem, 1)
                eng.tensor_tensor(b_[kk], b_[kk], t1[kk], ALU.add).then_inc(sem, 1)

        wi = {n: i for i, n in enumerate(FLAT)}
        pi = {n: i for i, n in enumerate(PADDED)}
        ci = {n: i for i, n in enumerate(CTXW)}
        bi = {n: i for i, n in enumerate(BROW)}
        bc = {n: 2 * i for i, n in enumerate(BCOL)}
        runs = [("B", "B0", True), ("C", "C1", False), ("D", "D2", False), ("E", "E3", False)]
        block = ctx.enter_context(nc.Block())

        def batch_end(eng, name):
            eng.drain().then_inc(arrived, 1)
            eng.wait_ge(go[name], 1)
            eng.sem_clear(go[name])

        @block.sync
        def _(sp):
            sp.dma_start(identf[:], A["c_ident"]).then_inc(once["low_w"], 16)
            sp.dma_start(low_w, A["low_w"]).then_inc(once["low_w"], 16)
            for dst, src in [(stage_flat, A["wflat"]), (stage_pad, A["wpad"]), (ident[:], A["c_ident16"]),
                             (causal[:], A["c_causal"]), (E4[:], A["c_E4"]), (E64[:], A["c_E64"]), (iota[:], A["c_iota"]),
                             (BC[:, 0:NBC], A["bcol"]), (gateb[:], A["gate_b"].partition_broadcast(P)),
                             (epsc[:], A["c_eps"]), (high_w, A["high_w"]), (rows_c, A["W_con"]), (brf[0:len(BROW), :], A["brow"]),
                             (gwf[:], A["gate_W"]), (lamr[:, 0:4 * P], A["lam"].partition_broadcast(P)),
                             (F3Wr[:], A["F3_Wr"]), (F3br[:], A["F3_br"]),
                             (fW1, A["L1_W1"]), (fW2, A["L1_W2"])]:
                sp.dma_start(dst, src).then_inc(once["load"], 16)
            for w in range(len(CTXW)):
                sp.wait_ge(once["ctxw"], w + 1)
                sp.dma_start(d_ctxw[:, w, :], ctx_split[:, (w % 4) * 2 * FLAT_N:(w % 4 + 1) * 2 * FLAT_N]).then_inc(once[f"store{w % 4}"], 16)
            sp.wait_ge(once["staged"], 1)
            for i in range(4):
                sp.wait_ge(once[f"store{i}"], 16 * len(CTXW) // 4)
            sp.dma_start(rows_e, A["W_exp"]).then_inc(once["rows_e"], 16)
            sp.dma_start(KVW.rearrange("p w s k d -> p w (s k d)"), d_ctxw).then_inc(once["kvw"], 16)
            sp.wait_ge(once["spread_down"], LOW)
            sp.wait_ge(once["spread_up"], LOW)
            sp.dma_start(KX[:MROW + 2], A["c_kx"]).then_inc(once["kvw"], 16)

            def load_inputs(x, ctx_, mask, sem):
                sp.dma_start(H[:], x.rearrange("o (t p) d -> p (o t) d", p=P)).then_inc(sem, 16)
                sp.dma_start(CTf[:], ctx_.rearrange("o (k p) c -> p (o k) c", p=P)).then_inc(sem, 16)
                sp.dma_start(maskr[:, 0:TC], mask).then_inc(sem, 16)

            sp.wait_ge(once["ternary"], 1)
            load_inputs(A["x"][0:1], A["ctxT"][0:1], A["mask"][0:1], once["first"])
            sp.wait_ge(once["first"], 48)
            sp.wait_ge(arrived, 4)
            sp.wait_ge(once["kvw"], 32)
            sp.sem_clear(arrived)
            for n in go:
                sp.sem_inc(go[n], 1)

            with sp.Fori(0, NB) as b:
                bs = bass.ds(b, 1)
                sp.dma_start(QS[48:MROW, :, :, :], A["c_qs"]).then_inc(*did("ld_const", 1))
                sp.dma_start(KS[48:MROW + 2, :, :, :], A["c_ks"]).then_inc(*did("ld_const", 2))
                sp.wait_ge(*of("dve", "kxs"))
                for s in range(2):
                    for l in range(len(XL)):
                        sp.dma_start(d_kx[s, l, :, 0:TC].rearrange("(k p) c -> p k c", p=P), kxs[:, s, l, :, 0:TC]).then_inc(*did("st_kx", s, l))
                sp.wait_ge(*of("st_kx", 1, 2))
                for n, s in enumerate((0, 1, 0)):
                    for l in range(len(XL)):
                        sp.dma_start(KX[16 * n:16 * n + 16, l, :, 0:TC],
                                     d_kx[s, l, :, 0:TC].rearrange("(h i) c -> i h c", i=DH)).then_inc(*did("ld_kx", n, l))
                sp.wait_ge(*of("dve", "mask"))
                sp.dma_start(KX[48:49, 2, :, 0:TC], maskb[:, :, 0:TC]).then_inc(*did("ld_kx", "mask"))

                def stacks(L, own, g):
                    buf = g % 2
                    if g >= 2:
                        sp.wait_ge(*of("pe", L, "ST", g - 2, NT - 1 if own else 0, GH - 1))
                    for n, s in enumerate((0, 0, 1)):
                        sp.dma_start(QS[16 * n:16 * n + 16, buf],
                                     d_q[s, g * GH * DH:(g + 1) * GH * DH].rearrange("(h i) c -> i h c", i=DH)).then_inc(*did(f"ld_stack{buf}", L, g, "q", n))
                    if own:
                        for n, s in enumerate((0, 1, 0)):
                            sp.dma_start(KS[16 * n:16 * n + 16, buf],
                                         d_k[s, g * GH * DH:(g + 1) * GH * DH].rearrange("(h i) c -> i h c", i=DH)).then_inc(*did(f"ld_stack{buf}", L, g, "k", n))

                def max_rows(L, g):
                    sp.wait_ge(*of("dve", L, "mrow", g))
                    n = NT if L == "F3" else GH * NT if L == "B0" else 2 * GH * NT
                    for s in range(2):
                        r = slice(MROW + s, MROW + s + 1)
                        dst = QS[r, 1, g, :] if L == "F3" else QS[r, g % 2] if L == "B0" else (QS, KS)[g][r]
                        if L == "F3":
                            dst = dst.rearrange("s (n q) -> s n q", q=P)
                        elif L == "B0":
                            dst = dst.rearrange("s h (t q) -> s (h t) q", q=P)
                        else:
                            dst = dst.rearrange("s b h (t q) -> s (b h t) q", q=P)
                        sp.dma_start(dst, mrow[0:n, g % 2, s]).then_inc(*did(f"ld_m{g % 2}", L, g, s))

                def sums(L, ot, g, rows):
                    n = len(range(*rows.indices(P)))
                    w = n * T // P
                    sp.wait_ge(*of("act", L, "ot", g, 1))
                    sp.dma_start(rsum[:, g, 0:w], ot[rows, :].rearrange("j (a b) -> j a b", b=w)).then_inc(*did(f"ld_s{g}", L))
                    sp.wait_ge(*of("dve", L, "rinv", g))
                    sp.dma_start(ot[rows, :].rearrange("j (a b) -> j a b", b=w), rinv[:, g, 0:w]).then_inc(*did(f"ld_r{g}", L))

                def spill_half(L, n, dst, src, m):
                    sp.wait_ge(*of("dve", L, n + "lo", m))
                    sp.dma_start(dst[:, m * P:(m + 1) * P].rearrange("s p c -> p s c"), src[:, :, m]).then_inc(*did(f"st_{n}{m}", L))

                def spill(L, own):
                    for m in range(KD):
                        spill_half(L, "q", d_q, qhl, m)
                    if own:
                        for m in range(KD):
                            spill_half(L, "k", d_k, khl, m)
                    for m in range(KD):
                        sp.wait_ge(*of(f"st_q{m}", L))
                        if own:
                            sp.wait_ge(*of(f"st_k{m}", L))

                def context_attention(L):
                    spill_half(L, "q", d_q, qhl, 0)
                    spill_half(L, "q", d_q, qhl, 1)
                    for pair, stack in enumerate((QS, KS)):
                        sp.wait_ge(*of(f"st_q{pair}", L))
                        for n, s in enumerate((0, 0, 1)):
                            sp.dma_start(stack[16 * n:16 * n + 16].rearrange("i b h c -> i (b h) c"),
                                         d_q[s, pair * P:(pair + 1) * P].rearrange("(h i) c -> i h c", i=DH)).then_inc(*did(f"ld_stack{pair}", L, n))
                    max_rows(L, 0)
                    max_rows(L, 1)
                    for g in range(NG):
                        sums(L, OT[False][g], g, slice(DH, P, QUARTER))

                def own_attention(L):
                    spill(L, True)
                    stacks(L, True, 0)
                    stacks(L, True, 1)
                    max_rows(L, 0)
                    for g in range(NG):
                        if g:
                            sums(L, OT[True][g - 1], g - 1, slice(DH, P, QUARTER))
                        if g + 1 < NG:
                            max_rows(L, g + 1)
                        if g + 2 < NG:
                            stacks(L, True, g + 2)
                    sums(L, OT[True][NG - 1], NG - 1, slice(DH, P, QUARTER))

                if "B" in stages:
                    own_attention("B0")
                if "B" in stages or "C" in stages or "D" in stages or "E" in stages:
                    if "B" in stages:
                        sp.wait_ge(*of("pe", "B0", "ST", NG - 1, NT - 1, GH - 1))
                    else:
                        sp.wait_ge(*of("ld_const", 2))
                    sp.dma_start(KS[48:MROW, :, :, :], A["c_qs"]).then_inc(*did("ld_const", 3))
                if "M" in stages:
                    sp.wait_ge(*of("pe", "B0", "PV", NG - 1, NT - 1, 1))
                    for e in range(NE):
                        if e:
                            sp.wait_ge(*of("dve", "M", "wlo", e - 1, 1))
                        sp.dma_start(WSt[:, 0], A["exp_W1"][e]).then_inc(*did("ld_wexp0", e))
                        sp.dma_start(WSt[:, 1], A["exp_W2"][e]).then_inc(*did("ld_wexp1", e))
                if "C" in stages:
                    context_attention("C1")
                if "L1" in stages:
                    sp.wait_ge(*of("dve", "L1", "xs"))
                    sp.dma_start(b1b, A["L1_b1"].partition_broadcast(P)).then_inc(*did("ld_b12", 0))
                    sp.dma_start(b2b, A["L1_b2"].partition_broadcast(P)).then_inc(*did("ld_b12", 1))
                if "D" in stages:
                    context_attention("D2")
                if "E" in stages:
                    context_attention("E3")
                if "A" not in stages:
                    sp.wait_ge(*of("dve", "debug"))
                load_inputs(A["x"][1:][bs], A["ctxT"][1:][bs], A["mask"][1:][bs], did("ld_next", 0)[0])
                did("ld_next", 1), did("ld_next", 2)

                def next_context_weights():
                    sp.dma_start(KVW.rearrange("p w s k d -> p w (s k d)"), d_ctxw).then_inc(*did("ld_kvw"))

                if "F" in stages:
                    if "E" in stages:
                        sp.wait_ge(*of("pe", "E3", "ST", NG - 1, 0, GH - 1))
                    else:
                        sp.wait_ge(*of("ld_const", 2))
                    sp.dma_start(KS[MROW:MROW + 2, :, :, :], A["c_ks"][MROW - 48:MROW - 46]).then_inc(*did("ld_const", 4))
                    sp.wait_ge(*of("dve", "F", "index"))
                    for k in range(HS):
                        h = sp.value_load(rti[0:1, k:k + 1], min_val=0, max_val=15)
                        for w, n in enumerate(("Wq", "Wk", "Wv")):
                            sp.dma_start(Wst[:, w, :, k * DS:(k + 1) * DS],
                                         A["F3_" + n][:, :, bass.ds(h * DS, DS)]).then_inc(*did("ld_sel", k, w))
                        for w, n in enumerate(("bq", "bk")):
                            sp.dma_start(bsel[DS * (k % 2):DS * (k % 2) + DS, 2 * w + k // 2:2 * w + k // 2 + 1],
                                         A["F3_" + n][bass.ds(h * DS, DS)]).then_inc(*did("ld_sel", k, "b", w))
                        sp.dma_start(bvr[0:1, k * DS:(k + 1) * DS], A["F3_bv"][:, bass.ds(h * DS, DS)]).then_inc(*did("ld_sel", k, "bv"))
                    spill("F3", True)
                    for n, (dst, src) in enumerate([(QS[0:64, 0], d_q[0]), (QS[64:P, 0], d_q[1]), (KS[0:64, 0], d_k[0]),
                                                    (KS[64:P, 0], d_k[0]), (QS[0:64, 1], d_q[0]), (KS[0:64, 1], d_k[1])]):
                        sp.dma_start(dst, src.rearrange("(h i) c -> i h c", i=DS)).then_inc(*did("ld_stack0", "F3", n))
                    max_rows("F3", 0)
                    for h in range(HS):
                        if h + 1 < HS:
                            max_rows("F3", h + 1)
                        if h == HS - 1:
                            sp.wait_ge(*of("pe", "F3", "PV", h, NT - 1, 1))
                            next_context_weights()
                        sums("F3", OT4[h % 2], h, slice(DS, DS + 1, 1))
                else:
                    sp.wait_ge(*of("dve", "final"))
                    next_context_weights()
                result = out[bs].rearrange("o (t p) d -> p (o t) d", p=P)
                for p in range(NT // 2):
                    sp.wait_ge(*(of("dve", "F3", "x", p) if "F" in stages else of("dve", "final")))
                    sp.dma_start(result[:, 2 * p:2 * p + 2], X[:, 2 * p:2 * p + 2]).then_inc(*did("st_out", p))
                sp.wait_ge(*of("dve", "final"))
                for n in names:
                    if n in led.count:
                        sp.wait_ge(sems[n], led.count[n])
                sp.wait_ge(arrived, 4)
                sp.sem_clear(range(first_num, first_num + len(sems)))
                sp.sem_clear(arrived)
                for n in go:
                    sp.sem_inc(go[n], 1)

        @block.tensor
        def _(pe):
            holder, turn = {}, {"A": 0, "S": 0, "SB": 0}

            def claim(kind, *key):
                name = kind
                if kind in turn:
                    ring = ("S0", "S1", "B0", "B1") if kind == "SB" else (kind + "0", kind + "1")
                    name = ring[turn[kind] % len(ring)]
                    turn[kind] += 1
                led.slot[key] = name
                if name in holder:
                    reader = led.known.freed[holder[name]] if known else None
                    pe.wait_ge(sems[reader[0] if known else "act"], led.known.value[reader] if known else 1)
                holder[name] = key
                return SLOT[name]

            def split3(o, left, right, first, last, **kw):
                pe.matmul(o, left[0], right[0], start=first, stop=False, **kw)
                pe.matmul(o, left[0], right[1], start=False, stop=False, **kw)
                return pe.matmul(o, left[1], right[0], start=False, stop=last, **kw)

            def bias_rows(o, name, n, idt=None, last=True, **kw):
                row = (ident if idt is None else idt)[:, bi[name]:bi[name] + 1].to_broadcast([P, n])
                pe.matmul(o, row, BR[:, 0], start=False, stop=False, **kw)
                return pe.matmul(o, row, BR[:, 1], start=False, stop=last, **kw)

            def parts(t, *i):
                return t[(slice(None), 0) + i], t[(slice(None), 1) + i]

            pe.wait_ge(once["low_w"], 32)
            for i in range(LOW):
                for n, (row, ring, col) in enumerate(((i, "ring_up", 0), (LOW + i, "ring_down", 2 * HID))):
                    if i:
                        pe.wait_ge(once[ring], i)
                    for c in range(4):
                        mm = pe.matmul(flat[:, col + c * CH:col + (c + 1) * CH], identf[0:MROW + 2, row:row + 1].to_broadcast([MROW + 2, P]),
                                       low_w[:, c * CH:(c + 1) * CH], start=True, stop=True)
                    mm.then_inc(once[("spread_up", "spread_down")[n]], 1)
            pe.wait_ge(once["ring_up"], LOW)
            pe.wait_ge(once["ring_down"], LOW)
            pe.wait_ge(once["wsum"], 2)
            pe.wait_ge(once["pool"], 1)
            pe.matmul(SLOT["S0"][:, 0:2], onesf[:], wsc[:, 0:2], start=True, stop=True).then_inc(once["pe"], 1)
            pe.wait_ge(once["up"], 6 * LOW)
            pe.wait_ge(once["rows_e"], 16)
            pe.wait_ge(once["ternary"], 1)
            for m in range(NM):
                mm = pe.matmul(PS[:, m, 0:D + 1], low_up[:, 0, m * P:(m + 1) * P], rows_e[:, m], start=True, stop=True)
            mm.then_inc(once["pe"], 1)
            pe.wait_ge(once["down"], 6 * LOW)
            pe.wait_ge(once["high"], 16 * HIGH + 1)
            for m in range(NM):
                mm = pe.matmul(flat[:, m * D:(m + 1) * D], low_down[:, 0, m * P:(m + 1) * P], rows_c[:, m], start=True, stop=True)
            mm.then_inc(once["pe"], 1)
            pe.wait_ge(once["high"], 2 * 16 * HIGH + 1)
            for k in range(KD):
                for m in range(NM):
                    mm = pe.transpose(flat[:, 2 * HID + k * HID + m * P:2 * HID + k * HID + (m + 1) * P], rows_e[:, m, k * P:(k + 1) * P], identf[:])
            mm.then_inc(once["pe"], 1)
            batch_end(pe, "pe")

            with pe.Fori(0, NB):
                def turn_x(N):
                    for k in range(KD):
                        s = claim("A", "T", N, k)
                        for t in range(NT):
                            pe.wait_ge(*of("dve", N, "xn", t))
                            mm = pe.transpose(s[:, t * P:(t + 1) * P], XN[N][:, t, k * P:(k + 1) * P], identf[:])
                        mm.then_inc(*did("pe", "T", N, k))

                def project(key, weight):
                    s = claim("A", *key)
                    for c in range(2):
                        for k in range(KD):
                            mm = split3(s[:, c * CH:(c + 1) * CH], weight(k), parts(XT, k, slice(c * CH, (c + 1) * CH)), k == 0, k == KD - 1)
                    mm.then_inc(*did("pe", *key))

                def wflat(name, m):
                    return lambda k: (Wf[:, wi[name], 0, k, m * P:(m + 1) * P], Wf[:, wi[name], 1, k, m * P:(m + 1) * P])

                if "A" in stages:
                    turn_x("A")
                pe.wait_ge(*of("dve", "ctlo"))

                def kvw(name, k, a, b):
                    return KVW[:, ci[name], 0, k, a:b], KVW[:, ci[name], 1, k, a:b]

                s = claim("S", "K0")
                for k in range(KD):
                    mm = split3(s[:, 0:TC], kvw("A0k", k, 0, P), parts(CT, k, slice(0, TC)), k == 0, k == KD - 1)
                mm.then_inc(*did("pe", "K0"))
                s = claim("S", "V0")
                for k in range(KD):
                    mm = split3(s[0:TC, 0:D], parts(CT, k, slice(0, TC)), kvw("A0v", k, 0, D), k == 0, k == KD - 1)
                mm.then_inc(*did("pe", "V0"))
                for l, L in enumerate(XL):
                    for m in range(KD):
                        s = claim("S", "KX", l, m)
                        for k in range(KD):
                            mm = split3(s[:, 0:TC], kvw(L + "k", k, m * P, (m + 1) * P), parts(CT, k, slice(0, TC)), k == 0, k == KD - 1)
                        mm.then_inc(*did("pe", "KX", l, m))
                    s = claim("S", "VX", l)
                    for k in range(KD):
                        mm = split3(s[0:TC, 0:D], parts(CT, k, slice(0, TC)), kvw(L + "v", k, 0, D), k == 0, k == KD - 1 and L == "C1")
                    if L != "C1":
                        mm = bias_rows(s[0:TC, 0:D], L + "v", TC)
                    mm.then_inc(*did("pe", "VX", l))

                if "A" in stages:
                    pe.wait_ge(*of("dve", "A", "xlo", 1))
                    for h in range(2):
                        project(("A", "Q", h), wflat("A0q", h))
                    pe.wait_ge(*of("dve", "A", "kp0"))
                    pe.wait_ge(*of("dve", "A", "qlo", 1))
                    for t in range(NT):
                        s = claim("S", "A", "S", t)
                        for h in range(2):
                            mm = split3(s[:, h * TC:(h + 1) * TC], (q0[:, 0, h, t * P:(t + 1) * P], q0[:, 1, h, t * P:(t + 1) * P]),
                                        parts(KP0, slice(0, TC)), True, True)
                        mm.then_inc(*did("pe", "A", "S", t))
                    s = claim("A", "A", "PT")
                    for t in range(NT):
                        pe.wait_ge(*of("dve", "A", "p", t))
                        mm = pe.transpose(s[0:TC, t * P:(t + 1) * P], A0[:, t, :], identf[:])
                    mm.then_inc(*did("pe", "A", "PT"))
                    pe.wait_ge(*of("dve", "A", "ptlo"))
                    pe.wait_ge(*of("dve", "A", "vp0"))
                    for m in range(KD):
                        s = claim("A", "A", "O", m)
                        for c in range(2):
                            mm = split3(s[:, c * CH:(c + 1) * CH], (VP0[0:TC, 0, m * P:(m + 1) * P], VP0[0:TC, 1, m * P:(m + 1) * P]),
                                        (AT0[0:TC, 0, c * CH:(c + 1) * CH], AT0[0:TC, 1, c * CH:(c + 1) * CH]), True, True)
                        mm.then_inc(*did("pe", "A", "O", m))
                    for t in range(NT):
                        s = claim("S", "A", "N", t)
                        split3(s[:, 0:D], (AT0[0:TC, 0, t * P:(t + 1) * P], AT0[0:TC, 1, t * P:(t + 1) * P]),
                               (VP0[0:TC, 0, :], VP0[0:TC, 1, :]), True, True).then_inc(*did("pe", "A", "N", t))
                    pe.wait_ge(*of("dve", "A", "olo", 1))
                    for t in range(NT):
                        s = claim("S", "A", "W", t)
                        for k in range(KD):
                            mm = split3(s[:, 0:D], parts(AO0, k, slice(t * P, (t + 1) * P)),
                                        (Wf[:, wi["A0o"], 0, k, :], Wf[:, wi["A0o"], 1, k, :]), k == 0, k == KD - 1)
                        mm.then_inc(*did("pe", "A", "W", t))

                banks = [None] * (NT // 2)

                def output_part(L, kind, g, on, w, bias):
                    if kind == "WS":
                        pe.wait_ge(*of("dve", L, "onlo", g))
                    for p, name in enumerate(("S0", "S1", "B0", "B1")):
                        if (p >= 2) != (kind == "WB"):
                            continue
                        if g == 0:
                            banks[p] = claim(name, L, "W", p)
                        for i in range(2):
                            o = banks[p][:, i * D:(i + 1) * D]
                            t = 2 * p + i
                            split3(o, parts(on, g, slice(t * P, (t + 1) * P)), (w[0:on.shape[0], 0, g, :], w[0:on.shape[0], 1, g, :]),
                                   g == 0 and i == 0, False, skip_group_check=True)
                            if bias and g == 0:
                                bias_rows(o, bias, P, last=False, skip_group_check=True)

                def output_last(L, g, on, w):
                    pe.wait_ge(*of("dve", L, "onlo", g))
                    for t in range(NT):
                        mm = split3(banks[t // 2][:, (t % 2) * D:(t % 2 + 1) * D], parts(on, g, slice(t * P, (t + 1) * P)),
                                    (w[0:on.shape[0], 0, g, :], w[0:on.shape[0], 1, g, :]), False, True, skip_group_check=True)
                        if t % 2:
                            mm.then_inc(*did("pe", L, "W", t // 2))

                def attention(L, own):
                    for m in range(KD):
                        project((L, "q", m), wflat(L + "q", m))
                    if own:
                        for m in range(KD):
                            project((L, "k", m), wflat(L + "k", m))
                        for t in range(NT):
                            s = claim("S", L, "v", t)
                            for k in range(KD):
                                split3(s[:, 0:D], parts(XT, k, slice(t * P, (t + 1) * P)),
                                       (Wf[:, wi[L + "v"], 0, k, :], Wf[:, wi[L + "v"], 1, k, :]), k == 0, False)
                            bias_rows(s[:, 0:D], L + "v", P).then_inc(*did("pe", L, "v", t))
                    l = None if own else XL.index(L)
                    steps = attention_steps(own)
                    probs, np_ = (PR, NP) if own else (PRX, NPX)
                    ring = {s[1:]: n % np_ for n, s in enumerate(s for s in steps if s[0] == "ST")}
                    for step in steps:
                        kind = step[0]
                        g = step[1] if len(step) > 1 else None
                        if g is not None:
                            buf = g % 2
                            q_stack = QS if own or g < 2 else KS
                        if kind == "S" and own:
                            t, j = step[2:]
                            if t == 0 and j == 0:
                                pe.wait_ge(*of(f"ld_stack{buf}", L, g, "k", 2))
                                pe.wait_ge(*of("ld_const", 2))
                            keys = (t + 1) * P
                            for c in range((keys + CH - 1) // CH):
                                n = min(CH, keys - c * CH)
                                s = claim("S" if g else "SB", L, "S", g, t, j, c)
                                on_edge = c * CH + n == keys
                                mm = pe.matmul(s[:, 0:n], QS[0:MROW, buf, j, t * P:(t + 1) * P], KS[0:MROW, buf, j, c * CH:c * CH + n],
                                               start=True, stop=not on_edge)
                                if on_edge:
                                    mm = pe.matmul(s[:, n - P:n], big[:], causal[:, 0, :], start=False, stop=True)
                                mm.then_inc(*did("pe", L, "S", g, t, j, c))
                        elif kind == "S":
                            t = step[2]
                            if t == 0:
                                pe.wait_ge(*of(f"ld_stack{g // 2}", L, 2))
                                pe.wait_ge(*of("ld_const", 3))
                                pe.wait_ge(*of("ld_kx", "mask"))
                            s = claim("SB", L, "S", g, t)
                            for j in range(GH):
                                mm = pe.matmul(s[:, j * TX:(j + 1) * TX], q_stack[0:MROW, buf, j, t * P:(t + 1) * P],
                                               KX[0:MROW, l, g * GH + j, :], start=True, stop=True)
                            mm.then_inc(*did("pe", L, "S", g, t))
                        elif kind == "MT":
                            s = claim("S", L, "MT", g)
                            if own:
                                pe.wait_ge(*of("dve", L, "negm", g))
                                pe.transpose(s[0:GH * NT, 0:P], negm[:, g % 2, :], identf[:]).then_inc(*did("pe", L, "MT", g))
                            else:
                                pe.wait_ge(*of("dve", "free", L, "S", 2 * g + 1, NT - 1))
                                pe.transpose(s[0:2 * GH * NT, 0:P], negp[g], identf[:]).then_inc(*did("pe", L, "MT", g))
                        elif kind == "ST":
                            kt, j = step[2:]
                            if kt == 0 and j == 0:
                                m = g if own else g // 2
                                pe.wait_ge(*of(f"ld_m{m % 2}", L, m, 1))
                            s = claim("A", L, "ST", g, kt, j)
                            q0_ = kt * P
                            for c in range(2):
                                a = max(q0_, c * CH)
                                if a >= (c + 1) * CH:
                                    continue
                                key_rows = KS[0:MROW + 2, buf, j, kt * P:(kt + 1) * P] if own else KX[0:MROW + 2, l, g * GH + j, :]
                                o = s[0:P if own else TX, a:(c + 1) * CH]
                                edge = own and a == q0_
                                mm = pe.matmul(o, key_rows, q_stack[0:MROW + 2, buf, j, a:(c + 1) * CH], start=True, stop=not edge)
                                if edge:
                                    mm = pe.matmul(s[:, a:a + P], big[:], causal[:, 1, :], start=False, stop=True)
                            mm.then_inc(*did("pe", L, "ST", g, kt, j))
                        elif kind == "PV":
                            kt, c = step[2:]
                            if kt == 0 and c == 0:
                                acc = [claim("B0", L, "PVacc", g, 0), claim("B1", L, "PVacc", g, 1)]
                                if g == 0:
                                    pe.wait_ge(*(of("act", L, "vp", NT - 1) if own else of("act", "free", "VX", len(XL) - 1)))
                            if c == 0 or kt >= NT // 2:
                                pe.wait_ge(*of("act", L, "exp", g, kt, GH - 1))
                            a = max(kt * P, c * CH)
                            final = kt == (min(NT if own else 1, NT // 2 * (c + 1)) - 1)
                            for j in range(GH):
                                v = VP[:, kt, g * GH + j, :] if own else VX[0:TX, l, g * GH + j, :]
                                p = probs[0:P if own else TX, ring[g, kt, j], a:(c + 1) * CH]
                                mm = pe.matmul(acc[c][QUARTER * j:QUARTER * (j + 1), a - c * CH:CH], v, p, start=kt == 0, stop=final,
                                               tile_position=(0, QUARTER * j))
                            mm.then_inc(*did("pe", L, "PV", g, kt, c))
                        elif kind == "NB":
                            s = claim("A", L, "NB", g)
                            pe.wait_ge(*of(f"ld_r{g}", L))
                            for c in range(2):
                                mm = pe.matmul(s[:, c * CH:(c + 1) * CH], E4[:], OT[own][g][:, c * CH:(c + 1) * CH], start=True, stop=True)
                            mm.then_inc(*did("pe", L, "NB", g))
                        elif kind in ("WS", "WB"):
                            name, bias = {"B0": ("B0p", "B0p"), "C1": ("C1o", "C1o"), "D2": ("D2o", "D2o"), "E3": ("E3id", None)}[L]
                            output_part(L, kind, g, ON, Wp[:, pi[name]], bias)
                        elif kind == "WL":
                            output_last(L, NG - 1, ON, Wp[:, pi[name]])

                def block_of(N, L, own):
                    turn_x(N)
                    pe.wait_ge(*of("dve", N, "xlo", 1))
                    attention(L, own)

                if "B" in stages:
                    block_of("B", "B0", True)

                if "M" in stages:
                    turn_x("M")
                    pe.wait_ge(*of("dve", "M", "xlo", 1))
                    s = claim("S", "M", "gate")
                    for t in range(NT):
                        for k in range(KD):
                            mm = split3(s[:, t * NE:(t + 1) * NE], parts(XT, k, slice(t * P, (t + 1) * P)), parts(gateW, k), k == 0, k == KD - 1)
                    mm.then_inc(*did("pe", "M", "gate"))
                    order = [(e, c, m) for e in range(NE) for c in range(2) for m in range(NM)]

                    def up(e, c, m):
                        if c == 0 and m == 0:
                            pe.wait_ge(*of("dve", "M", "wlo", e, 1))
                        s = claim("A", "M", "U", e, c, m)
                        w1 = Wm[e % 2][:, 0].rearrange("p s (k n) -> p s k n", k=KD)
                        for k in range(KD):
                            mm = split3(s[:, 0:CH], parts(w1, k, slice(m * P, (m + 1) * P)), parts(XT, k, slice(c * CH, (c + 1) * CH)),
                                        k == 0, k == KD - 1)
                        mm.then_inc(*did("pe", "M", "U", e, c, m))

                    def down(e, c, m):
                        n = (e * 2 + c) * NM + m
                        if m == 0:
                            pair = ("B0", "B1") if (2 * e + c) % 2 == 0 else ("S0", "S1")
                            acc[:] = [claim(pair[0], "M", "D", e, c, 0), claim(pair[1], "M", "D", e, c, 1)]
                        pe.wait_ge(*of("dve", "M", "midlo", e, c, m))
                        w2 = Wm[e % 2][:, 1].rearrange("p s (m n) -> p s m n", m=NM)
                        for i in range(4):
                            o = acc[i // 2][:, (i % 2) * D:(i % 2 + 1) * D]
                            left = (mid[:, n % 4, 0, i * P:(i + 1) * P], mid[:, n % 4, 1, i * P:(i + 1) * P])
                            mm = split3(o, left, parts(w2, m), m == 0 and i % 2 == 0, False, skip_group_check=True)
                            if m == NM - 1:
                                mm = bias_rows(o, f"e{e}", P, last=True, skip_group_check=True)
                        mm.then_inc(*did("pe", "M", "D", e, c, m))

                    acc = [None, None]
                    for n in range(len(order) + 2):
                        if n < len(order):
                            up(*order[n])
                        if n >= 2:
                            down(*order[n - 2])

                if "C" in stages:
                    block_of("C", "C1", False)

                if "L1" in stages:
                    for k in range(KD):
                        s = claim("A", "L1", "XQ", k).bitcast(F16)
                        for t in range(NT):
                            pe.wait_ge(*of("dve", "L1", "xq", t))
                            mm = pe.transpose(s[:, t * P:(t + 1) * P], xq[:, t, k * P:(k + 1) * P], ident[:])
                        mm.then_inc(*did("pe", "L1", "XQ", k))
                    pe.wait_ge(*of("act", "L1", "xqT", 1))

                    def ternary_up(t):
                        s = claim("A", "L1", "H1", t)
                        for c in range(2):
                            for k in range(KD):
                                mm = pe.matmul(s[:, c * CH:(c + 1) * CH], xqT[:, k, t * P:(t + 1) * P], Wq1[:, k, c * CH:(c + 1) * CH],
                                               start=k == 0, stop=k == KD - 1)
                        mm.then_inc(*did("pe", "L1", "H1", t))

                    def ternary_down(t):
                        s = claim("S", "L1", "HQ", t).bitcast(F16)
                        pe.wait_ge(*of("dve", "L1", "hq", t))
                        for m in range(NM):
                            mm = pe.transpose(s[:, m * P:(m + 1) * P], hq[:, t % 2, m * P:(m + 1) * P], ident[:])
                        mm.then_inc(*did("pe", "L1", "HQ", t))
                        s = claim("S", "L1", "H2", t)
                        pe.wait_ge(*of("act", "L1", "hqT", t))
                        for m in range(NM):
                            mm = pe.matmul(s[:, 0:D], hqT[:, t % 2, m * P:(m + 1) * P], Wq2[:, m, :], start=m == 0, stop=m == NM - 1)
                        mm.then_inc(*did("pe", "L1", "H2", t))

                    for t in range(NT + 2):
                        if t < NT:
                            ternary_up(t)
                        if t >= 2:
                            ternary_down(t - 2)

                if "D" in stages:
                    block_of("D", "D2", False)

                if "L2" in stages:
                    turn_x("L2")
                    pe.wait_ge(*of("act", "L2", "xf", 1))

                    def butterfly_up(c):
                        for m in range(NM):
                            s = claim("A", "L2", "G", c, m)
                            for k in range(KD):
                                mm = pe.matmul(s[:, 0:CH], Wexp[:, k, m * P:(m + 1) * P], XTf[:, k, c * CH:(c + 1) * CH],
                                               start=k == 0, stop=k == KD - 1)
                            mm.then_inc(*did("pe", "L2", "G", c, m))

                    def butterfly_down(c):
                        for t in range(4 * c, 4 * c + 4):
                            s = claim("S", "L2", "Y", t)
                            pe.wait_ge(*of("act", "L2", "g", c, NM - 1))
                            for m in range(NM):
                                pe.matmul(s[:, 0:D], gT[:, c, m, (t % 4) * P:(t % 4 + 1) * P], RT[:, m, :], start=m == 0, stop=False)
                            bias_rows(s[:, 0:D], "L2con", P, idt=small, last=False)
                            bias_rows(s[:, 0:D], "L2down", P, idt=small).then_inc(*did("pe", "L2", "Y", t))

                    butterfly_up(0)
                    butterfly_up(1)
                    butterfly_down(0)
                    butterfly_down(1)

                if "E" in stages:
                    block_of("E", "E3", False)

                if "F" in stages:
                    turn_x("F")
                    s = claim("S", "F", "R")
                    pe.wait_ge(*of("dve", "F", "xmean", 1))
                    for k in range(KD):
                        mm = pe.matmul(s[0:1, 0:NH], xmean[:, k:k + 1], F3Wr[:, k, :], start=k == 0, stop=k == KD - 1)
                    mm.then_inc(*did("pe", "F", "R"))
                    s = claim("S", "F", "G")
                    pe.wait_ge(*of("dve", "F", "gates"))
                    pe.matmul(s[:, 0:HS], onesf[0:1, :], rt[0:1, 48:48 + HS], start=True, stop=True).then_inc(*did("pe", "F", "G"))
                    pe.wait_ge(*of("dve", "F", "xlo", 1))
                    pe.wait_ge(*of("dve", "F", "wsel_lo"))
                    for w, n in enumerate("qk"):
                        for m in range(KD):
                            project(("F3", n, m), lambda k: (Wsel[:, w, 0, k, m * P:(m + 1) * P], Wsel[:, w, 1, k, m * P:(m + 1) * P]))
                    pe.wait_ge(*of("dve", "F", "bv_lo"))
                    for t in range(NT):
                        s = claim("S", "F3", "v", t)
                        for k in range(KD):
                            split3(s[:, 0:D], parts(XT, k, slice(t * P, (t + 1) * P)), (Wsel[:, 2, 0, k, :], Wsel[:, 2, 1, k, :]), k == 0, False)
                        pe.matmul(s[:, 0:D], ident[0:1, 0:1].to_broadcast([1, P]), bvh[:, 0, :], start=False, stop=False)
                        pe.matmul(s[:, 0:D], ident[0:1, 0:1].to_broadcast([1, P]), bvh[:, 1, :], start=False, stop=True).then_inc(*did("pe", "F3", "v", t))
                    pe.wait_ge(*of("ld_stack0", "F3", 5))
                    pe.wait_ge(*of("ld_const", 4))
                    for step in last_attention_steps():
                        kind = step[0]
                        h = step[1] if len(step) > 1 else None
                        if kind == "S":
                            t, c = step[2:]
                            s = claim("S" if h else "SB", "F3", "S", h, t, c)
                            pe.matmul(s[:], QS[:, 0, h, t * P:(t + 1) * P], KS[:, 0, h, c * CH:(c + 1) * CH], start=True, stop=False)
                            pe.matmul(s[:], QS[0:MROW, 1, h, t * P:(t + 1) * P], KS[0:MROW, 1, h, c * CH:(c + 1) * CH],
                                      start=False, stop=True).then_inc(*did("pe", "F3", "S", h, t, c))
                        elif kind == "MT":
                            pe.wait_ge(*of("dve", "F3", "negm", h))
                            s = claim("S", "F3", "MT", h)
                            pe.transpose(s[0:NT, 0:P], negm[:, h % 2, 0:NT], identf[:]).then_inc(*did("pe", "F3", "MT", h))
                        elif kind == "ST":
                            kt = step[2]
                            if kt == 0:
                                pe.wait_ge(*of(f"ld_m{h % 2}", "F3", h, 1))
                            s = claim("A", "F3", "ST", h, kt)
                            for c in range(2):
                                pe.matmul(s[:, c * CH:(c + 1) * CH], KS[:, 0, h, kt * P:(kt + 1) * P], QS[:, 0, h, c * CH:(c + 1) * CH],
                                          start=True, stop=False)
                                mm = pe.matmul(s[:, c * CH:(c + 1) * CH], KS[0:MROW + 2, 1, h, kt * P:(kt + 1) * P],
                                               QS[0:MROW + 2, 1, h, c * CH:(c + 1) * CH], start=False, stop=True)
                            mm.then_inc(*did("pe", "F3", "ST", h, kt))
                        elif kind == "PV":
                            kt, c = step[2:]
                            if kt == 0 and c == 0:
                                acc = [claim("B0", "F3", "PVacc", h, 0), claim("B1", "F3", "PVacc", h, 1)]
                                if h == 0:
                                    pe.wait_ge(*of("act", "F3", "vp", NT - 1))
                            if c == 0:
                                pe.wait_ge(*of("act", "F3", "exp", h, kt))
                            pe.matmul(acc[c][0:TX], VP4[:, kt, h, :], PR4[:, (h * NT + kt) % NP, c * CH:(c + 1) * CH],
                                      start=kt == 0, stop=kt == NT - 1).then_inc(*did("pe", "F3", "PV", h, kt, c))
                        elif kind == "NB":
                            s = claim("A", "F3", "NB", h)
                            pe.wait_ge(*of(f"ld_r{h}", "F3"))
                            for c in range(2):
                                mm = pe.matmul(s[0:TX, c * CH:(c + 1) * CH], E64[:], OT4[h % 2][:, c * CH:(c + 1) * CH], start=True, stop=True)
                            mm.then_inc(*did("pe", "F3", "NB", h))
                        elif kind in ("WS", "WB"):
                            output_part("F3", kind, h, ON4, Wp[:, pi["F3o"]], "F3o")
                        elif kind == "WL":
                            output_last("F3", HS - 1, ON4, Wp[:, pi["F3o"]])
                batch_end(pe, "pe")

        @block.scalar
        def _(act):
            for i in range(LOW):
                for spread, ring, user, dst, col in (("spread_up", "ring_up", "up", ring_up, 0),
                                                     ("spread_down", "ring_down", "down", ring_down, 2 * HID)):
                    act.wait_ge(once[spread], i + 1)
                    if i >= 2:
                        act.wait_ge(once[user], 6 * (i - 1))
                    act.activation(dst[:, i % 2], flat[:, col:col + 2 * HID], ACT.Copy).then_inc(once[ring], 1)
                if i == 1:
                    act.wait_ge(once["load"], 16 * N_LOADS)
                    act.activation(Wf[:, :, 0].rearrange("p w k d -> p w (k d)"),
                                   stage_flat[:, 0:len(FLAT) * FLAT_N].rearrange("p (w n) -> p w n", n=FLAT_N), ACT.Copy, scale=WS).then_inc(once["act"], 1)
                if i == 2:
                    act.activation(Wp[:, :, 0].rearrange("p w k d -> p w (k d)"), stage_pad.rearrange("p (w n) -> p w n", n=PAD_N),
                                   ACT.Copy, scale=WS).then_inc(once["act"], 1)
            act.wait_ge(once["lambda"], 1)
            act.activation(lamt[:, 2:4], lamt[:, 0:2], ACT.Exp).then_inc(once["act"], 1)
            act.wait_ge(once["pe"], 2)
            act.activation(rows_e, PS[:, :, 0:D + 1], ACT.Copy).then_inc(once["act"], 1)
            act.wait_ge(once["pe"], 3)
            act.activation(RT[:].rearrange("p m d -> p (m d)"), flat[:, 0:NM * D], ACT.Copy).then_inc(once["act"], 1)
            batch_end(act, "act")

            with act.Fori(0, NB):
                def norm_std(N):
                    act.wait_ge(*of("dve", N, "mv"))
                    act.activation(sd[:], mv[:, :, 1], ACT.Sqrt, bias=epsc[:, 0:1], scale=1.0).then_inc(*did("act", N, "sd"))

                def x_hi(N):
                    for k in range(KD):
                        act.wait_ge(*of("pe", "T", N, k))
                        act.activation(XT[:, 0, k], slot("T", N, k), ACT.Copy).then_inc(*did("act", N, "xhi", k))

                def x_affine(N, g_, b_):
                    for k in range(KD):
                        act.wait_ge(*of("pe", "T", N, k))
                        if k:
                            act.wait_ge(*of("dve", N, "xlo", k - 1))
                        act.activation(tmp, slot("T", N, k), ACT.Identity, bias=BC[:, bc[b_] + k:bc[b_] + k + 1],
                                       scale=BC[:, bc[g_] + k:bc[g_] + k + 1]).then_inc(*frees("act", "T", N, k))

                def q_f32(L, n, scale):
                    for m in range(KD):
                        act.wait_ge(*of("pe", L, n, m))
                        if (n, m) != ("q", 0):
                            act.wait_ge(*of("dve", L, *(("qlo", 0) if (n, m) == ("q", 1) else ("qlo", 1) if m == 0 else ("klo", 0))))
                        name = L + n
                        b = BC[:, bc[name] + m:bc[name] + m + 1] if name in bc else epsc[:, 1:2]
                        act.activation(tmp, slot(L, n, m), ACT.Identity, bias=b, scale=scale / WS).then_inc(*frees("act", L, n, m))

                act.activation(CT[:, 0, :, 0:TC], CTf[:], ACT.Copy).then_inc(*did("act", "cthi"))
                if "A" in stages:
                    norm_std("A")
                    x_hi("A")
                act.wait_ge(*of("pe", "K0"))
                act.activation(KP0[:, 0, 0:TC], slot("K0")[:, 0:TC], ACT.Copy, scale=1.0 / WS).then_inc(*did("act", "kp0hi"))
                act.wait_ge(*of("pe", "V0"))
                act.activation(VP0[0:TC, 0, :], slot("V0")[0:TC, 0:D], ACT.Copy, scale=1.0 / WS).then_inc(*did("act", "vp0hi"))
                for l, L in enumerate(XL):
                    for m in range(KD):
                        act.wait_ge(*of("pe", "KX", l, m))
                        b = BC[:, bc[L + "k"] + m:bc[L + "k"] + m + 1] if L != "C1" else epsc[:, 1:2]
                        act.activation(kxf[:, l, m, 0:TC], slot("KX", l, m)[:, 0:TC], ACT.Identity, bias=b,
                                       scale=1.0 / WS).then_inc(*frees("act", "KX", l, m))
                    act.wait_ge(*of("pe", "VX", l))
                    act.activation(VX[0:TC, l, :, 0:DH], slot("VX", l)[0:TC, 0:D].rearrange("p (h d) -> p h d", d=DH), ACT.Copy,
                                   scale=1.0 / WS).then_inc(*frees("act", "VX", l))

                if "A" in stages:
                    for h in range(2):
                        act.wait_ge(*of("pe", "A", "Q", h))
                        act.activation(q0[:, 0, h], slot("A", "Q", h), ACT.Copy, scale=float(P) ** -0.5 / WS).then_inc(*did("act", "A", "qhi", h))
                    for t in range(NT):
                        act.wait_ge(*of("dve", "A", "m", t))
                        if t >= 2:
                            act.wait_ge(*of("dve", "A", "p", t - 2))
                        for h in range(2):
                            act.activation(E0[:, t % 2, h], slot("A", "S", t)[:, h * TC:(h + 1) * TC], ACT.Exp, bias=sm[:, 2 * t + h:2 * t + h + 1],
                                           scale=1.0, accum_out=sm[:, 16 + 2 * t + h:17 + 2 * t + h]
                                           ).then_inc(*(frees("act", "A", "S", t) if h else did("act", "A", "e0", t)))
                    act.wait_ge(*of("pe", "A", "PT"))
                    act.activation(AT0[0:TC, 0, :], slot("A", "PT")[0:TC], ACT.Copy).then_inc(*did("act", "A", "pthi"))
                    for m in range(KD):
                        act.wait_ge(*of("pe", "A", "O", m))
                        act.activation(AO0[:, 0, m], slot("A", "O", m), ACT.Copy).then_inc(*did("act", "A", "ohi", m))
                    for t in range(NT):
                        act.wait_ge(*of("pe", "A", "N", t))
                        if t >= 2:
                            act.wait_ge(*of("act", "free", "A", "N", t - 2))
                        act.activation(sq0[:, t % 2], slot("A", "N", t)[:, 0:D], ACT.Square,
                                       accum_out=sm[:, 64 + t:65 + t]).then_inc(*frees("act", "A", "N", t))
                    act.wait_ge(*of("act", "free", "A", "N", NT - 1))
                    act.activation(sm[:, 72:80], sm[:, 64:72], ACT.Sqrt, bias=epsc[:, 0:1], scale=1.0 / D).then_inc(*did("act", "A", "rms"))

                def exps(L, own, steps):
                    n = 0
                    probs, np_ = (PR, NP) if own else (PRX, NPX)
                    for step in steps:
                        if step[0] == "ST":
                            _, g, kt, j = step
                            act.wait_ge(*of("pe", L, "ST", g, kt, j))
                            if n >= np_:
                                g0, k0, j0 = [s[1:] for s in steps if s[0] == "ST"][n - np_]
                                act.wait_ge(*of("pe", L, "PV", g0, k0, 1))
                            rows = P if own else TX
                            act.activation(probs[0:rows, n % np_, kt * P:T], slot(L, "ST", g, kt, j)[0:rows, kt * P:T],
                                           ACT.Exp).then_inc(*did("act", L, "exp", g, kt, j))
                            led.freed[(L, "ST", g, kt, j)] = ("act", (L, "exp", g, kt, j))
                            n += 1
                        elif step[0] == "PV" and step[2:] == (NT - 1 if own else 0, 1):
                            g = step[1]
                            act.wait_ge(*of("pe", L, "PV", g, step[2], 1))
                            if own and g >= 2:
                                act.wait_ge(*of("dve", L, "onf", g - 2))
                            for c in range(2):
                                act.activation(OT[own][g][:, c * CH:(c + 1) * CH], slot(L, "PVacc", g, c), ACT.Copy).then_inc(*did("act", L, "ot", g, c))
                                led.freed[(L, "PVacc", g, c)] = ("act", (L, "ot", g, c))

                def attention(L, own):
                    q_f32(L, "q", 0.25)
                    if own:
                        q_f32(L, "k", 1.0)
                        act.wait_ge(*of("dve", L, "ones"))
                        for t in range(NT):
                            act.wait_ge(*of("pe", L, "v", t))
                            act.activation(VP[:, t, :, 0:DH], slot(L, "v", t)[:, 0:D].rearrange("p (h d) -> p h d", d=DH), ACT.Copy,
                                           scale=1.0 / WS).then_inc(*did("act", L, "vp", t))
                            led.freed[(L, "v", t)] = ("act", (L, "vp", t))
                    exps(L, own, attention_steps(own))

                if "B" in stages:
                    norm_std("B1")
                    norm_std("B")
                    x_affine("B", "ln1_g", "ln1_b")
                    attention("B0", True)

                if "M" in stages:
                    def weights_hi(e, w):
                        act.wait_ge(*of(f"ld_wexp{w}", e))
                        if e >= 2:
                            act.wait_ge(*of("pe", "M", "D", e - 2, 1, NM - 1))
                        act.activation(Wm[e % 2][:, w, 0], WSt[:, w], ACT.Copy, scale=WS).then_inc(*did("act", "M", "whi", e, w))

                    weights_hi(0, 0)
                    weights_hi(0, 1)
                    norm_std("M")
                    x_affine("M", "ln2_g", "ln2_b")
                    act.wait_ge(*of("dve", "M", "d"))
                    act.activation(sm[:, 88:96], sm[:, 80:88], ACT.Exp).then_inc(*did("act", "M", "e"))
                    n = 0
                    for e in range(NE):
                        for c in range(2):
                            for m in range(NM):
                                act.wait_ge(*of("pe", "M", "U", e, c, m))
                                if n >= 3:
                                    act.wait_ge(*of("dve", "M", "midlo", *back(e, c, m, 3)))
                                act.activation(midf[:, n % 3], slot("M", "U", e, c, m)[:, 0:CH], ACT.Gelu,
                                               bias=BC[:, BC_E1 + e * NM + m:BC_E1 + e * NM + m + 1],
                                               scale=1.0 / WS).then_inc(*frees("act", "M", "U", e, c, m))
                                n += 1
                                if e + 1 < NE and (c, m) in ((0, 4), (1, 0)):
                                    weights_hi(e + 1, c)

                if "C" in stages:
                    norm_std("C")
                    x_hi("C")
                    attention("C1", False)

                if "L1" in stages:
                    norm_std("L1")
                    for k in range(KD):
                        act.wait_ge(*of("pe", "L1", "XQ", k))
                        act.activation(xqT[:, k], slot("L1", "XQ", k).bitcast(F16)[:, 0:T], ACT.Copy).then_inc(*did("act", "L1", "xqT", k))
                        led.freed[("L1", "XQ", k)] = ("act", ("L1", "xqT", k))
                    for t in range(NT + 1):
                        if t < NT:
                            act.wait_ge(*of("dve", "L1", "h", t))
                            act.activation(hb[:, t % 3], hb[:, t % 3], ACT.Gelu).then_inc(*did("act", "L1", "gelu", t))
                        if t:
                            act.wait_ge(*of("pe", "L1", "HQ", t - 1))
                            if t >= 3:
                                act.wait_ge(*of("pe", "L1", "H2", t - 3))
                            act.activation(hqT[:, (t - 1) % 2], slot("L1", "HQ", t - 1).bitcast(F16)[:, 0:HID], ACT.Copy
                                           ).then_inc(*did("act", "L1", "hqT", t - 1))
                            led.freed[("L1", "HQ", t - 1)] = ("act", ("L1", "hqT", t - 1))

                if "D" in stages:
                    norm_std("D")
                    x_hi("D")
                    attention("D2", False)

                if "L2" in stages:
                    norm_std("L2")
                    for k in range(KD):
                        act.wait_ge(*of("pe", "T", "L2", k))
                        act.activation(XTf[:, k], slot("T", "L2", k), ACT.Copy).then_inc(*did("act", "L2", "xf", k))
                        led.freed[("T", "L2", k)] = ("act", ("L2", "xf", k))
                    for c in range(2):
                        for m in range(NM):
                            act.wait_ge(*of("pe", "L2", "G", c, m))
                            act.activation(gT[:, c, m], slot("L2", "G", c, m)[:, 0:CH], ACT.Gelu, bias=upb[:, m:m + 1],
                                           scale=1.0).then_inc(*did("act", "L2", "g", c, m))
                            led.freed[("L2", "G", c, m)] = ("act", ("L2", "g", c, m))

                if "E" in stages:
                    norm_std("E")
                    x_hi("E")
                    attention("E3", False)

                if "F" in stages:
                    norm_std("F")
                    x_hi("F")
                    act.wait_ge(*of("dve", "F", "lmax"))
                    act.activation(rt[0:1, 0:NH], rt[0:1, 0:NH], ACT.Exp, bias=rt[0:1, 24:25], scale=1.0,
                                   accum_out=rt[0:1, 25:26]).then_inc(*did("act", "F", "e1"))
                    act.wait_ge(*of("dve", "F", "index"))
                    act.activation(rt[0:1, 40:44], rt[0:1, 28:32], ACT.Exp, bias=rt[0:1, 36:37], scale=1.0,
                                   accum_out=rt[0:1, 44:45]).then_inc(*did("act", "F", "e2"))
                    act.activation(rt[0:1, 45:46], rt[0:1, 36:37], ACT.Exp).then_inc(*did("act", "F", "e3"))
                    act.wait_ge(*of("dve", "F", "wscaled"))
                    act.activation(Wsel[:, :, 0], Wst, ACT.Copy).then_inc(*did("act", "F", "wsel_hi"))
                    act.wait_ge(*of("dve", "F", "qkscale"))
                    for w, n in enumerate("qk"):
                        for m in range(KD):
                            act.wait_ge(*of("pe", "F3", n, m))
                            if (n, m) != ("q", 0):
                                act.wait_ge(*of("dve", "F3", *(("qlo", 0) if (n, m) == ("q", 1) else ("qlo", 1) if m == 0 else ("klo", 0))))
                            act.activation(tmp, slot("F3", n, m), ACT.Identity, bias=bsel[:, 2 * w + m:2 * w + m + 1],
                                           scale=gcol[:, 4 + 2 * w + m:5 + 2 * w + m]).then_inc(*frees("act", "F3", n, m))
                    act.wait_ge(*of("dve", "F3", "ones"))
                    for t in range(NT):
                        act.wait_ge(*of("pe", "F3", "v", t))
                        act.activation(VP4[:, t, :, 0:DS], slot("F3", "v", t)[:, 0:D].rearrange("p (h d) -> p h d", d=DS), ACT.Copy,
                                       scale=1.0 / WS).then_inc(*did("act", "F3", "vp", t))
                        led.freed[("F3", "v", t)] = ("act", ("F3", "vp", t))
                    act.wait_ge(*of("pe", "F3", "v", NT - 1))
                    n = 0
                    for step in last_attention_steps():
                        if step[0] == "ST":
                            _, h, kt = step
                            act.wait_ge(*of("pe", "F3", "ST", h, kt))
                            if n >= NP:
                                act.wait_ge(*of("pe", "F3", "PV", (n - NP) // NT, (n - NP) % NT, 1))
                            act.activation(PR4[:, n % NP], slot("F3", "ST", h, kt), ACT.Exp).then_inc(*did("act", "F3", "exp", h, kt))
                            led.freed[("F3", "ST", h, kt)] = ("act", ("F3", "exp", h, kt))
                            n += 1
                        elif step[0] == "PV" and step[2:] == (NT - 1, 1):
                            h = step[1]
                            act.wait_ge(*of("pe", "F3", "PV", h, NT - 1, 1))
                            if h >= 2:
                                act.wait_ge(*of("dve", "F3", "onf", h - 2))
                            for c in range(2):
                                act.activation(OT4[h % 2][:, c * CH:(c + 1) * CH], slot("F3", "PVacc", h, c)[0:TX], ACT.Copy
                                               ).then_inc(*did("act", "F3", "ot", h, c))
                                led.freed[("F3", "PVacc", h, c)] = ("act", ("F3", "ot", h, c))
                batch_end(act, "act")

        @block.gpsimd
        def _(pool):
            pool.memset(onesf[:], 1.0).then_inc(once["pool"], 1)
            pool.memset(VX[:], 0.0).then_inc(once["pool"], 1)
            pool.memset(mpart[:], -3.0e38).then_inc(once["pool"], 1)
            pool.wait_ge(once["pool"], 3)
            pool.memset(VX[0:TX, :, :, DH:QUARTER], 1.0).then_inc(once["pool"], 1)
            pool.wait_ge(once["low_w"], 32)
            pool.tensor_copy(low_down.rearrange("p k (m c) -> p (k m) c", c=P), identf[:].unsqueeze(1).broadcast_to([P, NM, P])).then_inc(once["pool"], 1)
            pool.wait_ge(once["pool"], 5)
            for i in range(LOW):
                pool.wait_ge(once["ring_down"], i + 1)
                butterfly(pool, once["down"], low_down, low_down_t, ring_down[:, i % 2], LOW - 1 - i, i, True)
            batch_end(pool, "pool")
            with pool.Fori(0, NB):
                batch_end(pool, "pool")

        @block.vector
        def _(dve):
            count = 0

            def then(ins, complete=True):
                nonlocal count
                ins.then_inc(once["dve"], 1)
                count += 1
                if complete:
                    dve.wait_ge(once["dve"], count)

            def low_stage(i):
                dve.wait_ge(once["ring_up"], i + 1)
                butterfly(dve, once["up"], low_up, low_up_t, ring_up[:, i % 2], i, i, False)

            n_high = 0

            def high_stage(rows, e, s, turned, first):
                nonlocal n_high
                d = 2 ** s
                pairs = [(q // d * 2 * d + q % d, q // d * 2 * d + q % d + d) for q in range(NM // 2)]
                w = high_w[:, e, s]
                n = rows.shape[2]
                if not first:
                    dve.wait_ge(once["high"], n_high)
                for q, (a, b_) in enumerate(pairs):
                    dve.tensor_scalar(high_t[:, 0, q, 0:n], rows[:, a], w[:, q, 0:1], None, ALU.mult).then_inc(once["high"], 1)
                    c = 1 if turned else 2
                    dve.tensor_scalar(high_t[:, 1, q, 0:n], rows[:, a], w[:, q, c:c + 1], None, ALU.mult).then_inc(once["high"], 1)
                dve.wait_ge(once["high"], n_high + 8)
                for q, (a, b_) in enumerate(pairs):
                    c = 2 if turned else 1
                    dve.scalar_tensor_tensor(rows[:, a], rows[:, b_], w[:, q, c:c + 1], high_t[:, 0, q, 0:n], ALU.mult, ALU.add).then_inc(once["high"], 1)
                n_high += 12
                dve.wait_ge(once["high"], n_high)
                for q, (a, b_) in enumerate(pairs):
                    dve.scalar_tensor_tensor(rows[:, b_], rows[:, b_], w[:, q, 3:4], high_t[:, 1, q, 0:n], ALU.mult, ALU.add).then_inc(once["high"], 1)
                n_high += 4

            dve.wait_ge(once["low_w"], 32)
            then(dve.tensor_copy(low_up.rearrange("p k (m c) -> p (k m) c", c=P), identf[:].unsqueeze(1).broadcast_to([P, NM, P])))
            low_stage(0)
            low_stage(1)
            dve.wait_ge(once["load"], 16 * N_LOADS)
            pr = lamr[:, 4 * P:6 * P].rearrange("p (a c) -> p a c", a=2)
            q_k = lamr[:, 0:4 * P].rearrange("p (a b c) -> p a b c", a=2, b=2)
            then(dve.tensor_tensor(pr, q_k[:, :, 0], q_k[:, :, 1], ALU.mult))
            dve.tensor_reduce(lamt[:, 0:2], pr, AX, ALU.add).then_inc(once["lambda"], 1)
            for w in range(len(CTXW)):
                if w >= 4:
                    dve.wait_ge(once[f"store{w % 4}"], 16)
                src = stage_flat[:, (len(FLAT) + w) * FLAT_N:(len(FLAT) + w + 1) * FLAT_N]
                dst = ctx_split[:, (w % 4) * 2 * FLAT_N:(w % 4 + 1) * 2 * FLAT_N]
                then(dve.tensor_scalar(dst[:, 0:FLAT_N], src, WS, None, ALU.mult))
                dve.scalar_tensor_tensor(dst[:, FLAT_N:2 * FLAT_N], src, WS, dst[:, 0:FLAT_N], ALU.mult, ALU.subtract).then_inc(once["ctxw"], 1)
                if w in (3, 7):
                    low_stage(2 + w // 4)
            dve.wait_ge(once["act"], 1)
            then(dve.scalar_tensor_tensor(Wf[:, :, 1].rearrange("p w k d -> p w (k d)"),
                                          stage_flat[:, 0:len(FLAT) * FLAT_N].rearrange("p (w n) -> p w n", n=FLAT_N), WS,
                                          Wf[:, :, 0].rearrange("p w k d -> p w (k d)"), ALU.mult, ALU.subtract))
            low_stage(4)
            dve.wait_ge(once["act"], 2)
            then(dve.scalar_tensor_tensor(Wp[:, :, 1].rearrange("p w k d -> p w (k d)"), stage_pad.rearrange("p (w n) -> p w n", n=PAD_N), WS,
                                          Wp[:, :, 0].rearrange("p w k d -> p w (k d)"), ALU.mult, ALU.subtract))
            then(dve.memset(BR[:], 0.0))
            nb = len(BROW)
            then(dve.tensor_scalar(BR[0:nb, 0], brf[0:nb], WS, None, ALU.mult))
            then(dve.scalar_tensor_tensor(BR[0:nb, 1], brf[0:nb], WS, BR[0:nb, 0], ALU.mult, ALU.subtract))
            dve.memset(rt[0:1, 95:96], 0.0).then_inc(once["staged"], 1)
            high_stage(rows_c, 1, 2, True, True)
            low_stage(5)
            high_stage(rows_c, 1, 1, True, False)
            dve.tensor_reduce(wsc[:, 0:1], fW1, AX, ALU.add, apply_absolute_value=True).then_inc(once["wsum"], 1)
            dve.tensor_reduce(wsc[:, 1:2], fW2, AX, ALU.add, apply_absolute_value=True).then_inc(once["wsum"], 1)
            low_stage(6)
            high_stage(rows_c, 1, 0, True, False)
            gw = gwf[:, :].rearrange("p (k n) -> p k n", k=KD)
            then(dve.tensor_scalar(gateW[:, 0], gw, WS, None, ALU.mult))
            then(dve.scalar_tensor_tensor(gateW[:, 1], gw, WS, gateW[:, 0], ALU.mult, ALU.subtract))
            for n in ("B0q", "D2q", "E3q"):
                then(dve.tensor_scalar(BC[:, bc[n]:bc[n] + 2], BC[:, bc[n]:bc[n] + 2], 0.25, None, ALU.mult))
            then(dve.tensor_scalar(big[:], ident[:], BIG, None, ALU.mult))
            then(dve.tensor_scalar(small[:], ident[:], 1.0 / WS, None, ALU.mult))
            dve.wait_ge(once["act"], 3)
            then(dve.tensor_tensor(lamt[:, 4:5], lamt[:, 3:4], lamt[:, 2:3], ALU.subtract))
            then(dve.tensor_scalar(lamt[:, 5:6], lamt[:, 4:5], -LAM0, None, ALU.add))

            dve.wait_ge(once["pe"], 1)
            then(dve.tensor_scalar(wsc[:, 2:4], SLOT["S0"][:, 0:2], 1.0 / (HID * D), EPS, ALU.mult, ALU.max))
            then(dve.reciprocal(wsc[:, 4:6], wsc[:, 2:4]))
            for i, (f, w) in enumerate(((fW1, Wq1[:, :, :].rearrange("p k n -> p (k n)")), (fW2, Wq2[:, :, :].rearrange("p k n -> p (k n)")))):
                then(dve.tensor_scalar(f, f, wsc[:, 4 + i:5 + i], MAGIC, ALU.mult, ALU.add))
                then(dve.tensor_scalar(f, f, -MAGIC, 1.0, ALU.add, ALU.min))
                then(dve.tensor_scalar(w, f, -1.0, None, ALU.max))
            dve.tensor_scalar(wsc[:, 2:4], wsc[:, 2:4], 1.0 / QB, None, ALU.mult).then_inc(once["ternary"], 1)
            dve.wait_ge(once["act"], 4)
            dve.memset(rt[0:1, 95:96], 0.0).then_inc(once["high"], 1)
            n_high += 1
            for s in range(HIGH):
                high_stage(rows_e, 0, s, False, False)
            dve.wait_ge(once["high"], n_high)
            then(dve.tensor_tensor(upb[:], rows_e[:, :, D], BC[:, BC_UP:BC_UP + NM], ALU.add))
            dve.wait_ge(once["pe"], 4)
            then(dve.tensor_copy(Wexp[:].rearrange("p k n -> p (k n)"), flat[:, 2 * HID:4 * HID]))
            batch_end(dve, "dve")

            with dve.Fori(0, NB):
                def step(*key):
                    return did("dve", *key)

                begun = set()

                def statistics(N, src, t, written):
                    begun.add(N)
                    if t >= 0:
                        dve.wait_ge(*of("dve", *written, t))
                        if N:
                            dve.bn_stats(stats[:, t], src[:, t]).then_inc(*step(N, "bn", t))

                def norm(N, src, dst):
                    if N not in begun:
                        for t in range(NT):
                            dve.bn_stats(stats[:, t], src[:, t]).then_inc(*step(N, "bn", t))
                    for t in range(NT):
                        dve.wait_ge(*of("dve", N, "bn", t))
                        dve.bn_aggr(mv[:, t], stats[:, t]).then_inc(*(step(N, "mv") if t == NT - 1 else step(N, "ag", t)))
                    dve.wait_ge(*of("act", N, "sd"))
                    dve.reciprocal(rstd[:], sd[:]).then_inc(*step(N, "rstd"))
                    dve.wait_ge(*of("dve", N, "rstd"))
                    for t in range(NT):
                        dve.tensor_scalar(dst[:, t], src[:, t], mv[:, t, 0:1], rstd[:, t:t + 1], ALU.subtract, ALU.mult).then_inc(*step(N, "xn", t))

                def x_lo(N):
                    for k in range(KD):
                        dve.wait_ge(*of("act", N, "xhi", k))
                        if N == "F":
                            dve.tensor_reduce(xmean[:, k:k + 1], slot("T", N, k), AX, ALU.add).then_inc(*step(N, "xmean", k))
                        dve.tensor_tensor(XT[:, 1, k], slot("T", N, k), XT[:, 0, k], ALU.subtract).then_inc(*step(N, "xlo", k))
                        led.freed[("T", N, k)] = ("dve", (N, "xlo", k))

                def halves(src, hi, lo, ready, key):
                    dve.wait_ge(*ready)
                    dve.tensor_copy(hi, src).then_inc(*step(*key, "hi"))
                    dve.wait_ge(*of("dve", *key, "hi"))
                    dve.tensor_tensor(lo, src, hi, ALU.subtract).then_inc(*step(*key))

                def x_affine(N):
                    for k in range(KD):
                        halves(tmp, XT[:, 0, k], XT[:, 1, k], of("act", "free", "T", N, k), (N, "xlo", k))

                dve.tensor_scalar(maskb[:, :, 0:TC], maskr[:, 0:TC].unsqueeze(1).broadcast_to([1, NH, TC]), 0.0, -BIG, ALU.is_gt, ALU.mult).then_inc(*step("mask"))
                if "A" in stages:
                    norm("A", H, XN["A"])
                dve.wait_ge(*of("act", "cthi"))
                dve.tensor_tensor(CT[:, 1, :, 0:TC], CTf[:], CT[:, 0, :, 0:TC], ALU.subtract).then_inc(*step("ctlo"))
                if "A" in stages:
                    x_lo("A")
                dve.wait_ge(*of("act", "kp0hi"))
                dve.scalar_tensor_tensor(KP0[:, 1, 0:TC], slot("K0")[:, 0:TC], 1.0 / WS, KP0[:, 0, 0:TC], ALU.mult, ALU.subtract).then_inc(*step("A", "kp0"))
                led.freed[("K0",)] = ("dve", ("A", "kp0"))
                dve.wait_ge(*of("act", "vp0hi"))
                dve.scalar_tensor_tensor(VP0[0:TC, 1], slot("V0")[0:TC, 0:D], 1.0 / WS, VP0[0:TC, 0], ALU.mult, ALU.subtract).then_inc(*step("A", "vp0"))
                led.freed[("V0",)] = ("dve", ("A", "vp0"))
                dve.wait_ge(*of("act", "free", "KX", len(XL) - 1, KD - 1))
                for s in range(2):
                    if s:
                        dve.wait_ge(*of("dve", "kxhi"))
                        dve.tensor_tensor(kxs[:, 1, :, :, 0:TC], kxf[:, :, :, 0:TC], kxs[:, 0, :, :, 0:TC], ALU.subtract).then_inc(*step("kxs"))
                    else:
                        dve.tensor_copy(kxs[:, 0, :, :, 0:TC], kxf[:, :, :, 0:TC]).then_inc(*step("kxhi"))
                if "A" not in stages:
                    dve.wait_ge(*of("ld_kx", "mask"))
                    dve.tensor_copy(X[:], H[:]).then_inc(*step("debug"))
                    dve.wait_ge(*of("dve", "debug"))

                if "A" in stages:
                    for h in range(2):
                        dve.wait_ge(*of("act", "A", "qhi", h))
                        dve.scalar_tensor_tensor(q0[:, 1, h], slot("A", "Q", h), float(P) ** -0.5 / WS, q0[:, 0, h], ALU.mult,
                                                 ALU.subtract).then_inc(*step("A", "qlo", h))
                        led.freed[("A", "Q", h)] = ("dve", ("A", "qlo", h))
                    for t in range(NT + 1):
                        if t < NT:
                            dve.wait_ge(*of("pe", "A", "S", t))
                            dve.tensor_reduce(sm[:, 2 * t:2 * t + 2], slot("A", "S", t)[:, 0:2 * TC].rearrange("p (h c) -> p h c", h=2), AX, ALU.max,
                                              negate=True).then_inc(*step("A", "m", t))
                        if t:
                            u = t - 1
                            dve.wait_ge(*of("act", "free", "A", "S", u))
                            dve.reciprocal(sm[:, 32 + 2 * u:34 + 2 * u], sm[:, 16 + 2 * u:18 + 2 * u]).then_inc(*step("A", "r", u))
                            dve.wait_ge(*of("dve", "A", "r", u))
                            dve.tensor_tensor(sm[:, 48 + u:49 + u], sm[:, 33 + 2 * u:34 + 2 * u], lamt[:, 5:6], ALU.mult).then_inc(*step("A", "r1", u))
                            dve.wait_ge(*of("dve", "A", "r1", u))
                            dve.tensor_scalar(A0[:, u], E0[:, u % 2, 1], sm[:, 48 + u:49 + u], None, ALU.mult).then_inc(*step("A", "p1", u))
                            dve.wait_ge(*of("dve", "A", "p1", u))
                            dve.scalar_tensor_tensor(A0[:, u], E0[:, u % 2, 0], sm[:, 32 + 2 * u:33 + 2 * u], A0[:, u], ALU.mult,
                                                     ALU.add).then_inc(*step("A", "p", u))
                    dve.wait_ge(*of("act", "A", "pthi"))
                    dve.tensor_tensor(AT0[0:TC, 1], slot("A", "PT")[0:TC], AT0[0:TC, 0], ALU.subtract).then_inc(*step("A", "ptlo"))
                    led.freed[("A", "PT")] = ("dve", ("A", "ptlo"))
                    for m in range(KD):
                        dve.wait_ge(*of("act", "A", "ohi", m))
                        dve.tensor_tensor(AO0[:, 1, m], slot("A", "O", m), AO0[:, 0, m], ALU.subtract).then_inc(*step("A", "olo", m))
                        led.freed[("A", "O", m)] = ("dve", ("A", "olo", m))
                    dve.wait_ge(*of("act", "A", "rms"))
                    dve.reciprocal(sm[:, 120:128], sm[:, 72:80]).then_inc(*step("A", "rr"))
                    dve.wait_ge(*of("dve", "A", "rr"))
                    dve.tensor_scalar(sm[:, 128:136], sm[:, 120:128], (1.0 - LAM0) / WS, None, ALU.mult).then_inc(*step("A", "rw"))
                    dve.wait_ge(*of("dve", "A", "rw"))
                    for t in range(NT):
                        dve.wait_ge(*of("pe", "A", "W", t))
                        dve.scalar_tensor_tensor(X[:, t], slot("A", "W", t)[:, 0:D], sm[:, 128 + t:129 + t], H[:, t], ALU.mult,
                                                 ALU.add).then_inc(*step("A", "x", t))
                        led.freed[("A", "W", t)] = ("dve", ("A", "x", t))
                        statistics("B1", X, t - 1, ("A", "x"))
                    statistics("B1", X, NT - 1, ("A", "x"))

                def maxima(L, own, step_):
                    g, t = step_[1:3]
                    last = None
                    if own:
                        j = step_[3]
                        for c in range(((t + 1) * P + CH - 1) // CH):
                            n = min(CH, (t + 1) * P - c * CH)
                            dve.wait_ge(*of("pe", L, "S", g, t, j, c))
                            dve.tensor_reduce(mpart[:, j * NT + t, c:c + 1], slot(L, "S", g, t, j, c)[:, 0:n], AX,
                                              ALU.max).then_inc(*frees("dve", L, "S", g, t, j, c))
                            last = (L, "S", g, t, j, c)
                    else:
                        dve.wait_ge(*of("pe", L, "S", g, t))
                        mine = negp[g // 2][:, (g % 2) * GH * NT:(g % 2 + 1) * GH * NT]
                        dve.tensor_reduce(mine.rearrange("p (j t) -> p j t", t=NT)[:, :, t],
                                          slot(L, "S", g, t)[:, 0:GH * TX].rearrange("p (j c) -> p j c", c=TX), AX, ALU.max,
                                          negate=True).then_inc(*frees("dve", L, "S", g, t))
                        last = (L, "S", g, t)
                    return last

                def minus_max_rows(L, g, last, n):
                    if n:
                        dve.wait_ge(*of("dve", "free", *last))
                        dve.tensor_reduce(negm[:, g % 2, 0:n], mpart[:, 0:n], AX, ALU.max, negate=True).then_inc(*step(L, "negm", g))

                def minus_max_parts(L, g, n):
                    dve.wait_ge(*of("pe", L, "MT", g))
                    if g >= 2:
                        dve.wait_ge(*of(f"ld_m{g % 2}", L, g - 2, 1))
                    dve.tensor_copy(mrow[0:n, g % 2, 0], slot(L, "MT", g)[0:n, 0:P]).then_inc(*step(L, "mhi", g))
                    dve.wait_ge(*of("dve", L, "mhi", g))
                    dve.tensor_tensor(mrow[0:n, g % 2, 1], slot(L, "MT", g)[0:n, 0:P], mrow[0:n, g % 2, 0], ALU.subtract).then_inc(*step(L, "mrow", g))
                    led.freed[(L, "MT", g)] = ("dve", (L, "mrow", g))

                def inverse_sums(L, g, w):
                    dve.wait_ge(*of(f"ld_s{g}", L))
                    dve.reciprocal(rinv[:, g, 0:w], rsum[:, g, 0:w]).then_inc(*step(L, "rinv", g))

                def normalised(L, own, g):
                    dve.wait_ge(*of("pe", L, "NB", g))
                    dve.tensor_tensor(tmp, OT[own][g], slot(L, "NB", g), ALU.mult).then_inc(*step(L, "onf", g))
                    led.freed[(L, "NB", g)] = ("dve", (L, "onf", g))
                    halves(tmp, ON[:, 0, g], ON[:, 1, g], of("dve", L, "onf", g), (L, "onlo", g))
                    dve.wait_ge(*of("dve", L, "onlo", g))

                def attention(L, own, dst, follows):
                    for m in range(KD):
                        halves(tmp, qhl[:, 0, m], qhl[:, 1, m], of("act", "free", L, "q", m), (L, "qlo", m))
                    if own:
                        for m in range(KD):
                            halves(tmp, khl[:, 0, m], khl[:, 1, m], of("act", "free", L, "k", m), (L, "klo", m))
                        dve.memset(VP[:, :, :, DH:QUARTER], 1.0).then_inc(*step(L, "ones"))
                    steps = attention_steps(own)
                    last = None
                    for i, s in enumerate(steps):
                        if s[0] == "S":
                            last = maxima(L, own, s)
                        elif s[0] == "MT":
                            minus_max_rows(L, s[1], last, GH * NT if own else 0)
                            minus_max_parts(L, s[1], GH * NT if own else 2 * GH * NT)
                        elif s[0] == "ST" and own and s[1] and s[2:] == (2, 0):
                            inverse_sums(L, s[1] - 1, QUARTER)
                        elif s[0] == "PV" and not own and s[1] and s[3] == 0:
                            inverse_sums(L, s[1] - 1, QUARTER)
                        elif s[0] == "NB":
                            if s[1] == NG - 1:
                                inverse_sums(L, NG - 1, QUARTER)
                            normalised(L, own, s[1])
                    residual(L, dst, follows)

                def residual(L, dst, follows):
                    begun.add(follows)

                    def pair_statistics(p):
                        dve.wait_ge(*of("dve", L, "x", p))
                        for t in (2 * p, 2 * p + 1):
                            if follows:
                                dve.bn_stats(stats[:, t], dst[:, t]).then_inc(*step(follows, "bn", t))

                    for p in range(NT // 2):
                        dve.wait_ge(*of("pe", L, "W", p))
                        pair = dst[:, 2 * p:2 * p + 2].rearrange("p t d -> p (t d)")
                        dve.scalar_tensor_tensor(pair, slot(L, "W", p), 1.0 / WS, pair, ALU.mult, ALU.add).then_inc(*step(L, "x", p))
                        led.freed[(L, "W", p)] = ("dve", (L, "x", p))
                        if p:
                            pair_statistics(p - 1)
                    pair_statistics(NT // 2 - 1)

                if "B" in stages:
                    dve.wait_ge(*of("ld_kx", "mask"))
                    norm("B1", X, H)
                    dve.wait_ge(*of("dve", "B1", "xn", NT - 1))
                    norm("B", H, XN["B"])
                    x_affine("B")
                    attention("B0", True, H, "M")

                if "M" in stages:
                    norm("M", H, XN["M"])

                    def weights_lo(e, w):
                        dve.wait_ge(*of("act", "M", "whi", e, w))
                        dve.scalar_tensor_tensor(Wm[e % 2][:, w, 1], WSt[:, w], WS, Wm[e % 2][:, w, 0], ALU.mult, ALU.subtract).then_inc(*step("M", "wlo", e, w))

                    weights_lo(0, 0)
                    x_affine("M")
                    weights_lo(0, 1)
                    dve.wait_ge(*of("pe", "M", "gate"))
                    lg = sm[:, 0:64].rearrange("p (t e) -> p t e", e=NE)
                    dve.scalar_tensor_tensor(lg, slot("M", "gate")[:, 0:NT * NE].rearrange("p (t e) -> p t e", e=NE), 1.0 / WS,
                                             gateb[:].unsqueeze(1).broadcast_to([P, NT, NE]), ALU.mult, ALU.add).then_inc(*frees("dve", "M", "gate"))
                    dve.wait_ge(*of("dve", "free", "M", "gate"))
                    for t in range(NT):
                        dve.max(maxv[:, t], lg[:, t]).then_inc(*step("M", "top", t))
                    for t in range(NT):
                        dve.wait_ge(*of("dve", "M", "top", t))
                        dve.max_index(maxi[:, t], maxv[:, t], lg[:, t]).then_inc(*step("M", "idx", t))
                    dve.tensor_tensor(sm[:, 80:88], maxv[:, :, 1], maxv[:, :, 0], ALU.subtract).then_inc(*step("M", "d"))
                    dve.wait_ge(*of("act", "M", "e"))
                    dve.tensor_scalar(sm[:, 96:104], sm[:, 88:96], WS, WS, ALU.mult, ALU.add).then_inc(*step("M", "den"))
                    dve.wait_ge(*of("dve", "M", "den"))
                    dve.reciprocal(sm[:, 104:112], sm[:, 96:104]).then_inc(*step("M", "w1"))
                    dve.wait_ge(*of("dve", "M", "w1"))
                    dve.tensor_tensor(sm[:, 112:120], sm[:, 88:96], sm[:, 104:112], ALU.mult).then_inc(*step("M", "w2"))
                    dve.tensor_copy(sm[:, 64:80].rearrange("p (t i) -> p t i", i=2), maxi[:, :, 0:2]).then_inc(*step("M", "idxf"))
                    dve.wait_ge(*of("dve", "M", "idxf"))
                    io = iota[:].unsqueeze(1).broadcast_to([P, NT, NE])
                    ix = sm[:, 64:80].rearrange("p (t i) -> p t i", i=2)
                    for i, dst in enumerate((wfull[:], lg)):
                        dve.tensor_tensor(dst, io, ix[:, :, i:i + 1].broadcast_to([P, NT, NE]), ALU.is_equal).then_inc(*step("M", "eq", i))
                        dve.wait_ge(*of("dve", "M", "eq", i))
                        dve.tensor_tensor(dst, dst, sm[:, 104 + 8 * i:112 + 8 * i].unsqueeze(2).broadcast_to([P, NT, NE]), ALU.mult).then_inc(*step("M", "wm", i))
                        dve.wait_ge(*of("dve", "M", "wm", i))
                    dve.tensor_tensor(wfull[:], wfull[:], lg, ALU.add).then_inc(*step("M", "wfull"))
                    dve.wait_ge(*of("dve", "M", "wfull"))

                    def expert_out(e, c):
                        for i in range(4):
                            dve.wait_ge(*of("pe", "M", "D", e, c, NM - 1))
                            t = 4 * c + i
                            if e:
                                dve.wait_ge(*of("dve", "M", "h", e - 1, t))
                            key = ("M", "h", e, t)
                            dve.scalar_tensor_tensor(H[:, t], slot("M", "D", e, c, i // 2)[:, (i % 2) * D:(i % 2 + 1) * D], wfull[:, t, e:e + 1],
                                                     H[:, t], ALU.mult, ALU.add).then_inc(*step(*key))
                            if i % 2:
                                led.freed[("M", "D", e, c, i // 2)] = ("dve", key)

                    n = 0
                    for e in range(NE):
                        for c in range(2):
                            for m in range(NM):
                                if n >= 4:
                                    dve.wait_ge(*of("pe", "M", "D", *back(e, c, m, 4)))
                                halves(midf[:, n % 3], mid[:, n % 4, 0], mid[:, n % 4, 1], of("act", "free", "M", "U", e, c, m), ("M", "midlo", e, c, m))
                                n += 1
                                if e + 1 < NE and (c, m) in ((0, 5), (1, 1)):
                                    weights_lo(e + 1, c)
                                if m == 3 and (e, c) != (0, 0):
                                    expert_out(*back(e, c, 0, 1)[:2])
                    expert_out(NE - 1, 1)
                    for t in range(NT):
                        dve.wait_ge(*of("dve", "M", "h", NE - 1, t))
                        dve.tensor_tensor(X[:, t], X[:, t], H[:, t], ALU.add).then_inc(*step("M", "x", t))
                        statistics("C", X, t - 1, ("M", "x"))
                    statistics("C", X, NT - 1, ("M", "x"))

                if "C" in stages:
                    norm("C", X, XN["C"])
                    x_lo("C")
                    attention("C1", False, X, "L1")

                if "L1" in stages:
                    norm("L1", X, XN["L1"])
                    dve.wait_ge(*of("dve", "L1", "xn", NT - 1))
                    dve.tensor_reduce(sm[:, 0:8], XN["L1"], AX, ALU.max, apply_absolute_value=True).then_inc(*step("L1", "amax"))
                    dve.wait_ge(*of("dve", "L1", "amax"))
                    dve.tensor_scalar(sm[:, 0:8], sm[:, 0:8], EPS, None, ALU.max).then_inc(*step("L1", "xs"))
                    dve.wait_ge(*of("dve", "L1", "xs"))
                    dve.reciprocal(sm[:, 8:16], sm[:, 0:8]).then_inc(*step("L1", "xr"))
                    dve.wait_ge(*of("dve", "L1", "xr"))
                    dve.tensor_scalar(sm[:, 16:24], sm[:, 8:16], QB, None, ALU.mult).then_inc(*step("L1", "xm"))
                    dve.tensor_scalar(sm[:, 24:32], sm[:, 0:8], wsc[:, 2:3], None, ALU.mult).then_inc(*step("L1", "xsc"))
                    dve.wait_ge(*of("dve", "L1", "xsc"))
                    for t in range(NT):
                        dve.tensor_scalar(XN["L1"][:, t], XN["L1"][:, t], sm[:, 16 + t:17 + t], MAGIC, ALU.mult, ALU.add).then_inc(*step("L1", "xr1", t))
                    for t in range(NT):
                        dve.wait_ge(*of("dve", "L1", "xr1", t))
                        dve.tensor_scalar(XN["L1"][:, t], XN["L1"][:, t], -MAGIC, QB, ALU.add, ALU.min).then_inc(*step("L1", "xr2", t))
                    for t in range(NT):
                        dve.wait_ge(*of("dve", "L1", "xr2", t))
                        dve.tensor_scalar(xq[:, t], XN["L1"][:, t], -QB - 1.0, None, ALU.max).then_inc(*step("L1", "xq", t))
                    dve.wait_ge(*of("ld_b12", 1))

                    def hidden(t):
                        dve.wait_ge(*of("pe", "L1", "H1", t))
                        if t >= 3:
                            dve.wait_ge(*of("dve", "L1", "hr1", t - 3))
                        dve.scalar_tensor_tensor(hb[:, t % 3], slot("L1", "H1", t), sm[:, 24 + t:25 + t], b1b, ALU.mult, ALU.add).then_inc(*step("L1", "h", t))
                        led.freed[("L1", "H1", t)] = ("dve", ("L1", "h", t))

                    def quantise(t):
                        a, b_, c_ = 32 + t, 40 + t, 48 + t
                        dve.wait_ge(*of("act", "L1", "gelu", t))
                        dve.tensor_reduce(sm[:, a:a + 1], hb[:, t % 3], AX, ALU.max, apply_absolute_value=True).then_inc(*step("L1", "ha", t))
                        dve.wait_ge(*of("dve", "L1", "ha", t))
                        dve.tensor_scalar(sm[:, a:a + 1], sm[:, a:a + 1], EPS, None, ALU.max).then_inc(*step("L1", "hs", t))
                        dve.wait_ge(*of("dve", "L1", "hs", t))
                        dve.reciprocal(sm[:, b_:b_ + 1], sm[:, a:a + 1]).then_inc(*step("L1", "hrc", t))
                        dve.tensor_scalar(sm[:, c_:c_ + 1], sm[:, a:a + 1], wsc[:, 3:4], None, ALU.mult).then_inc(*step("L1", "hsc", t))
                        dve.wait_ge(*of("dve", "L1", "hrc", t))
                        dve.tensor_scalar(sm[:, 56 + t:57 + t], sm[:, b_:b_ + 1], QB, None, ALU.mult).then_inc(*step("L1", "hm", t))
                        dve.wait_ge(*of("dve", "L1", "hm", t))
                        if t >= 2:
                            dve.wait_ge(*of("dve", "L1", "hq", t - 2))
                            dve.wait_ge(*of("pe", "L1", "HQ", t - 2))
                        dve.tensor_scalar(hr[:, t % 2], hb[:, t % 3], sm[:, 56 + t:57 + t], MAGIC, ALU.mult, ALU.add).then_inc(*step("L1", "hr1", t))
                        dve.wait_ge(*of("dve", "L1", "hr1", t))
                        dve.tensor_scalar(hr[:, t % 2], hr[:, t % 2], MAGIC - QB - 1.0, MAGIC + QB, ALU.max, ALU.min).then_inc(*step("L1", "hr2", t))
                        dve.wait_ge(*of("dve", "L1", "hr2", t))
                        dve.tensor_scalar(hq[:, t % 2], hr[:, t % 2], -MAGIC, None, ALU.add).then_inc(*step("L1", "hq", t))

                    def ternary_out(t):
                        dve.wait_ge(*of("pe", "L1", "H2", t))
                        dve.scalar_tensor_tensor(X[:, t], slot("L1", "H2", t)[:, 0:D], sm[:, 48 + t:49 + t], X[:, t], ALU.mult, ALU.add).then_inc(*step("L1", "x1", t))
                        led.freed[("L1", "H2", t)] = ("dve", ("L1", "x1", t))
                        dve.wait_ge(*of("dve", "L1", "x1", t))
                        dve.tensor_tensor(X[:, t], X[:, t], b2b, ALU.add).then_inc(*step("L1", "x", t))
                        statistics("D", X, t, ("L1", "x"))

                    hidden(0)
                    for t in range(NT):
                        if t + 1 < NT:
                            hidden(t + 1)
                        quantise(t)
                        if t:
                            ternary_out(t - 1)
                    ternary_out(NT - 1)

                if "D" in stages:
                    norm("D", X, XN["D"])
                    x_lo("D")
                    attention("D2", False, X, "L2")

                if "L2" in stages:
                    norm("L2", X, XN["L2"])
                    for t in range(NT):
                        dve.wait_ge(*of("pe", "L2", "Y", t))
                        dve.tensor_tensor(X[:, t], X[:, t], slot("L2", "Y", t)[:, 0:D], ALU.add).then_inc(*step("L2", "x", t))
                        led.freed[("L2", "Y", t)] = ("dve", ("L2", "x", t))
                        statistics("E", X, t - 1, ("L2", "x"))
                    statistics("E", X, NT - 1, ("L2", "x"))

                if "E" in stages:
                    norm("E", X, XN["E"])
                    x_lo("E")
                    attention("E3", False, X, "F")

                if "F" in stages:
                    norm("F", X, XN["F"])
                    x_lo("F")

                    def small_step(key, ins):
                        ins.then_inc(*step("F", key))
                        dve.wait_ge(*of("dve", "F", key))

                    dve.wait_ge(*of("pe", "F", "R"))
                    small_step("lg", dve.scalar_tensor_tensor(rt[0:1, 0:NH], slot("F", "R")[0:1, 0:NH], 1.0 / T, F3br[:], ALU.mult, ALU.add))
                    led.freed[("F", "R")] = ("dve", ("F", "lg"))
                    small_step("l8", dve.max(rt[0:1, 16:24], rt[0:1, 0:NH]))
                    small_step("lmax", dve.tensor_scalar(rt[0:1, 24:25], rt[0:1, 16:17], -1.0, None, ALU.mult))
                    dve.wait_ge(*of("act", "F", "e1"))
                    small_step("r1", dve.reciprocal(rt[0:1, 26:27], rt[0:1, 25:26]))
                    small_step("dist", dve.tensor_scalar(rt[0:1, 64:80], rt[0:1, 0:NH], rt[0:1, 26:27], None, ALU.mult))
                    small_step("top", dve.max(rt[0:1, 28:36], rt[0:1, 64:80]))
                    small_step("neg", dve.tensor_scalar(rt[0:1, 36:37], rt[0:1, 28:29], -1.0, None, ALU.mult))
                    small_step("index", dve.max_index(rti[:], rt[0:1, 28:36], rt[0:1, 64:80]))
                    dve.wait_ge(*of("act", "F", "e3"))
                    small_step("den", dve.scalar_tensor_tensor(rt[0:1, 46:47], rt[0:1, 45:46], float(NH - HS), rt[0:1, 44:45], ALU.mult, ALU.add))
                    small_step("rden", dve.reciprocal(rt[0:1, 47:48], rt[0:1, 46:47]))
                    small_step("gates", dve.tensor_scalar(rt[0:1, 48:52], rt[0:1, 40:44], rt[0:1, 47:48], None, ALU.mult))
                    dve.wait_ge(*of("pe", "F", "G"))
                    small_step("gcol", dve.tensor_copy(gcol[:, 0:4], slot("F", "G")[:, 0:4]))
                    led.freed[("F", "G")] = ("dve", ("F", "gcol"))
                    for m in range(KD):
                        for i in range(2):
                            r = slice(DS * i, DS * (i + 1))
                            g_ = gcol[r, 2 * m + i:2 * m + i + 1]
                            small_step(("gq", m, i), dve.tensor_scalar(gcol[r, 4 + m:5 + m], g_, float(DS) ** -0.5 / WS, None, ALU.mult))
                            small_step(("gk", m, i), dve.tensor_scalar(gcol[r, 6 + m:7 + m], g_, 1.0 / WS, None, ALU.mult))
                    dve.wait_ge(*of("ld_sel", HS - 1, "bv"))
                    small_step("bs", dve.tensor_scalar(bsel[:], bsel[:], WS, None, ALU.mult))
                    small_step("qkscale", dve.tensor_tensor(bsel[:], bsel[:], gcol[:, 4:8], ALU.mult))
                    small_step("bv_hi", dve.tensor_scalar(bvh[:, 0], bvr[:], WS, None, ALU.mult))
                    small_step("bv_lo", dve.scalar_tensor_tensor(bvh[:, 1], bvr[:], WS, bvh[:, 0], ALU.mult, ALU.subtract))
                    small_step("wscaled", dve.tensor_scalar(Wst, Wst, WS, None, ALU.mult))
                    dve.wait_ge(*of("act", "F", "wsel_hi"))
                    dve.tensor_tensor(Wsel[:, :, 1], Wst, Wsel[:, :, 0], ALU.subtract).then_inc(*step("F", "wsel_lo"))
                    for n, hl in (("q", qhl), ("k", khl)):
                        for m in range(KD):
                            halves(tmp, hl[:, 0, m], hl[:, 1, m], of("act", "free", "F3", n, m), ("F3", n + "lo", m))
                    dve.memset(VP4[:, :, :, DS:TX], 1.0).then_inc(*step("F3", "ones"))
                    for s in last_attention_steps():
                        if s[0] == "S":
                            _, h, t, c = s
                            dve.wait_ge(*of("pe", "F3", "S", h, t, c))
                            dve.tensor_reduce(mpart[:, t, c:c + 1], slot("F3", "S", h, t, c), AX, ALU.max).then_inc(*frees("dve", "F3", "S", h, t, c))
                        elif s[0] == "MT":
                            h = s[1]
                            minus_max_rows("F3", h, ("F3", "S", h, NT - 1, 1), NT)
                            minus_max_parts("F3", h, NT)
                        elif s[0] == "ST" and s[1] and s[2] == 3:
                            inverse_sums("F3", s[1] - 1, NT)
                        elif s[0] == "NB":
                            h = s[1]
                            if h == HS - 1:
                                inverse_sums("F3", h, NT)
                            dve.wait_ge(*of("pe", "F3", "NB", h))
                            dve.scalar_tensor_tensor(tmp[0:TX], OT4[h % 2], gcol[0:TX, h:h + 1], slot("F3", "NB", h)[0:TX], ALU.mult,
                                                     ALU.mult).then_inc(*step("F3", "onf", h))
                            led.freed[("F3", "NB", h)] = ("dve", ("F3", "onf", h))
                            halves(tmp[0:TX], ON4[:, 0, h], ON4[:, 1, h], of("dve", "F3", "onf", h), ("F3", "onlo", h))
                            dve.wait_ge(*of("dve", "F3", "onlo", h))
                    dve.memset(mpart[:], -3.0e38).then_inc(*step("F3", "mpart"))
                    residual("F3", X, None)
                dve.memset(rt[0:1, 95:96], 0.0).then_inc(*step("final"))
                batch_end(dve, "dve")
        return led


def halves_of(w):
    return w.reshape(KD, P, -1).transpose(1, 0, 2).reshape(P, -1)


def by_heads(w, heads, width, tall, groups):
    out = np.zeros((heads, tall, w.shape[1]), np.float32)
    out[:, :width] = w.reshape(heads, width, -1)
    return out.reshape(groups, -1, w.shape[1])


def with_next(a):
    return np.concatenate([a, a[:1]])


def layouts(i):
    f = {k: np.asarray(v) for k, v in i.items()}
    z = np.zeros
    pad_k = z((D, D), np.float32)
    pad_k[:, :P] = f["L0_xattn_Wk"].T
    mats = {"A0q": f["L0_xattn_Wq"].T, "A0o": f["L0_xattn_Wo"].T, "A0k": pad_k, "A0v": f["L0_xattn_Wv"].T,
            "B0q": f["L0_ffn_Wq"], "B0k": f["L0_ffn_Wk"], "B0v": f["L0_ffn_Wv"],
            "C1q": f["L1_xattn_Wq"].T, "C1k": f["L1_xattn_Wk"].T, "C1v": f["L1_xattn_Wv"].T,
            "D2q": f["L2_xattn_Wq"].T, "D2k": f["L2_xattn_Wk"].T, "D2v": f["L2_xattn_Wv"].T,
            "E3q": f["L3_xattn_q_w"].T, "E3k": f["L3_xattn_k_w"].T, "E3v": f["L3_xattn_v_w"].T}
    padded = {"B0p": f["L0_ffn_Wp"], "C1o": f["L1_xattn_Wo"].T, "D2o": f["L2_xattn_Wo"].T, "E3id": np.eye(D, dtype=np.float32)}
    pads = [by_heads(padded[n], NH, DH, QUARTER, NG) for n in PADDED[:-1]]
    pads.append(by_heads(f["L3_ffn_Wo"], HS, DS, P, HS))
    rows = {"B0v": f["L0_ffn_bv"], "B0p": f["L0_ffn_bp"], "C1o": f["L1_xattn_bo"], "D2v": f["L2_xattn_bv"], "D2o": f["L2_xattn_bo"],
            "E3v": f["L3_xattn_v_b"], "F3o": f["L3_ffn_bo"], "L2con": f["L2_ffn_b_con"], "L2down": f["L2_ffn_down_bias"]}
    rows.update({f"e{e}": f["L0_ffn_exp_b2"][e] for e in range(NE)})
    cols = {"B0q": f["L0_ffn_bq"], "B0k": f["L0_ffn_bk"], "D2q": f["L2_xattn_bq"], "D2k": f["L2_xattn_bk"], "E3q": f["L3_xattn_q_b"],
            "E3k": f["L3_xattn_k_b"], "ln1_g": f["L0_ffn_ln1_g"], "ln1_b": f["L0_ffn_ln1_b"], "ln2_g": f["L0_ffn_ln2_g"], "ln2_b": f["L0_ffn_ln2_b"]}
    w_exp = z((P, NM, D + 1), np.float32)
    w_exp[:, :, :D] = f["L2_ffn_W_exp"].T.reshape(NM, P, D).transpose(1, 0, 2)
    w_exp[:, :, D] = f["L2_ffn_b_exp"].reshape(NM, P).T
    up, down = f["L2_ffn_up_weights"].reshape(LOW + HIGH, -1), f["L2_ffn_down_weights"].reshape(LOW + HIGH, -1)
    low = z((MROW + 2, 2 * HID), np.float32)
    low[:2 * LOW] = np.concatenate([up[:LOW], down[:LOW][::-1]])
    high = [w[LOW:].reshape(HIGH, NM // 2, P, 4).transpose(2, 0, 1, 3).reshape(P, -1) for w in (up, down)]
    eye = np.eye(P, dtype=np.float32)
    k_, q_ = np.arange(P)[:, None], np.arange(P)[None, :]
    causal = np.stack([np.where(q_ > k_, -BIG, 0.0), np.where(k_ > q_, -BIG, 0.0)], 1).astype(np.float16)
    e4 = z((P, P), np.float32)
    for j in range(GH):
        e4[QUARTER * j + DH, QUARTER * j:QUARTER * (j + 1)] = 1.0
    e64 = z((TX, TX), np.float32)
    e64[DS] = 1.0
    kx = z((MROW + 2, len(XL), NH, TX), np.float16)
    kx[48, :, :, TC:] = -BIG
    kx[MROW:] = 1.0
    qs = z((MROW - 48, 2, GH, T), np.float16)
    qs[0] = BIG
    ks = z((MROW + 2 - 48, 2, GH, T), np.float16)
    ks[MROW - 48:] = 1.0
    eps = z((P, 2), np.float32)
    eps[:, 0] = EPS
    a = {
        "x": with_next(f["x"]), "ctxT": with_next(f["ctx_1024"].transpose(0, 2, 1)), "mask": with_next(f["mask_BxS2_ik0"]),
        "wflat": np.concatenate([halves_of(mats[n]) for n in FLAT + CTXW], 1),
        "wpad": np.concatenate([p.transpose(1, 0, 2).reshape(P, -1) for p in pads], 1),
        "bcol": np.concatenate([cols[n].reshape(KD, P).T for n in BCOL] + [f["L2_ffn_up_bias"].reshape(NM, P).T,
                               f["L0_ffn_exp_b1"].reshape(NE * NM, P).T], 1),
        "brow": np.stack([rows[n] for n in BROW]),
        "gate_W": halves_of(f["L0_ffn_gate_W"]), "gate_b": f["L0_ffn_gate_b"].reshape(1, NE),
        "lam": np.concatenate([f["L0_xattn_lambda_" + n] for n in ("q1", "k1", "q2", "k2")]).reshape(1, -1),
        "exp_W1": f["L0_ffn_exp_W1"].reshape(NE, KD, P, HID).transpose(0, 2, 1, 3).reshape(NE, P, -1),
        "exp_W2": f["L0_ffn_exp_W2"].reshape(NE, NM, P, D).transpose(0, 2, 1, 3).reshape(NE, P, -1),
        "L1_W1": halves_of(f["L1_ffn_W1"].T), "L1_W2": f["L1_ffn_W2"].T.reshape(NM, P, D).transpose(1, 0, 2).reshape(P, -1),
        "L1_b1": f["L1_ffn_b1"].reshape(1, -1), "L1_b2": f["L1_ffn_b2"].reshape(1, -1),
        "W_exp": w_exp, "W_con": f["L2_ffn_W_con"].reshape(NM, P, D).transpose(1, 0, 2),
        "low_w": low, "high_w": np.concatenate(high, 1),
        "F3_Wq": f["L3_ffn_Wq"].reshape(KD, P, HID).transpose(1, 0, 2), "F3_Wk": f["L3_ffn_Wk"].reshape(KD, P, HID).transpose(1, 0, 2),
        "F3_Wv": f["L3_ffn_Wv"].reshape(KD, P, HID).transpose(1, 0, 2),
        "F3_bq": f["L3_ffn_bq"].reshape(-1, 1), "F3_bk": f["L3_ffn_bk"].reshape(-1, 1), "F3_bv": f["L3_ffn_bv"].reshape(1, -1),
        "F3_Wr": f["L3_ffn_Wr"].reshape(KD, P, NH).transpose(1, 0, 2), "F3_br": f["L3_ffn_br"].reshape(1, -1),
        "c_ident": eye, "c_ident16": eye.astype(np.float16), "c_causal": causal, "c_E4": e4, "c_E64": e64,
        "c_iota": np.tile(np.arange(NE, dtype=np.float32), (P, 1)), "c_eps": eps, "c_kx": kx, "c_qs": qs, "c_ks": ks,
    }
    return {k: np.ascontiguousarray(v) for k, v in a.items()}


STAGES = ("A", "B", "M", "C", "L1", "D", "L2", "E", "F")


def program(nc, arrays, known, stages):
    args = {k: nc.dram_tensor(f"in_{k}", v.shape, mybir.dt.from_np(v.dtype), kind="ExternalInput").ap() for k, v in arrays.items()}
    out = nc.dram_tensor("out_0", (NB, T, D), F32, kind="ExternalOutput").ap()
    return build(nc, args, out, known, stages)


def kernel(**inputs):
    import concourse.bacc as _bacc
    from concourse.bass_utils import run_bass_kernel_spmd as _run

    arrays = layouts(inputs)
    counted = program(_bacc.Bacc("TRN2", target_bir_lowering=False, num_devices=1), arrays, None, STAGES)
    nc = _bacc.Bacc("TRN2", target_bir_lowering=False, num_devices=1)
    program(nc, arrays, counted, STAGES)
    r = _run(nc, [{f"in_{k}": v for k, v in arrays.items()}], core_ids=[0])
    return r.results[0]["out_0"]
```

```python
from contextlib import ExitStack

import concourse.bass as bass
from concourse import mybir
import numpy as np

P = 128
NB, T, D, TC = 4, 1024, 256, 77
NT = T // P
KD = D // P
CH = 512
HID = 4 * D
NM = HID // P
NE = 8
NH, DH = 16, 16
NG, GH = 4, 4
TX = 104
TV = 96
HS, DS = 4, 64
QUARTER = 32
EPS = 1e-5
LAM0 = 0.8 - 0.6 * float(np.exp(-0.3 * 12))
WS = 64.0
BIG = 60000.0
MAGIC = 1.5 * 2.0 ** 23
QB = 127.0
MROW = 96
NP, NPX = 5, 7

F32, F16, I32, U32 = mybir.dt.float32, mybir.dt.float16, mybir.dt.int32, mybir.dt.uint32
ALU, ACT, AX = mybir.AluOpType, mybir.ActivationFunctionType, mybir.AxisListType.X

FLAT = ["A0q", "A0o", "B0q", "B0k", "B0v", "C1q", "D2q", "E3q"]
PADDED = ["B0p", "C1o", "D2o", "E3id", "F3o"]
CTXW = ["A0k", "A0v", "C1k", "C1v", "D2k", "D2v", "E3k", "E3v"]
BROW = ["B0v", "B0p", "C1o", "D2v", "D2o", "E3v", "F3o", "L2con", "L2down"] + [f"e{e}" for e in range(NE)]
BCOL = ["B0q", "B0k", "D2q", "D2k", "E3q", "E3k", "ln1_g", "ln1_b", "ln2_g", "ln2_b"]
BC_UP = 2 * len(BCOL)
BC_E1 = BC_UP + NM
NBC = BC_E1 + NE * NM
LOW, HIGH = 7, 3
XL = ["C1", "D2", "E3"]
FLAT_N, PAD_N = KD * D, GH * D


N_LOADS = 19


class Ledger:

    def __init__(self, known):
        self.count, self.value, self.slot, self.freed = {}, {}, {}, {}
        self.known = known

    def mark(self, name, key, inc):
        self.count[name] = self.count.get(name, 0) + inc
        if (name, key) in self.value:
            raise KeyError(f"twice: {name} {key}")
        self.value[name, key] = self.count[name]
        return inc

    def at(self, name, key):
        return self.known.value[name, key] if self.known else 1


def own_attention_steps():
    order = [(t, j) for pair in ((0, 7), (1, 6), (2, 5), (3, 4)) for j in range(GH) for t in pair]
    spread = [4, 6, 6, 6, 5, 5, 0, 0]
    steps = [("S", 0, t, j) for t in range(NT) for j in range(GH)] + [("MT", 0)]
    for g in range(NG):
        ahead = [("S", g + 1) + o for o in order] if g + 1 < NG else []
        for kt in range(NT):
            mine = [("ST", g, kt, 0)] + ([("PV", g, kt - 1, c) for c in range(2) if kt <= 4 * (c + 1)] if kt else [])
            mine += [("ST", g, kt, j) for j in range(1, GH)]
            for i, step in enumerate(mine):
                late = 2 if kt == 0 else 0
                n = spread[kt] * max(i + 1 - late, 0) // (len(mine) - late) - spread[kt] * max(i - late, 0) // (len(mine) - late)
                steps += [step] + ahead[:n]
                del ahead[:n]
            if g + 1 < NG and kt == 5:
                steps += [("MT", g + 1)]
            if g and kt == 1:
                steps += [("RINV", g - 1)]
            if g and kt == 3:
                steps += [("NB", g - 1)]
        steps += [("PV", g, NT - 1, 1)]
    return steps + [("WS", 0), ("WS", 1), ("RINV", NG - 1), ("WS", 2), ("WB", 0), ("WB", 1), ("NB", NG - 1), ("WB", 2), ("WL",)]


def context_attention_steps():
    def S(g, a, b):
        return [("S", g, t) for t in range(a, b)]

    def ST(g, a, b):
        return [("ST", g, 0, j) for j in range(a, b)]

    def PV(g):
        return [("PV", g, 0, 0), ("PV", g, 0, 1)]

    steps = S(0, 0, NT) + [("MT", 0)] + S(1, 0, NT) + [("MT", 1)]
    for j in range(GH):
        steps += ST(0, j, j + 1) + S(2, 2 * j, 2 * j + 2)
    steps += [("MT", 2)]
    for g in range(NG):
        for j in range(GH if g + 1 < NG else 0):
            if j == 3:
                steps += PV(g)
            steps += ST(g + 1, j, j + 1) + (S(3, 2 * j, 2 * j + 2) if g == 0 else [])
        if g == 0:
            steps += [("MT", 3)]
        if g == NG - 1:
            steps += [("WS", 0)] + PV(g)
        else:
            steps += [("RINV", g)]
        if g:
            steps += [("NB", g - 1)]
    return steps + [("RINV", NG - 1), ("WS", 1), ("WB", 0), ("WB", 1), ("NB", NG - 1), ("WS", 2), ("WB", 2), ("WL",)]


def attention_steps(own):
    return own_attention_steps() if own else context_attention_steps()


def last_attention_steps():
    steps = [("S", 0, t, c) for t in range(NT) for c in range(2)] + [("MT", 0)]
    for h in range(HS):
        ahead = [("S", h + 1, t, c) for t in range(NT) for c in range(2)] if h + 1 < HS else []
        for kt in range(NT):
            steps += [("ST", h, kt)] + ahead[:1]
            if kt:
                steps += [("PV", h, kt - 1, 0)] + ahead[1:2] + [("PV", h, kt - 1, 1)] + ahead[2:3]
            else:
                steps += ahead[1:3]
            del ahead[:3]
            if h + 1 < HS and kt == 6:
                steps += [("MT", h + 1)]
            if h and kt == 2:
                steps += [("RINV", h - 1)]
            if h and kt == 3:
                steps += [("NB", h - 1)]
        steps += [("PV", h, NT - 1, 0), ("PV", h, NT - 1, 1)]
    return steps + [("WS", 0), ("WS", 1), ("RINV", HS - 1), ("WS", 2), ("WB", 0), ("WB", 1), ("WB", 2), ("NB", HS - 1), ("WL",)]


def build(nc, A, out, known):
    led = Ledger(known)
    with ExitStack() as ctx:
        def sb(name, shape, dt):
            return ctx.enter_context(nc.sbuf_tensor(name, shape, dt))

        def dram(name, shape, dt):
            return nc.dram_tensor(name, shape, dt, kind="Internal").ap()

        Wf = sb("weights_flat", [P, len(FLAT), 2, KD, D], F16)
        Wp = sb("weights_padded", [P, len(PADDED), 2, GH, D], F16)
        Wq1 = sb("ternary_W1", [P, KD, HID], F16)
        Wq2 = sb("ternary_W2", [P, NM, D], F16)
        Wexp = sb("butterflied_W_exp", [P, KD, HID], F32)
        RT = sb("butterflied_W_con_turned", [P, NM, D], F32)
        X = sb("x_tokens", [P, NT, D], F32)
        H = sb("h_tokens", [P, NT, D], F32)
        XT = sb("x_channels_hi_lo", [P, 2, KD, T], F16)
        QS = sb("q_stack", [P, 2, GH, T], F16)
        KS = sb("k_stack", [P, 2, GH, T], F16)
        KX = sb("k_stack_context", [MROW + 2, len(XL), NH, TX], F16)
        VX = sb("v_context", [P, len(XL), NH, QUARTER], F32)
        KP0 = sb("k_context_0", [P, 2, TX], F16)
        VP0 = sb("v_context_0", [P, 2, D], F16)
        CTf = sb("context_f32", [P, KD, TC], F32)
        identf = sb("identf", [P, P], F32)
        ident = sb("ident", [P, P], F16)
        big = sb("big_ident", [P, P], F16)
        small = sb("small_ident", [P, P], F16)
        causal = sb("causal", [P, 2, P], F16)
        E4 = sb("spread_sums", [P, P], F32)
        E64 = sb("spread_sums_last", [TV, TV], F32)
        onesf = sb("ones_f32", [P, P], F32)
        BR = sb("bias_rows", [P, 2, D], F16)
        BC = sb("bias_columns", [P, NBC], F32)
        upb = sb("up_bias_whole", [P, NM], F32)
        gateW = sb("gate_W", [P, 2, KD, NE], F16)
        gateb = sb("gate_b", [P, NE], F32)
        iota = sb("iota", [P, NE], F32)
        lamt = sb("lambda_work", [P, 8], F32)
        epsc = sb("eps_zero_minus_magic", [P, 3], F32)
        F3Wr = sb("router_W", [P, KD, NH], F32)
        F3br = sb("router_b", [1, NH], F32)
        wsc = sb("ternary_scales", [P, 8], F32)
        stats = sb("ln_stats", [P, NT, 6], F32)
        mv = sb("ln_mean_var", [P, NT, 2], F32)
        rstd = sb("ln_rstd", [P, NT], F32)
        sd = sb("ln_std", [P, NT], F32)
        mpart = sb("max_parts", [P, GH * NT, 2], F32)
        negm = sb("minus_max", [P, 2, GH * NT], F32)
        mrow = sb("minus_max_rows", [GH * NT, 2, 2, P], F16)
        rsum = sb("sums_by_token", [P, NG, QUARTER], F32)
        rinv = sb("inverse_sums_by_token", [P, NG, QUARTER], F32)
        sm = sb("small_work", [P, 160], F32)
        maxv = sb("top_values", [P, NT, NE], F32)
        maxi = sb("top_indices", [P, NT, NE], U32)
        wfull = sb("expert_weights", [P, NT, NE], F32)
        maskr = sb("mask_row", [1, TX], I32)
        rt = sb("router_row", [1, 96], F32)
        rti = sb("router_index", [1, NE], U32)
        xmean = sb("sum_x", [P, 2, KD], F32)
        gcol = sb("gates_by_row", [P, 8], F32)
        arena = sb("arena", [P, 16 * 1024], F32)

        def area(kb, n, dt=F32, rows=P):
            v = arena[0:rows, int(kb * 256):int(kb * 256) + (n if dt == F32 else n // 2)]
            return v if dt == F32 else v.bitcast(dt)

        stage_flat = area(0, len(FLAT + CTXW) * FLAT_N)
        stage_pad = area(32, len(PADDED) * PAD_N)
        ctx_split = area(52, FLAT_N * 8, F16)
        lamr = area(60, 6 * P)
        gwf = area(63, KD * NE)
        spare = KX[:, :, :, :].rearrange("p l h c -> p (l h c)").bitcast(F32)
        low_w = spare[:, 0:2 * HID]
        brf = spare[:, 2 * HID:2 * HID + D]
        KVW = area(0, len(CTXW) * 2 * FLAT_N, F16).rearrange("p (w s k d) -> p w s k d", s=2, k=KD, d=D)
        kxs = area(40, 2 * 3 * KD * TX, F16).rearrange("p (s l k c) -> p s l k c", s=2, l=3, k=KD)
        kxf = area(44, 3 * KD * TX).rearrange("p (l k c) -> p l k c", l=3, k=KD)
        CT = area(47, 2 * KD * TX, F16).rearrange("p (s k c) -> p s k c", s=2, k=KD)
        maskb = area(57, NH * TX, F16, rows=1).rearrange("p (h c) -> p h c", h=NH)
        tmp = area(60, T)
        XN = {k: area(o, NT * D).rearrange("p (t d) -> p t d", d=D) for k, o in
              {"A": 48, "B": 16, "M": 48, "C": 16, "D": 16, "E": 16, "L1": 16, "L2": 16, "F": 28}.items()}
        VP = area(0, NT * NH * QUARTER).rearrange("p (t h d) -> p t h d", h=NH, d=QUARTER)
        PR = area(16, NP * T).rearrange("p (n c) -> p n c", c=T)
        PRX = area(8, NPX * T).rearrange("p (n c) -> p n c", c=T)
        OT = {True: [area(36 + 4 * (g % 2), T) for g in range(NG)],
              False: [area(36, T), area(40, T), area(0, T), area(4, T)]}
        ON = area(44, 2 * NG * T, F16).rearrange("p (s g c) -> p s g c", s=2, g=NG)
        qhl = area(44, 2 * KD * T, F16).rearrange("p (s k c) -> p s k c", s=2, k=KD)
        khl = area(52, 2 * KD * T, F16).rearrange("p (s k c) -> p s k c", s=2, k=KD)
        q0 = area(0, 2 * 2 * T, F16).rearrange("p (s h c) -> p s h c", s=2, h=2)
        E0 = area(8, 2 * 2 * TC).rearrange("p (n h c) -> p n h c", n=2, h=2)
        A0 = area(12, NT * TC).rearrange("p (t c) -> p t c", c=TC)
        AT0 = area(32, 2 * T, F16).rearrange("p (s c) -> p s c", s=2)
        AO0 = area(20, 2 * KD * T, F16).rearrange("p (s k c) -> p s k c", s=2, k=KD)
        sq0 = area(36, 2 * D).rearrange("p (n d) -> p n d", n=2)
        WSt = area(0, 2 * KD * HID).rearrange("p (w n) -> p w n", w=2)
        Wm = [area(16 + 16 * i, 2 * 2 * KD * HID, F16).rearrange("p (w s n) -> p w s n", w=2, s=2) for i in range(2)]
        midf = area(48, 3 * CH).rearrange("p (n c) -> p n c", n=3)
        mid = area(54, 4 * 2 * CH, F16).rearrange("p (n s c) -> p n s c", n=4, s=2)
        b1b = area(0, HID)
        hb = area(4, 3 * HID).rearrange("p (n c) -> p n c", n=3)
        xq = area(24, NT * D, F16).rearrange("p (t d) -> p t d", d=D)
        xqT = area(28, KD * T, F16).rearrange("p (k c) -> p k c", k=KD)
        hq = area(32, 2 * HID, F16).rearrange("p (n c) -> p n c", n=2)
        hqT = area(36, 2 * HID, F16).rearrange("p (n c) -> p n c", n=2)
        b2b = area(40, D)
        hr = area(44, 2 * HID).rearrange("p (n c) -> p n c", n=2)
        XTf = area(0, KD * T).rearrange("p (k c) -> p k c", k=KD)
        gT = area(24, 2 * NM * CH).rearrange("p (n m c) -> p n m c", n=2, m=NM)
        VP4 = area(0, NT * HS * TV).rearrange("p (t h d) -> p t h d", h=HS, d=TV)
        Wst = area(12, 3 * KD * D).rearrange("p (w k d) -> p w k d", w=3, k=KD)
        Wsel = area(18, 3 * 2 * KD * D, F16).rearrange("p (w s k d) -> p w s k d", w=3, s=2, k=KD)
        PR4 = area(16, NP * T).rearrange("p (n c) -> p n c", c=T)
        OT4 = [area(36, T, rows=TV), area(40, T, rows=TV)]
        ON4 = area(44, 2 * HS * T, F16, rows=TV).rearrange("p (s g c) -> p s g c", s=2, g=HS)
        bsel = sb("selected_biases", [P, 4], F32)
        bvr = area(24, D, rows=1)
        bvh = area(25, 2 * D, F16, rows=1).rearrange("p (s d) -> p s d", s=2)

        low_up = RT[:, :, :].rearrange("p m d -> p (m d)")[:, 0:HID].unsqueeze(1)
        low_up_t = RT[:, :, :].rearrange("p m d -> p (m d)")[:, HID:2 * HID].rearrange("p (n k c) -> p n k c", n=2, k=1)
        low_down = Wexp[:, 0:1, :]
        low_down_t = Wexp[:, 1, :].rearrange("p (n k c) -> p n k c", n=2, k=1)
        ring_up = QS[:, :, :, :].rearrange("p b h c -> p (b h c)").bitcast(F32).rearrange("p (n c) -> p n c", n=2)
        ring_down = KS[:, :, :, :].rearrange("p b h c -> p (b h c)").bitcast(F32).rearrange("p (n c) -> p n c", n=2)
        rows_e = area(33, NM * (D + 1)).rearrange("p (m d) -> p m d", d=D + 1)
        rows_c = XT[:, :, :, :].rearrange("p s k c -> p (s k c)").bitcast(F32).rearrange("p (m d) -> p m d", d=D)
        high_t = area(42, NM * (D + 1)).rearrange("p (n q d) -> p n q d", n=2, q=NM // 2)
        high_w = sm[:, 0:2 * HIGH * 2 * NM].rearrange("p (e s q rc) -> p e s q rc", e=2, s=HIGH, rc=4)
        fW1 = X[:, :, :].rearrange("p t d -> p (t d)")
        fW2 = H[:, :, :].rearrange("p t d -> p (t d)")

        PS = ctx.enter_context(nc.psum_tensor("ps", [P, 8, CH], F32))
        flat = PS[:, :, :].rearrange("p b c -> p (b c)")
        SLOT = {"A0": flat[:, 0:1024], "A1": flat[:, 1024:2048], "B0": flat[:, 2048:2560], "B1": flat[:, 2560:3072],
                "S0": flat[:, 3072:3584], "S1": flat[:, 3584:4096]}

        d_ctxw = dram("scr_ctx_weights", [P, len(CTXW), 2 * FLAT_N], F16)
        d_kx = dram("scr_k_context", [2, len(XL), KD * P, TX], F16)
        d_q = dram("scr_q", [2, KD * P, T], F16)
        d_k = dram("scr_k", [2, KD * P, T], F16)

        negp = [negm[:, :, :].rearrange("p b n -> p (b n)"), mpart[:, :, :].rearrange("p n c -> p (n c)")]

        names = ["pe", "act", "dve", "pool", "ld_next", "ld_kvw", "ld_const", "st_kx", "ld_kx", "st_q0", "st_q1", "st_k0", "st_k1",
                 "ld_stack0", "ld_stack1", "ld_m0", "ld_m1", "ld_wexp0", "ld_wexp1", "ld_b12",
                 "ld_sel", "st_out"] + [f"{n}{g}" for n in ("ld_s", "ld_r") for g in range(NG)]
        sems = {n: ctx.enter_context(nc.semaphore("s_" + n)) for n in names}
        first_num = min(s.num for s in sems.values())
        assert max(s.num for s in sems.values()) - first_num == len(sems) - 1
        once = {n: ctx.enter_context(nc.semaphore("u_" + n)) for n in (
            "load", "lambda", "ternary", "first", "kvw", "pe", "act", "dve", "pool", "ctxw", "staged", "low_w", "rows_e", "spread_up", "spread_down", "ring_up", "ring_down",
            "up", "down", "high", "wsum", "store0", "store1", "store2", "store3")}
        arrived = ctx.enter_context(nc.semaphore("arrived"))
        go = {n: ctx.enter_context(nc.semaphore("go_" + n)) for n in ("pe", "act", "dve", "pool")}

        def did(name, *key):
            inc = 16 if name[:3] in ("ld_", "st_") else 1
            return sems[name], led.mark(name, key, inc)

        def of(name, *key):
            return sems[name], led.at(name, key)

        def slot(*key):
            return SLOT[led.slot[key]]

        def frees(name, *key):
            led.freed[key] = (name, ("free",) + key)
            return did(name, "free", *key)

        def back(e, c, m, n):
            i = (e * 2 + c) * NM + m - n
            return i // (2 * NM), i // NM % 2, i % NM

        def butterfly(eng, sem, y, t, w, s, i, turned):
            st, k = 2 ** s, y.shape[1]
            pair = y.rearrange("p k (n two s) -> p k n two s", two=2, s=st)
            wv = w.rearrange("p (n s rc) -> p n s rc", s=st, rc=4)
            a = [pair[:, kk, :, 0, :] for kk in range(k)]
            b_ = [pair[:, kk, :, 1, :] for kk in range(k)]
            t0 = [t[:, 0, kk].rearrange("p (n s) -> p n s", s=st) for kk in range(k)]
            t1 = [t[:, 1, kk].rearrange("p (n s) -> p n s", s=st) for kk in range(k)]
            c_ba, c_ab = (1, 2) if turned else (2, 1)
            n = 6 * i * k
            if n:
                eng.wait_ge(sem, n)
            for kk in range(k):
                eng.tensor_tensor(t0[kk], a[kk], wv[:, :, :, 0], ALU.mult).then_inc(sem, 1)
                eng.tensor_tensor(t1[kk], a[kk], wv[:, :, :, c_ba], ALU.mult).then_inc(sem, 1)
            eng.wait_ge(sem, n + 2 * k)
            for kk in range(k):
                eng.tensor_tensor(a[kk], b_[kk], wv[:, :, :, c_ab], ALU.mult).then_inc(sem, 1)
                eng.tensor_tensor(b_[kk], b_[kk], wv[:, :, :, 3], ALU.mult).then_inc(sem, 1)
            eng.wait_ge(sem, n + 4 * k)
            for kk in range(k):
                eng.tensor_tensor(a[kk], a[kk], t0[kk], ALU.add).then_inc(sem, 1)
                eng.tensor_tensor(b_[kk], b_[kk], t1[kk], ALU.add).then_inc(sem, 1)

        wi = {n: i for i, n in enumerate(FLAT)}
        pi = {n: i for i, n in enumerate(PADDED)}
        ci = {n: i for i, n in enumerate(CTXW)}
        bi = {n: i for i, n in enumerate(BROW)}
        bc = {n: 2 * i for i, n in enumerate(BCOL)}
        runs = [("B", "B0", True), ("C", "C1", False), ("D", "D2", False), ("E", "E3", False)]
        block = ctx.enter_context(nc.Block())

        def batch_end(eng, name):
            eng.drain().then_inc(arrived, 1)
            eng.wait_ge(go[name], 1)
            eng.sem_clear(go[name])

        @block.sync
        def _(sp):
            sp.dma_start(identf[:], A["c_ident"]).then_inc(once["low_w"], 16)
            sp.dma_start(low_w, A["low_w"]).then_inc(once["low_w"], 16)
            for dst, src in [(stage_flat, A["wflat"]), (stage_pad, A["wpad"]), (ident[:], A["c_ident16"]),
                             (causal[:], A["c_causal"]), (E4[:], A["c_E4"]), (E64[:], A["c_E64"]), (iota[:], A["c_iota"]),
                             (BC[:, 0:NBC], A["bcol"]), (gateb[:], A["gate_b"].partition_broadcast(P)),
                             (epsc[:], A["c_eps"]), (high_w, A["high_w"]), (rows_c, A["W_con"]), (brf[0:len(BROW), :], A["brow"]),
                             (gwf[:], A["gate_W"]), (lamr[:, 0:4 * P], A["lam"].partition_broadcast(P)),
                             (F3Wr[:], A["F3_Wr"]), (F3br[:], A["F3_br"]),
                             (fW1, A["L1_W1"]), (fW2, A["L1_W2"])]:
                sp.dma_start(dst, src).then_inc(once["load"], 16)
            for w in range(len(CTXW)):
                sp.wait_ge(once["ctxw"], w + 1)
                sp.dma_start(d_ctxw[:, w, :], ctx_split[:, (w % 4) * 2 * FLAT_N:(w % 4 + 1) * 2 * FLAT_N]).then_inc(once[f"store{w % 4}"], 16)
            sp.wait_ge(once["staged"], 1)
            for i in range(4):
                sp.wait_ge(once[f"store{i}"], 16 * len(CTXW) // 4)
            sp.dma_start(rows_e, A["W_exp"]).then_inc(once["rows_e"], 16)
            sp.dma_start(KVW.rearrange("p w s k d -> p w (s k d)"), d_ctxw).then_inc(once["kvw"], 16)
            sp.wait_ge(once["spread_down"], LOW)
            sp.wait_ge(once["spread_up"], LOW)
            sp.dma_start(KX[:MROW + 2], A["c_kx"]).then_inc(once["kvw"], 16)

            def load_inputs(x, ctx_, mask, sem):
                sp.dma_start(H[:], x.rearrange("o (t p) d -> p (o t) d", p=P)).then_inc(sem, 16)
                sp.dma_start(CTf[:], ctx_.rearrange("o (k p) c -> p (o k) c", p=P)).then_inc(sem, 16)
                sp.dma_start(maskr[:, 0:TC], mask).then_inc(sem, 16)

            sp.wait_ge(once["ternary"], 1)
            load_inputs(A["x"][0:1], A["ctxT"][0:1], A["mask"][0:1], once["first"])
            sp.wait_ge(once["first"], 48)
            sp.wait_ge(arrived, 4)
            sp.wait_ge(once["kvw"], 32)
            sp.sem_clear(arrived)
            for n in go:
                sp.sem_inc(go[n], 1)

            with sp.Fori(0, NB) as b:
                bs = bass.ds(b, 1)
                sp.dma_start(QS[48:MROW, :, :, :], A["c_qs"]).then_inc(*did("ld_const", 1))
                sp.dma_start(KS[48:MROW + 2, :, :, :], A["c_ks"]).then_inc(*did("ld_const", 2))
                sp.wait_ge(*of("dve", "kxs"))
                for s in range(2):
                    for l in range(len(XL)):
                        sp.dma_start(d_kx[s, l, :, 0:TC].rearrange("(k p) c -> p k c", p=P), kxs[:, s, l, :, 0:TC]).then_inc(*did("st_kx", s, l))
                sp.wait_ge(*of("st_kx", 1, 2))
                for n, s in enumerate((0, 1, 0)):
                    for l in range(len(XL)):
                        sp.dma_start(KX[16 * n:16 * n + 16, l, :, 0:TC],
                                     d_kx[s, l, :, 0:TC].rearrange("(h i) c -> i h c", i=DH)).then_inc(*did("ld_kx", n, l))
                sp.wait_ge(*of("dve", "mask"))
                sp.dma_start(KX[48:49, 2, :, 0:TC], maskb[:, :, 0:TC]).then_inc(*did("ld_kx", "mask"))

                def stacks(L, own, g):
                    buf = g % 2
                    if g >= 2:
                        sp.wait_ge(*of("pe", L, "ST", g - 2, NT - 1 if own else 0, GH - 1))
                    for n, s in enumerate((0, 0, 1)):
                        sp.dma_start(QS[16 * n:16 * n + 16, buf],
                                     d_q[s, g * GH * DH:(g + 1) * GH * DH].rearrange("(h i) c -> i h c", i=DH)).then_inc(*did(f"ld_stack{buf}", L, g, "q", n))
                    if own:
                        for n, s in enumerate((0, 1, 0)):
                            sp.dma_start(KS[16 * n:16 * n + 16, buf],
                                         d_k[s, g * GH * DH:(g + 1) * GH * DH].rearrange("(h i) c -> i h c", i=DH)).then_inc(*did(f"ld_stack{buf}", L, g, "k", n))

                def max_rows(L, g):
                    sp.wait_ge(*of("dve", L, "mrow", g))
                    n = NT if L == "F3" else GH * NT
                    stack = KS if L in XL and g >= 2 else QS
                    for s in range(2):
                        r = slice(MROW + s, MROW + s + 1)
                        if L == "F3":
                            dst = QS[r, 1, g, :].rearrange("s (n q) -> s n q", q=P)
                        else:
                            dst = stack[r, g % 2].rearrange("s h (t q) -> s (h t) q", q=P)
                        sp.dma_start(dst, mrow[0:n, g % 2, s]).then_inc(*did(f"ld_m{g % 2}", L, g, s))

                def sums(L, ot, g, rows):
                    n = len(range(*rows.indices(P)))
                    w = n * T // P
                    sp.wait_ge(*of("act", L, "ot", g, 1))
                    sp.dma_start(rsum[:, g, 0:w], ot[rows, :].rearrange("j (a b) -> j a b", b=w)).then_inc(*did(f"ld_s{g}", L))
                    sp.wait_ge(*of("dve", L, "rinv", g))
                    sp.dma_start(ot[rows, :].rearrange("j (a b) -> j a b", b=w), rinv[:, g, 0:w]).then_inc(*did(f"ld_r{g}", L))

                def spill_half(L, n, dst, src, m):
                    sp.wait_ge(*of("dve", L, n + "lo", m))
                    sp.dma_start(dst[:, m * P:(m + 1) * P].rearrange("s p c -> p s c"), src[:, :, m]).then_inc(*did(f"st_{n}{m}", L))

                def spill(L, m):
                    spill_half(L, "q", d_q, qhl, m)
                    spill_half(L, "k", d_k, khl, m)
                    sp.wait_ge(*of(f"st_q{m}", L))
                    sp.wait_ge(*of(f"st_k{m}", L))

                def context_attention(L):
                    for pair, stack in enumerate((QS, KS)):
                        spill_half(L, "q", d_q, qhl, pair)
                        sp.wait_ge(*of(f"st_q{pair}", L))
                        for n, s in enumerate((0, 0, 1)):
                            sp.dma_start(stack[16 * n:16 * n + 16].rearrange("i b h c -> i (b h) c"),
                                         d_q[s, pair * P:(pair + 1) * P].rearrange("(h i) c -> i h c", i=DH)).then_inc(*did(f"ld_stack{pair}", L, n))
                    for g in range(NG):
                        max_rows(L, g)
                    for g in range(NG):
                        sums(L, OT[False][g], g, slice(DH, P, QUARTER))

                def own_attention(L):
                    spill(L, 0)
                    stacks(L, True, 0)
                    spill_half(L, "q", d_q, qhl, 1)
                    spill_half(L, "k", d_k, khl, 1)
                    stacks(L, True, 1)
                    sp.wait_ge(*of("st_q1", L))
                    sp.wait_ge(*of("st_k1", L))
                    max_rows(L, 0)
                    for g in range(NG):
                        if g:
                            sums(L, OT[True][g - 1], g - 1, slice(DH, P, QUARTER))
                        if g + 1 < NG:
                            max_rows(L, g + 1)
                        if g + 2 < NG:
                            stacks(L, True, g + 2)
                    sums(L, OT[True][NG - 1], NG - 1, slice(DH, P, QUARTER))

                own_attention("B0")
                sp.wait_ge(*of("pe", "B0", "ST", NG - 1, NT - 1, GH - 1))
                sp.dma_start(KS[48:MROW, :, :, :], A["c_qs"]).then_inc(*did("ld_const", 3))
                sp.wait_ge(*of("pe", "B0", "PV", NG - 1, NT - 1, 1))
                for e in range(NE):
                    if e:
                        sp.wait_ge(*of("dve", "M", "wlo", e - 1, 1))
                    sp.dma_start(WSt[:, 0], A["exp_W1"][e]).then_inc(*did("ld_wexp0", e))
                    sp.dma_start(WSt[:, 1], A["exp_W2"][e]).then_inc(*did("ld_wexp1", e))
                context_attention("C1")
                sp.wait_ge(*of("dve", "L1", "xs"))
                sp.dma_start(b1b, A["L1_b1"].partition_broadcast(P)).then_inc(*did("ld_b12", 0))
                sp.dma_start(b2b, A["L1_b2"].partition_broadcast(P)).then_inc(*did("ld_b12", 1))
                context_attention("D2")
                context_attention("E3")
                sp.wait_ge(*of("dve", "M", "xh", NT - 1))
                load_inputs(A["x"][1:][bs], A["ctxT"][1:][bs], A["mask"][1:][bs], did("ld_next", 0)[0])
                did("ld_next", 1), did("ld_next", 2)

                def next_context_weights():
                    sp.dma_start(KVW.rearrange("p w s k d -> p w (s k d)"), d_ctxw).then_inc(*did("ld_kvw"))

                sp.wait_ge(*of("pe", "E3", "ST", NG - 1, 0, GH - 1))
                sp.dma_start(KS[MROW:MROW + 2, :, :, :], A["c_ks"][MROW - 48:MROW - 46]).then_inc(*did("ld_const", 4))
                sp.wait_ge(*of("dve", "F", "index"))
                for k in range(HS):
                    h = sp.value_load(rti[0:1, k:k + 1], min_val=0, max_val=15)
                    sp.dma_start(Wst.rearrange("p w k d -> p (w k) d")[:, :, k * DS:(k + 1) * DS],
                                 A["F3_W"][:, :, bass.ds(h * DS, DS)]).then_inc(*did("ld_sel", k, "W"))
                    sp.dma_start(bsel[DS * (k % 2):DS * (k % 2) + DS, k // 2 * 2:k // 2 * 2 + 2],
                                 A["F3_bqk"][bass.ds(h * DS, DS)]).then_inc(*did("ld_sel", k, "b"))
                    sp.dma_start(bvr[0:1, k * DS:(k + 1) * DS], A["F3_bv"][:, bass.ds(h * DS, DS)]).then_inc(*did("ld_sel", k, "bv"))
                for m in range(KD):
                    spill("F3", m)
                    for n, (dst, src) in enumerate([(QS[0:DS, 0], d_q[0]), (QS[DS:P, 0], d_q[1]), (KS[0:DS, 0], d_k[0]),
                                                    (KS[DS:P, 0], d_k[0]), (QS[0:DS, 1], d_q[0]), (KS[0:DS, 1], d_k[1])]):
                        sp.dma_start(dst[:, 2 * m:2 * m + 2], src[m * P:(m + 1) * P].rearrange("(h i) c -> i h c", i=DS)
                                     ).then_inc(*did(f"ld_stack{m}", "F3", n))
                max_rows("F3", 0)
                for h in range(HS):
                    if h + 1 < HS:
                        max_rows("F3", h + 1)
                    if h == HS - 1:
                        sp.wait_ge(*of("pe", "F3", "PV", h, NT - 1, 1))
                        next_context_weights()
                    sums("F3", OT4[h % 2], h, slice(DS, DS + 1, 1))
                result = out[bs].rearrange("o (t p) d -> p (o t) d", p=P)
                for p in range(NT // 2):
                    sp.wait_ge(*of("dve", "F3", "x", p))
                    sp.dma_start(result[:, 2 * p:2 * p + 2], X[:, 2 * p:2 * p + 2]).then_inc(*did("st_out", p))
                sp.wait_ge(*of("dve", "final"))
                for n in names:
                    if n in led.count:
                        sp.wait_ge(sems[n], led.count[n])
                sp.wait_ge(arrived, 4)
                sp.sem_clear(range(first_num, first_num + len(sems)))
                sp.sem_clear(arrived)
                for n in go:
                    sp.sem_inc(go[n], 1)

        @block.tensor
        def _(pe):
            holder, turn = {}, {"A": 0, "S": 0, "SB": 0}

            def claim(kind, *key):
                name = kind
                if kind in turn:
                    ring = ("S0", "S1", "B0", "B1") if kind == "SB" else (kind + "0", kind + "1")
                    name = ring[turn[kind] % len(ring)]
                    turn[kind] += 1
                led.slot[key] = name
                if name in holder:
                    reader = led.known.freed[holder[name]] if known else None
                    pe.wait_ge(sems[reader[0] if known else "act"], led.known.value[reader] if known else 1)
                holder[name] = key
                return SLOT[name]

            def split3(o, left, right, first, last, **kw):
                pe.matmul(o, left[0], right[0], start=first, stop=False, **kw)
                pe.matmul(o, left[0], right[1], start=False, stop=False, **kw)
                return pe.matmul(o, left[1], right[0], start=False, stop=last, **kw)

            def bias_rows(o, name, n, idt=None, last=True, **kw):
                row = (ident if idt is None else idt)[:, bi[name]:bi[name] + 1].to_broadcast([P, n])
                pe.matmul(o, row, BR[:, 0], start=False, stop=False, **kw)
                return pe.matmul(o, row, BR[:, 1], start=False, stop=last, **kw)

            def parts(t, *i):
                return t[(slice(None), 0) + i], t[(slice(None), 1) + i]

            pe.wait_ge(once["low_w"], 32)
            for i in range(LOW):
                for n, (row, ring, col) in enumerate(((i, "ring_up", 0), (LOW + i, "ring_down", 2 * HID))):
                    if i:
                        pe.wait_ge(once[ring], i)
                    for c in range(4):
                        mm = pe.matmul(flat[:, col + c * CH:col + (c + 1) * CH], identf[0:MROW + 2, row:row + 1].to_broadcast([MROW + 2, P]),
                                       low_w[:, c * CH:(c + 1) * CH], start=True, stop=True)
                    mm.then_inc(once[("spread_up", "spread_down")[n]], 1)
            pe.wait_ge(once["ring_up"], LOW)
            pe.wait_ge(once["ring_down"], LOW)
            pe.wait_ge(once["wsum"], 2)
            pe.wait_ge(once["pool"], 1)
            pe.matmul(SLOT["S0"][:, 0:2], onesf[:], wsc[:, 0:2], start=True, stop=True).then_inc(once["pe"], 1)
            pe.wait_ge(once["up"], 6 * LOW)
            pe.wait_ge(once["rows_e"], 16)
            pe.wait_ge(once["ternary"], 1)
            for m in range(NM):
                mm = pe.matmul(PS[:, m, 0:D + 1], low_up[:, 0, m * P:(m + 1) * P], rows_e[:, m], start=True, stop=True)
            mm.then_inc(once["pe"], 1)
            pe.wait_ge(once["down"], 6 * LOW)
            pe.wait_ge(once["high"], 16 * HIGH + 1)
            for m in range(NM):
                mm = pe.matmul(flat[:, m * D:(m + 1) * D], low_down[:, 0, m * P:(m + 1) * P], rows_c[:, m], start=True, stop=True)
            mm.then_inc(once["pe"], 1)
            pe.wait_ge(once["high"], 2 * 16 * HIGH + 1)
            for k in range(KD):
                for m in range(NM):
                    mm = pe.transpose(flat[:, 2 * HID + k * HID + m * P:2 * HID + k * HID + (m + 1) * P], rows_e[:, m, k * P:(k + 1) * P], identf[:])
            mm.then_inc(once["pe"], 1)
            batch_end(pe, "pe")

            with pe.Fori(0, NB):
                def turn_x(N):
                    for c in range(2):
                        s = claim("A", "T", N, c)
                        for t in range(4 * c, 4 * c + 4):
                            pe.wait_ge(*of("dve", N, "xn", t))
                            for k in range(KD):
                                mm = pe.transpose(s[:, k * CH + t % 4 * P:k * CH + (t % 4 + 1) * P], XN[N][:, t, k * P:(k + 1) * P], identf[:])
                        mm.then_inc(*did("pe", "T", N, c))

                def project(N, key, weight):
                    s = claim("A", *key)
                    for c in range(2):
                        pe.wait_ge(*of("dve", N, "xlo", c))
                        for k in range(KD):
                            mm = split3(s[:, c * CH:(c + 1) * CH], weight(k), parts(XT, k, slice(c * CH, (c + 1) * CH)), k == 0, k == KD - 1)
                    mm.then_inc(*did("pe", *key))

                def wflat(name, m):
                    return lambda k: (Wf[:, wi[name], 0, k, m * P:(m + 1) * P], Wf[:, wi[name], 1, k, m * P:(m + 1) * P])

                turn_x("A")
                pe.wait_ge(*of("dve", "ctlo"))

                def kvw(name, k, a, b):
                    return KVW[:, ci[name], 0, k, a:b], KVW[:, ci[name], 1, k, a:b]

                s = claim("S", "K0")
                for k in range(KD):
                    mm = split3(s[:, 0:TC], kvw("A0k", k, 0, P), parts(CT, k, slice(0, TC)), k == 0, k == KD - 1)
                mm.then_inc(*did("pe", "K0"))
                s = claim("S", "V0")
                for k in range(KD):
                    mm = split3(s[0:TC, 0:D], parts(CT, k, slice(0, TC)), kvw("A0v", k, 0, D), k == 0, k == KD - 1)
                mm.then_inc(*did("pe", "V0"))
                for l, L in enumerate(XL):
                    for m in range(KD):
                        s = claim("S", "KX", l, m)
                        for k in range(KD):
                            mm = split3(s[:, 0:TC], kvw(L + "k", k, m * P, (m + 1) * P), parts(CT, k, slice(0, TC)), k == 0, k == KD - 1)
                        mm.then_inc(*did("pe", "KX", l, m))
                    s = claim("S", "VX", l)
                    for k in range(KD):
                        mm = split3(s[0:TC, 0:D], parts(CT, k, slice(0, TC)), kvw(L + "v", k, 0, D), k == 0, k == KD - 1 and L == "C1")
                    if L != "C1":
                        mm = bias_rows(s[0:TC, 0:D], L + "v", TC)
                    mm.then_inc(*did("pe", "VX", l))

                for h in range(2):
                    project("A", ("A", "Q", h), wflat("A0q", h))
                pe.wait_ge(*of("dve", "A", "kp0"))
                pe.wait_ge(*of("dve", "A", "qlo", 1))
                for t in range(NT):
                    s = claim("S", "A", "S", t)
                    for h in range(2):
                        mm = split3(s[:, h * TC:(h + 1) * TC], (q0[:, 0, h, t * P:(t + 1) * P], q0[:, 1, h, t * P:(t + 1) * P]),
                                    parts(KP0, slice(0, TC)), True, True)
                    mm.then_inc(*did("pe", "A", "S", t))
                s = claim("A", "A", "PT")
                for t in range(NT):
                    pe.wait_ge(*of("dve", "A", "p", t))
                    mm = pe.transpose(s[0:TC, t * P:(t + 1) * P], A0[:, t, :], identf[:])
                mm.then_inc(*did("pe", "A", "PT"))
                pe.wait_ge(*of("dve", "A", "ptlo"))
                pe.wait_ge(*of("dve", "A", "vp0"))
                for m in range(KD):
                    s = claim("A", "A", "O", m)
                    for c in range(2):
                        mm = split3(s[:, c * CH:(c + 1) * CH], (VP0[0:TC, 0, m * P:(m + 1) * P], VP0[0:TC, 1, m * P:(m + 1) * P]),
                                    (AT0[0:TC, 0, c * CH:(c + 1) * CH], AT0[0:TC, 1, c * CH:(c + 1) * CH]), True, True)
                    mm.then_inc(*did("pe", "A", "O", m))
                for t in range(NT):
                    s = claim("S", "A", "N", t)
                    split3(s[:, 0:D], (AT0[0:TC, 0, t * P:(t + 1) * P], AT0[0:TC, 1, t * P:(t + 1) * P]),
                           (VP0[0:TC, 0, :], VP0[0:TC, 1, :]), True, True).then_inc(*did("pe", "A", "N", t))
                pe.wait_ge(*of("dve", "A", "olo", 1))
                for t in range(NT):
                    s = claim("S", "A", "W", t)
                    for k in range(KD):
                        mm = split3(s[:, 0:D], parts(AO0, k, slice(t * P, (t + 1) * P)),
                                    (Wf[:, wi["A0o"], 0, k, :], Wf[:, wi["A0o"], 1, k, :]), k == 0, k == KD - 1)
                    mm.then_inc(*did("pe", "A", "W", t))

                banks = [None] * (NT // 2)

                def output_part(L, kind, g, on, w, bias):
                    if kind == "WS":
                        pe.wait_ge(*of("dve", L, "onlo", g))
                    for p, name in enumerate(("S0", "S1", "B0", "B1")):
                        if (p >= 2) != (kind == "WB"):
                            continue
                        if g == 0:
                            banks[p] = claim(name, L, "W", p)
                        for i in range(2):
                            o = banks[p][:, i * D:(i + 1) * D]
                            t = 2 * p + i
                            split3(o, parts(on, g, slice(t * P, (t + 1) * P)), (w[0:on.shape[0], 0, g, :], w[0:on.shape[0], 1, g, :]),
                                   g == 0 and i == 0, False, skip_group_check=True)
                            if bias and g == 0:
                                bias_rows(o, bias, P, last=False, skip_group_check=True)

                def output_last(L, g, on, w):
                    pe.wait_ge(*of("dve", L, "onlo", g))
                    for t in range(NT):
                        mm = split3(banks[t // 2][:, (t % 2) * D:(t % 2 + 1) * D], parts(on, g, slice(t * P, (t + 1) * P)),
                                    (w[0:on.shape[0], 0, g, :], w[0:on.shape[0], 1, g, :]), False, True, skip_group_check=True)
                        if t % 2:
                            mm.then_inc(*did("pe", L, "W", t // 2))

                def attention(N, L, own):
                    for m in range(KD):
                        project(N, (L, "q", m), wflat(L + "q", m))
                        if own:
                            project(N, (L, "k", m), wflat(L + "k", m))
                    if own:
                        for t in range(NT):
                            s = claim("S", L, "v", t)
                            for k in range(KD):
                                split3(s[:, 0:D], parts(XT, k, slice(t * P, (t + 1) * P)),
                                       (Wf[:, wi[L + "v"], 0, k, :], Wf[:, wi[L + "v"], 1, k, :]), k == 0, False)
                            bias_rows(s[:, 0:D], L + "v", P).then_inc(*did("pe", L, "v", t))
                    l = None if own else XL.index(L)
                    steps = attention_steps(own)
                    probs, np_ = (PR, NP) if own else (PRX, NPX)
                    ring = {s[1:]: n % np_ for n, s in enumerate(s for s in steps if s[0] == "ST")}
                    for step in steps:
                        kind = step[0]
                        g = step[1] if len(step) > 1 else None
                        if g is not None:
                            buf = g % 2
                            q_stack = QS if own or g < 2 else KS
                        if kind == "S" and own:
                            t, j = step[2:]
                            if t == 0 and j == 0:
                                pe.wait_ge(*of(f"ld_stack{buf}", L, g, "k", 2))
                                pe.wait_ge(*of("ld_const", 2))
                            keys = (t + 1) * P
                            for c in range((keys + CH - 1) // CH):
                                n = min(CH, keys - c * CH)
                                s = claim("S" if g else "SB", L, "S", g, t, j, c)
                                on_edge = c * CH + n == keys
                                mm = pe.matmul(s[:, 0:n], QS[0:MROW, buf, j, t * P:(t + 1) * P], KS[0:MROW, buf, j, c * CH:c * CH + n],
                                               start=True, stop=not on_edge)
                                if on_edge:
                                    mm = pe.matmul(s[:, n - P:n], big[:], causal[:, 0, :], start=False, stop=True)
                                mm.then_inc(*did("pe", L, "S", g, t, j, c))
                        elif kind == "S":
                            t = step[2]
                            if t == 0:
                                pe.wait_ge(*of(f"ld_stack{g // 2}", L, 2))
                                pe.wait_ge(*of("ld_const", 3))
                                pe.wait_ge(*of("ld_kx", "mask"))
                            s = claim("SB" if g < 2 else "S", L, "S", g, t)
                            for j in range(GH):
                                mm = pe.matmul(s[:, j * TX:(j + 1) * TX], q_stack[0:MROW, buf, j, t * P:(t + 1) * P],
                                               KX[0:MROW, l, g * GH + j, :], start=True, stop=True)
                            mm.then_inc(*did("pe", L, "S", g, t))
                        elif kind == "MT":
                            s = claim("S", L, "MT", g)
                            if own:
                                pe.wait_ge(*of("dve", L, "negm", g))
                                pe.transpose(s[0:GH * NT, 0:P], negm[:, g % 2, :], identf[:]).then_inc(*did("pe", L, "MT", g))
                            else:
                                pe.wait_ge(*of("dve", "free", L, "S", g, NT - 1))
                                mine = negp[g // 2][:, (g % 2) * GH * NT:(g % 2 + 1) * GH * NT]
                                pe.transpose(s[0:GH * NT, 0:P], mine, identf[:]).then_inc(*did("pe", L, "MT", g))
                        elif kind == "ST":
                            kt, j = step[2:]
                            if kt == 0 and j == 0:
                                pe.wait_ge(*of(f"ld_m{buf}", L, g, 1))
                            s = claim("A", L, "ST", g, kt, j)
                            q0_ = kt * P
                            for c in range(2):
                                a = max(q0_, c * CH)
                                if a >= (c + 1) * CH:
                                    continue
                                key_rows = KS[0:MROW + 2, buf, j, kt * P:(kt + 1) * P] if own else KX[0:MROW + 2, l, g * GH + j, :]
                                o = s[0:P if own else TX, a:(c + 1) * CH]
                                edge = own and a == q0_
                                mm = pe.matmul(o, key_rows, q_stack[0:MROW + 2, buf, j, a:(c + 1) * CH], start=True, stop=not edge)
                                if edge:
                                    mm = pe.matmul(s[:, a:a + P], big[:], causal[:, 1, :], start=False, stop=True)
                            mm.then_inc(*did("pe", L, "ST", g, kt, j))
                        elif kind == "PV":
                            kt, c = step[2:]
                            if kt == 0 and c == 0:
                                acc = [claim("B0", L, "PVacc", g, 0), claim("B1", L, "PVacc", g, 1)]
                                if g == 0:
                                    pe.wait_ge(*(of("act", L, "vp", NT - 1) if own else of("act", "free", "VX", len(XL) - 1)))
                            if c == 0 or kt >= NT // 2:
                                pe.wait_ge(*of("act", L, "exp", g, kt, GH - 1))
                            a = max(kt * P, c * CH)
                            final = kt == (min(NT if own else 1, NT // 2 * (c + 1)) - 1)
                            for j in range(GH):
                                v = VP[:, kt, g * GH + j, :] if own else VX[0:TX, l, g * GH + j, :]
                                p = probs[0:P if own else TX, ring[g, kt, j], a:(c + 1) * CH]
                                mm = pe.matmul(acc[c][QUARTER * j:QUARTER * (j + 1), a - c * CH:CH], v, p, start=kt == 0, stop=final,
                                               tile_position=(0, QUARTER * j))
                            mm.then_inc(*did("pe", L, "PV", g, kt, c))
                        elif kind == "NB":
                            s = claim("A", L, "NB", g)
                            pe.wait_ge(*of(f"ld_r{g}", L))
                            for c in range(2):
                                mm = pe.matmul(s[:, c * CH:(c + 1) * CH], E4[:], OT[own][g][:, c * CH:(c + 1) * CH], start=True, stop=True)
                            mm.then_inc(*did("pe", L, "NB", g))
                        elif kind in ("WS", "WB"):
                            name, bias = {"B0": ("B0p", "B0p"), "C1": ("C1o", "C1o"), "D2": ("D2o", "D2o"), "E3": ("E3id", None)}[L]
                            output_part(L, kind, g, ON, Wp[:, pi[name]], bias)
                        elif kind == "WL":
                            output_last(L, NG - 1, ON, Wp[:, pi[name]])

                def block_of(N, L, own):
                    turn_x(N)
                    attention(N, L, own)

                block_of("B", "B0", True)

                turn_x("M")
                pe.wait_ge(*of("dve", "M", "xlo", 0))

                def gate():
                    pe.wait_ge(*of("dve", "M", "xlo", 1))
                    s = claim("S", "M", "gate")
                    for t in range(NT):
                        for k in range(KD):
                            mm = split3(s[:, t * NE:(t + 1) * NE], parts(XT, k, slice(t * P, (t + 1) * P)), parts(gateW, k), k == 0, k == KD - 1)
                    mm.then_inc(*did("pe", "M", "gate"))

                order = [(e, c, m) for e in range(NE) for c in range(2) for m in range(NM)]

                def up(e, c, m):
                    if c == 0 and m == 0:
                        pe.wait_ge(*of("dve", "M", "wlo", e, 0))
                    s = claim("A", "M", "U", e, c, m)
                    w1 = Wm[e % 2][:, 0].rearrange("p s (k n) -> p s k n", k=KD)
                    for k in range(KD):
                        mm = split3(s[:, 0:CH], parts(w1, k, slice(m * P, (m + 1) * P)), parts(XT, k, slice(c * CH, (c + 1) * CH)),
                                    k == 0, k == KD - 1)
                    mm.then_inc(*did("pe", "M", "U", e, c, m))

                def down(e, c, m):
                    n = (e * 2 + c) * NM + m
                    if m == 0:
                        pair = ("B0", "B1") if (2 * e + c) % 2 == 0 else ("S0", "S1")
                        acc[:] = [claim(pair[0], "M", "D", e, c, 0), claim(pair[1], "M", "D", e, c, 1)]
                    if c == 0 and m == 0:
                        pe.wait_ge(*of("dve", "M", "wlo", e, 1))
                    pe.wait_ge(*of("dve", "M", "midlo", e, c, m))
                    w2 = Wm[e % 2][:, 1].rearrange("p s (m n) -> p s m n", m=NM)
                    for i in range(4):
                        o = acc[i // 2][:, (i % 2) * D:(i % 2 + 1) * D]
                        left = (mid[:, n % 4, 0, i * P:(i + 1) * P], mid[:, n % 4, 1, i * P:(i + 1) * P])
                        mm = split3(o, left, parts(w2, m), m == 0 and i % 2 == 0, False, skip_group_check=True)
                        if m == NM - 1:
                            mm = bias_rows(o, f"e{e}", P, last=True, skip_group_check=True)
                    mm.then_inc(*did("pe", "M", "D", e, c, m))

                acc = [None, None]
                for n in range(len(order) + 2):
                    if n < len(order):
                        up(*order[n])
                    if n == 2:
                        gate()
                    if n >= 2:
                        down(*order[n - 2])

                block_of("C", "C1", False)

                for k in range(KD):
                    s = claim("A", "L1", "XQ", k).bitcast(F16)
                    for t in range(NT):
                        pe.wait_ge(*of("dve", "L1", "xq", t))
                        mm = pe.transpose(s[:, t * P:(t + 1) * P], xq[:, t, k * P:(k + 1) * P], ident[:])
                    mm.then_inc(*did("pe", "L1", "XQ", k))
                pe.wait_ge(*of("act", "L1", "xqT", 1))

                def ternary_up(t):
                    s = claim("A", "L1", "H1", t)
                    for c in range(2):
                        for k in range(KD):
                            mm = pe.matmul(s[:, c * CH:(c + 1) * CH], xqT[:, k, t * P:(t + 1) * P], Wq1[:, k, c * CH:(c + 1) * CH],
                                           start=k == 0, stop=k == KD - 1)
                    mm.then_inc(*did("pe", "L1", "H1", t))

                def ternary_down(t):
                    s = claim("S", "L1", "HQ", t).bitcast(F16)
                    pe.wait_ge(*of("act", "L1", "hq", t))
                    for m in range(NM):
                        mm = pe.transpose(s[:, m * P:(m + 1) * P], hq[:, t % 2, m * P:(m + 1) * P], ident[:])
                    mm.then_inc(*did("pe", "L1", "HQ", t))
                    s = claim("S", "L1", "H2", t)
                    pe.wait_ge(*of("act", "L1", "hqT", t))
                    for m in range(NM):
                        mm = pe.matmul(s[:, 0:D], hqT[:, t % 2, m * P:(m + 1) * P], Wq2[:, m, :], start=m == 0, stop=m == NM - 1)
                    mm.then_inc(*did("pe", "L1", "H2", t))

                for t in range(NT + 2):
                    if t < NT:
                        ternary_up(t)
                    if t >= 2:
                        ternary_down(t - 2)

                block_of("D", "D2", False)

                turn_x("L2")

                def butterfly_up(c):
                    pe.wait_ge(*of("act", "L2", "xf", c))
                    for m in range(NM):
                        s = claim("A", "L2", "G", c, m)
                        for k in range(KD):
                            mm = pe.matmul(s[:, 0:CH], Wexp[:, k, m * P:(m + 1) * P], XTf[:, k, c * CH:(c + 1) * CH],
                                           start=k == 0, stop=k == KD - 1)
                        mm.then_inc(*did("pe", "L2", "G", c, m))

                def butterfly_down(c):
                    for t in range(4 * c, 4 * c + 4):
                        s = claim("S", "L2", "Y", t)
                        pe.wait_ge(*of("act", "L2", "g", c, NM - 1))
                        for m in range(NM):
                            pe.matmul(s[:, 0:D], gT[:, c, m, (t % 4) * P:(t % 4 + 1) * P], RT[:, m, :], start=m == 0, stop=False)
                        bias_rows(s[:, 0:D], "L2con", P, idt=small, last=False)
                        bias_rows(s[:, 0:D], "L2down", P, idt=small).then_inc(*did("pe", "L2", "Y", t))

                butterfly_up(0)
                butterfly_up(1)
                butterfly_down(0)
                butterfly_down(1)

                block_of("E", "E3", False)

                turn_x("F")
                s = claim("S", "F", "R")
                pe.wait_ge(*of("dve", "F", "xmean", 1))
                for c in range(2):
                    for k in range(KD):
                        mm = pe.matmul(s[0:1, 0:NH], xmean[:, c, k:k + 1], F3Wr[:, k, :], start=c + k == 0, stop=c + k == KD)
                mm.then_inc(*did("pe", "F", "R"))
                s = claim("S", "F", "G")
                pe.wait_ge(*of("dve", "F", "gates"))
                pe.matmul(s[:, 0:HS], onesf[0:1, :], rt[0:1, 48:48 + HS], start=True, stop=True).then_inc(*did("pe", "F", "G"))
                for m in range(KD):
                    for w, n in enumerate("qk"):
                        pe.wait_ge(*of("dve", "F", "wsel_lo", w))
                        project("F", ("F3", n, m), lambda k: (Wsel[:, w, 0, k, m * P:(m + 1) * P], Wsel[:, w, 1, k, m * P:(m + 1) * P]))
                pe.wait_ge(*of("dve", "F", "bv_lo"))
                for t in range(NT):
                    s = claim("S", "F3", "v", t)
                    for k in range(KD):
                        split3(s[:, 0:D], parts(XT, k, slice(t * P, (t + 1) * P)), (Wsel[:, 2, 0, k, :], Wsel[:, 2, 1, k, :]), k == 0, False)
                    pe.matmul(s[:, 0:D], ident[0:1, 0:1].to_broadcast([1, P]), bvh[:, 0, :], start=False, stop=False)
                    pe.matmul(s[:, 0:D], ident[0:1, 0:1].to_broadcast([1, P]), bvh[:, 1, :], start=False, stop=True).then_inc(*did("pe", "F3", "v", t))
                pe.wait_ge(*of("ld_const", 4))
                for step in last_attention_steps():
                    kind = step[0]
                    h = step[1] if len(step) > 1 else None
                    if kind == "S":
                        t, c = step[2:]
                        if t == 0 and c == 0:
                            pe.wait_ge(*of(f"ld_stack{h // 2}", "F3", 5))
                        s = claim("S" if h else "SB", "F3", "S", h, t, c)
                        pe.matmul(s[:], QS[:, 0, h, t * P:(t + 1) * P], KS[:, 0, h, c * CH:(c + 1) * CH], start=True, stop=False)
                        pe.matmul(s[:], QS[0:MROW, 1, h, t * P:(t + 1) * P], KS[0:MROW, 1, h, c * CH:(c + 1) * CH],
                                  start=False, stop=True).then_inc(*did("pe", "F3", "S", h, t, c))
                    elif kind == "MT":
                        pe.wait_ge(*of("dve", "F3", "negm", h))
                        s = claim("S", "F3", "MT", h)
                        pe.transpose(s[0:NT, 0:P], negm[:, h % 2, 0:NT], identf[:]).then_inc(*did("pe", "F3", "MT", h))
                    elif kind == "ST":
                        kt = step[2]
                        if kt == 0:
                            pe.wait_ge(*of(f"ld_m{h % 2}", "F3", h, 1))
                        s = claim("A", "F3", "ST", h, kt)
                        for c in range(2):
                            pe.matmul(s[:, c * CH:(c + 1) * CH], KS[:, 0, h, kt * P:(kt + 1) * P], QS[:, 0, h, c * CH:(c + 1) * CH],
                                      start=True, stop=False)
                            mm = pe.matmul(s[:, c * CH:(c + 1) * CH], KS[0:MROW + 2, 1, h, kt * P:(kt + 1) * P],
                                           QS[0:MROW + 2, 1, h, c * CH:(c + 1) * CH], start=False, stop=True)
                        mm.then_inc(*did("pe", "F3", "ST", h, kt))
                    elif kind == "PV":
                        kt, c = step[2:]
                        if kt == 0 and c == 0:
                            acc = [claim("B0", "F3", "PVacc", h, 0), claim("B1", "F3", "PVacc", h, 1)]
                            if h == 0:
                                pe.wait_ge(*of("act", "F3", "vp", NT - 1))
                        if c == 0:
                            pe.wait_ge(*of("act", "F3", "exp", h, kt))
                        pe.matmul(acc[c][0:TV], VP4[:, kt, h, :], PR4[:, (h * NT + kt) % NP, c * CH:(c + 1) * CH],
                                  start=kt == 0, stop=kt == NT - 1).then_inc(*did("pe", "F3", "PV", h, kt, c))
                    elif kind == "NB":
                        s = claim("A", "F3", "NB", h)
                        pe.wait_ge(*of(f"ld_r{h}", "F3"))
                        for c in range(2):
                            mm = pe.matmul(s[0:TV, c * CH:(c + 1) * CH], E64[:], OT4[h % 2][:, c * CH:(c + 1) * CH], start=True, stop=True)
                        mm.then_inc(*did("pe", "F3", "NB", h))
                    elif kind in ("WS", "WB"):
                        output_part("F3", kind, h, ON4, Wp[:, pi["F3o"]], "F3o")
                    elif kind == "WL":
                        output_last("F3", HS - 1, ON4, Wp[:, pi["F3o"]])
                batch_end(pe, "pe")

        @block.scalar
        def _(act):
            for i in range(LOW):
                for spread, ring, user, dst, col in (("spread_up", "ring_up", "up", ring_up, 0),
                                                     ("spread_down", "ring_down", "down", ring_down, 2 * HID)):
                    act.wait_ge(once[spread], i + 1)
                    if i >= 2:
                        act.wait_ge(once[user], 6 * (i - 1))
                    act.activation(dst[:, i % 2], flat[:, col:col + 2 * HID], ACT.Copy).then_inc(once[ring], 1)
                if i == 1:
                    act.wait_ge(once["load"], 16 * N_LOADS)
                    act.activation(Wf[:, :, 0].rearrange("p w k d -> p w (k d)"),
                                   stage_flat[:, 0:len(FLAT) * FLAT_N].rearrange("p (w n) -> p w n", n=FLAT_N), ACT.Copy, scale=WS).then_inc(once["act"], 1)
                if i == 2:
                    act.activation(Wp[:, :, 0].rearrange("p w k d -> p w (k d)"), stage_pad.rearrange("p (w n) -> p w n", n=PAD_N),
                                   ACT.Copy, scale=WS).then_inc(once["act"], 1)
            act.wait_ge(once["lambda"], 1)
            act.activation(lamt[:, 2:4], lamt[:, 0:2], ACT.Exp).then_inc(once["act"], 1)
            act.wait_ge(once["pe"], 2)
            act.activation(rows_e, PS[:, :, 0:D + 1], ACT.Copy).then_inc(once["act"], 1)
            act.wait_ge(once["pe"], 3)
            act.activation(RT[:].rearrange("p m d -> p (m d)"), flat[:, 0:NM * D], ACT.Copy).then_inc(once["act"], 1)
            batch_end(act, "act")

            with act.Fori(0, NB):
                def norm_std(N):
                    act.wait_ge(*of("dve", N, "mv"))
                    act.activation(sd[:], mv[:, :, 1], ACT.Sqrt, bias=epsc[:, 0:1], scale=1.0).then_inc(*did("act", N, "sd"))

                def both(slot_):
                    return slot_.rearrange("p (k c) -> p k c", k=KD)

                def x_hi(N):
                    for c in range(2):
                        act.wait_ge(*of("pe", "T", N, c))
                        act.activation(XT[:, 0, :, c * CH:(c + 1) * CH], both(slot("T", N, c)), ACT.Copy).then_inc(*did("act", N, "xhi", c))

                def x_affine(N, g_, b_):
                    for c in range(2):
                        act.wait_ge(*of("pe", "T", N, c))
                        if c:
                            act.wait_ge(*of("dve", N, "xlo", c - 1))
                        for k in range(KD):
                            act.activation(tmp[:, k * CH:(k + 1) * CH], slot("T", N, c)[:, k * CH:(k + 1) * CH], ACT.Identity,
                                           bias=BC[:, bc[b_] + k:bc[b_] + k + 1], scale=BC[:, bc[g_] + k:bc[g_] + k + 1]
                                           ).then_inc(*(frees("act", "T", N, c) if k else did("act", N, "x0", c)))

                def q_f32(L, own):
                    before = None
                    for m in range(KD):
                        for n in ("q", "k") if own else ("q",):
                            act.wait_ge(*of("pe", L, n, m))
                            if before:
                                act.wait_ge(*of("dve", L, *before))
                            before = (n + "lo", m)
                            name = L + n
                            b = BC[:, bc[name] + m:bc[name] + m + 1] if name in bc else epsc[:, 1:2]
                            act.activation(tmp, slot(L, n, m), ACT.Identity, bias=b,
                                           scale=(0.25 if n == "q" else 1.0) / WS).then_inc(*frees("act", L, n, m))

                act.activation(CT[:, 0, :, 0:TC], CTf[:], ACT.Copy).then_inc(*did("act", "cthi"))
                norm_std("A")
                x_hi("A")
                act.wait_ge(*of("pe", "K0"))
                act.activation(KP0[:, 0, 0:TC], slot("K0")[:, 0:TC], ACT.Copy, scale=1.0 / WS).then_inc(*did("act", "kp0hi"))
                act.wait_ge(*of("pe", "V0"))
                act.activation(VP0[0:TC, 0, :], slot("V0")[0:TC, 0:D], ACT.Copy, scale=1.0 / WS).then_inc(*did("act", "vp0hi"))
                for l, L in enumerate(XL):
                    for m in range(KD):
                        act.wait_ge(*of("pe", "KX", l, m))
                        b = BC[:, bc[L + "k"] + m:bc[L + "k"] + m + 1] if L != "C1" else epsc[:, 1:2]
                        act.activation(kxf[:, l, m, 0:TC], slot("KX", l, m)[:, 0:TC], ACT.Identity, bias=b,
                                       scale=1.0 / WS).then_inc(*frees("act", "KX", l, m))
                    act.wait_ge(*of("pe", "VX", l))
                    act.activation(VX[0:TC, l, :, 0:DH], slot("VX", l)[0:TC, 0:D].rearrange("p (h d) -> p h d", d=DH), ACT.Copy,
                                   scale=1.0 / WS).then_inc(*frees("act", "VX", l))

                for h in range(2):
                    act.wait_ge(*of("pe", "A", "Q", h))
                    act.activation(q0[:, 0, h], slot("A", "Q", h), ACT.Copy, scale=float(P) ** -0.5 / WS).then_inc(*did("act", "A", "qhi", h))
                for t in range(NT):
                    act.wait_ge(*of("dve", "A", "m", t))
                    if t >= 2:
                        act.wait_ge(*of("dve", "A", "p", t - 2))
                    for h in range(2):
                        act.activation(E0[:, t % 2, h], slot("A", "S", t)[:, h * TC:(h + 1) * TC], ACT.Exp, bias=sm[:, 2 * t + h:2 * t + h + 1],
                                       scale=1.0, accum_out=sm[:, 16 + 2 * t + h:17 + 2 * t + h]
                                       ).then_inc(*(frees("act", "A", "S", t) if h else did("act", "A", "e0", t)))
                act.wait_ge(*of("pe", "A", "PT"))
                act.activation(AT0[0:TC, 0, :], slot("A", "PT")[0:TC], ACT.Copy).then_inc(*did("act", "A", "pthi"))
                for m in range(KD):
                    act.wait_ge(*of("pe", "A", "O", m))
                    act.activation(AO0[:, 0, m], slot("A", "O", m), ACT.Copy).then_inc(*did("act", "A", "ohi", m))
                for t in range(NT):
                    act.wait_ge(*of("pe", "A", "N", t))
                    if t >= 2:
                        act.wait_ge(*of("act", "free", "A", "N", t - 2))
                    act.activation(sq0[:, t % 2], slot("A", "N", t)[:, 0:D], ACT.Square,
                                   accum_out=sm[:, 64 + t:65 + t]).then_inc(*frees("act", "A", "N", t))
                act.wait_ge(*of("act", "free", "A", "N", NT - 1))
                act.activation(sm[:, 72:80], sm[:, 64:72], ACT.Sqrt, bias=epsc[:, 0:1], scale=1.0 / D).then_inc(*did("act", "A", "rms"))

                def exps(L, own, steps):
                    n = 0
                    probs, np_ = (PR, NP) if own else (PRX, NPX)
                    for step in steps:
                        if step[0] == "ST":
                            _, g, kt, j = step
                            act.wait_ge(*of("pe", L, "ST", g, kt, j))
                            if n >= np_:
                                g0, k0, j0 = [s[1:] for s in steps if s[0] == "ST"][n - np_]
                                act.wait_ge(*of("pe", L, "PV", g0, k0, 1))
                            rows = P if own else TX
                            act.activation(probs[0:rows, n % np_, kt * P:T], slot(L, "ST", g, kt, j)[0:rows, kt * P:T],
                                           ACT.Exp).then_inc(*did("act", L, "exp", g, kt, j))
                            led.freed[(L, "ST", g, kt, j)] = ("act", (L, "exp", g, kt, j))
                            n += 1
                        elif step[0] == "PV" and step[2:] == (NT - 1 if own else 0, 1):
                            g = step[1]
                            act.wait_ge(*of("pe", L, "PV", g, step[2], 1))
                            if own and g >= 2:
                                act.wait_ge(*of("dve", L, "onf", g - 2))
                            for c in range(2):
                                act.activation(OT[own][g][:, c * CH:(c + 1) * CH], slot(L, "PVacc", g, c), ACT.Copy).then_inc(*did("act", L, "ot", g, c))
                                led.freed[(L, "PVacc", g, c)] = ("act", (L, "ot", g, c))

                def attention(L, own):
                    q_f32(L, own)
                    if own:
                        act.wait_ge(*of("dve", L, "ones"))
                        for t in range(NT):
                            act.wait_ge(*of("pe", L, "v", t))
                            act.activation(VP[:, t, :, 0:DH], slot(L, "v", t)[:, 0:D].rearrange("p (h d) -> p h d", d=DH), ACT.Copy,
                                           scale=1.0 / WS).then_inc(*did("act", L, "vp", t))
                            led.freed[(L, "v", t)] = ("act", (L, "vp", t))
                    exps(L, own, attention_steps(own))

                norm_std("B1")
                norm_std("B")
                x_affine("B", "ln1_g", "ln1_b")
                attention("B0", True)

                def weights_hi(e, w):
                    act.wait_ge(*of(f"ld_wexp{w}", e))
                    if e >= 2:
                        act.wait_ge(*of("pe", "M", "D", e - 2, 1, NM - 1))
                    act.activation(Wm[e % 2][:, w, 0], WSt[:, w], ACT.Copy, scale=WS).then_inc(*did("act", "M", "whi", e, w))

                weights_hi(0, 0)
                weights_hi(0, 1)
                norm_std("M")
                x_affine("M", "ln2_g", "ln2_b")
                n = 0
                for e in range(NE):
                    for c in range(2):
                        for m in range(NM):
                            act.wait_ge(*of("pe", "M", "U", e, c, m))
                            if n >= 3:
                                act.wait_ge(*of("dve", "M", "midlo", *back(e, c, m, 3)))
                            act.activation(midf[:, n % 3], slot("M", "U", e, c, m)[:, 0:CH], ACT.Gelu,
                                           bias=BC[:, BC_E1 + e * NM + m:BC_E1 + e * NM + m + 1],
                                           scale=1.0 / WS).then_inc(*frees("act", "M", "U", e, c, m))
                            n += 1
                            if (e, c, m) == (0, 0, 5):
                                act.wait_ge(*of("dve", "M", "d"))
                                act.activation(sm[:, 88:96], sm[:, 80:88], ACT.Exp).then_inc(*did("act", "M", "e"))
                            if e + 1 < NE and (c, m) in ((0, 4), (1, 0)):
                                weights_hi(e + 1, c)

                norm_std("C")
                x_hi("C")
                attention("C1", False)

                norm_std("L1")
                for k in range(KD):
                    act.wait_ge(*of("pe", "L1", "XQ", k))
                    act.activation(xqT[:, k], slot("L1", "XQ", k).bitcast(F16)[:, 0:T], ACT.Copy).then_inc(*did("act", "L1", "xqT", k))
                    led.freed[("L1", "XQ", k)] = ("act", ("L1", "xqT", k))
                for t in range(NT + 1):
                    if t < NT:
                        act.wait_ge(*of("dve", "L1", "h", t))
                        act.activation(hb[:, t % 3], hb[:, t % 3], ACT.Gelu).then_inc(*did("act", "L1", "gelu", t))
                    if t:
                        act.wait_ge(*of("dve", "L1", "hr2", t - 1))
                        if t >= 3:
                            act.wait_ge(*of("pe", "L1", "HQ", t - 3))
                        act.activation(hq[:, (t - 1) % 2], hr[:, (t - 1) % 2], ACT.Identity, bias=epsc[:, 2:3], scale=1.0
                                       ).then_inc(*did("act", "L1", "hq", t - 1))
                        act.wait_ge(*of("pe", "L1", "HQ", t - 1))
                        if t >= 3:
                            act.wait_ge(*of("pe", "L1", "H2", t - 3))
                        act.activation(hqT[:, (t - 1) % 2], slot("L1", "HQ", t - 1).bitcast(F16)[:, 0:HID], ACT.Copy
                                       ).then_inc(*did("act", "L1", "hqT", t - 1))
                        led.freed[("L1", "HQ", t - 1)] = ("act", ("L1", "hqT", t - 1))

                norm_std("D")
                x_hi("D")
                attention("D2", False)

                norm_std("L2")
                for c in range(2):
                    act.wait_ge(*of("pe", "T", "L2", c))
                    act.activation(XTf[:, :, c * CH:(c + 1) * CH], both(slot("T", "L2", c)), ACT.Copy).then_inc(*did("act", "L2", "xf", c))
                    led.freed[("T", "L2", c)] = ("act", ("L2", "xf", c))
                for c in range(2):
                    for m in range(NM):
                        act.wait_ge(*of("pe", "L2", "G", c, m))
                        act.activation(gT[:, c, m], slot("L2", "G", c, m)[:, 0:CH], ACT.Gelu, bias=upb[:, m:m + 1],
                                       scale=1.0).then_inc(*did("act", "L2", "g", c, m))
                        led.freed[("L2", "G", c, m)] = ("act", ("L2", "g", c, m))

                norm_std("E")
                x_hi("E")
                attention("E3", False)

                norm_std("F")
                x_hi("F")
                act.wait_ge(*of("dve", "F", "lmax"))
                act.activation(rt[0:1, 0:NH], rt[0:1, 0:NH], ACT.Exp, bias=rt[0:1, 24:25], scale=1.0,
                               accum_out=rt[0:1, 25:26]).then_inc(*did("act", "F", "e1"))
                act.wait_ge(*of("dve", "F", "index"))
                act.activation(rt[0:1, 40:44], rt[0:1, 28:32], ACT.Exp, bias=rt[0:1, 36:37], scale=1.0,
                               accum_out=rt[0:1, 44:45]).then_inc(*did("act", "F", "e2"))
                act.activation(rt[0:1, 45:46], rt[0:1, 36:37], ACT.Exp).then_inc(*did("act", "F", "e3"))
                act.wait_ge(*of("ld_sel", HS - 1, "bv"))
                for w in range(3):
                    act.activation(Wsel[:, w, 0], Wst[:, w], ACT.Copy, scale=WS).then_inc(*did("act", "F", "wsel_hi", w))
                act.wait_ge(*of("dve", "F", "qkscale"))
                before = None
                for m in range(KD):
                    for w, n in enumerate("qk"):
                        act.wait_ge(*of("pe", "F3", n, m))
                        if before:
                            act.wait_ge(*of("dve", "F3", *before))
                        before = (n + "lo", m)
                        act.activation(tmp, slot("F3", n, m), ACT.Identity, bias=bsel[:, 2 * m + w:2 * m + w + 1],
                                       scale=gcol[:, 4 + 2 * m + w:5 + 2 * m + w]).then_inc(*frees("act", "F3", n, m))
                act.wait_ge(*of("dve", "F3", "ones"))
                for t in range(NT):
                    act.wait_ge(*of("pe", "F3", "v", t))
                    act.activation(VP4[:, t, :, 0:DS], slot("F3", "v", t)[:, 0:D].rearrange("p (h d) -> p h d", d=DS), ACT.Copy,
                                   scale=1.0 / WS).then_inc(*did("act", "F3", "vp", t))
                    led.freed[("F3", "v", t)] = ("act", ("F3", "vp", t))
                act.wait_ge(*of("pe", "F3", "v", NT - 1))
                n = 0
                for step in last_attention_steps():
                    if step[0] == "ST":
                        _, h, kt = step
                        act.wait_ge(*of("pe", "F3", "ST", h, kt))
                        if n >= NP:
                            act.wait_ge(*of("pe", "F3", "PV", (n - NP) // NT, (n - NP) % NT, 1))
                        act.activation(PR4[:, n % NP], slot("F3", "ST", h, kt), ACT.Exp).then_inc(*did("act", "F3", "exp", h, kt))
                        led.freed[("F3", "ST", h, kt)] = ("act", ("F3", "exp", h, kt))
                        n += 1
                    elif step[0] == "PV" and step[2:] == (NT - 1, 1):
                        h = step[1]
                        act.wait_ge(*of("pe", "F3", "PV", h, NT - 1, 1))
                        if h >= 2:
                            act.wait_ge(*of("dve", "F3", "onf", h - 2))
                        for c in range(2):
                            act.activation(OT4[h % 2][:, c * CH:(c + 1) * CH], slot("F3", "PVacc", h, c)[0:TV], ACT.Copy
                                           ).then_inc(*did("act", "F3", "ot", h, c))
                            led.freed[("F3", "PVacc", h, c)] = ("act", ("F3", "ot", h, c))
                batch_end(act, "act")

        @block.gpsimd
        def _(pool):
            pool.memset(onesf[:], 1.0).then_inc(once["pool"], 1)
            pool.memset(VX[:], 0.0).then_inc(once["pool"], 1)
            pool.memset(mpart[:], -3.0e38).then_inc(once["pool"], 1)
            pool.wait_ge(once["pool"], 3)
            pool.memset(VX[0:TX, :, :, DH:QUARTER], 1.0).then_inc(once["pool"], 1)
            pool.wait_ge(once["low_w"], 32)
            pool.tensor_copy(low_down.rearrange("p k (m c) -> p (k m) c", c=P), identf[:].unsqueeze(1).broadcast_to([P, NM, P])).then_inc(once["pool"], 1)
            pool.wait_ge(once["pool"], 5)
            for i in range(LOW):
                pool.wait_ge(once["ring_down"], i + 1)
                butterfly(pool, once["down"], low_down, low_down_t, ring_down[:, i % 2], LOW - 1 - i, i, True)
            batch_end(pool, "pool")
            with pool.Fori(0, NB):
                batch_end(pool, "pool")

        @block.vector
        def _(dve):
            count = 0

            def then(ins, complete=True):
                nonlocal count
                ins.then_inc(once["dve"], 1)
                count += 1
                if complete:
                    dve.wait_ge(once["dve"], count)

            def low_stage(i):
                dve.wait_ge(once["ring_up"], i + 1)
                butterfly(dve, once["up"], low_up, low_up_t, ring_up[:, i % 2], i, i, False)

            n_high = 0

            def high_stage(rows, e, s, turned, first):
                nonlocal n_high
                d = 2 ** s
                pairs = [(q // d * 2 * d + q % d, q // d * 2 * d + q % d + d) for q in range(NM // 2)]
                w = high_w[:, e, s]
                n = rows.shape[2]
                if not first:
                    dve.wait_ge(once["high"], n_high)
                for q, (a, b_) in enumerate(pairs):
                    dve.tensor_scalar(high_t[:, 0, q, 0:n], rows[:, a], w[:, q, 0:1], None, ALU.mult).then_inc(once["high"], 1)
                    c = 1 if turned else 2
                    dve.tensor_scalar(high_t[:, 1, q, 0:n], rows[:, a], w[:, q, c:c + 1], None, ALU.mult).then_inc(once["high"], 1)
                dve.wait_ge(once["high"], n_high + 8)
                for q, (a, b_) in enumerate(pairs):
                    c = 2 if turned else 1
                    dve.scalar_tensor_tensor(rows[:, a], rows[:, b_], w[:, q, c:c + 1], high_t[:, 0, q, 0:n], ALU.mult, ALU.add).then_inc(once["high"], 1)
                n_high += 12
                dve.wait_ge(once["high"], n_high)
                for q, (a, b_) in enumerate(pairs):
                    dve.scalar_tensor_tensor(rows[:, b_], rows[:, b_], w[:, q, 3:4], high_t[:, 1, q, 0:n], ALU.mult, ALU.add).then_inc(once["high"], 1)
                n_high += 4

            dve.wait_ge(once["low_w"], 32)
            then(dve.tensor_copy(low_up.rearrange("p k (m c) -> p (k m) c", c=P), identf[:].unsqueeze(1).broadcast_to([P, NM, P])))
            low_stage(0)
            low_stage(1)
            dve.wait_ge(once["load"], 16 * N_LOADS)
            pr = lamr[:, 4 * P:6 * P].rearrange("p (a c) -> p a c", a=2)
            q_k = lamr[:, 0:4 * P].rearrange("p (a b c) -> p a b c", a=2, b=2)
            then(dve.tensor_tensor(pr, q_k[:, :, 0], q_k[:, :, 1], ALU.mult))
            dve.tensor_reduce(lamt[:, 0:2], pr, AX, ALU.add).then_inc(once["lambda"], 1)
            for w in range(len(CTXW)):
                if w >= 4:
                    dve.wait_ge(once[f"store{w % 4}"], 16)
                src = stage_flat[:, (len(FLAT) + w) * FLAT_N:(len(FLAT) + w + 1) * FLAT_N]
                dst = ctx_split[:, (w % 4) * 2 * FLAT_N:(w % 4 + 1) * 2 * FLAT_N]
                then(dve.tensor_scalar(dst[:, 0:FLAT_N], src, WS, None, ALU.mult))
                dve.scalar_tensor_tensor(dst[:, FLAT_N:2 * FLAT_N], src, WS, dst[:, 0:FLAT_N], ALU.mult, ALU.subtract).then_inc(once["ctxw"], 1)
                if w in (3, 7):
                    low_stage(2 + w // 4)
            dve.wait_ge(once["act"], 1)
            then(dve.scalar_tensor_tensor(Wf[:, :, 1].rearrange("p w k d -> p w (k d)"),
                                          stage_flat[:, 0:len(FLAT) * FLAT_N].rearrange("p (w n) -> p w n", n=FLAT_N), WS,
                                          Wf[:, :, 0].rearrange("p w k d -> p w (k d)"), ALU.mult, ALU.subtract))
            low_stage(4)
            dve.wait_ge(once["act"], 2)
            then(dve.scalar_tensor_tensor(Wp[:, :, 1].rearrange("p w k d -> p w (k d)"), stage_pad.rearrange("p (w n) -> p w n", n=PAD_N), WS,
                                          Wp[:, :, 0].rearrange("p w k d -> p w (k d)"), ALU.mult, ALU.subtract))
            then(dve.memset(BR[:], 0.0))
            nb = len(BROW)
            then(dve.tensor_scalar(BR[0:nb, 0], brf[0:nb], WS, None, ALU.mult))
            then(dve.scalar_tensor_tensor(BR[0:nb, 1], brf[0:nb], WS, BR[0:nb, 0], ALU.mult, ALU.subtract))
            dve.memset(rt[0:1, 95:96], 0.0).then_inc(once["staged"], 1)
            high_stage(rows_c, 1, 2, True, True)
            low_stage(5)
            high_stage(rows_c, 1, 1, True, False)
            dve.tensor_reduce(wsc[:, 0:1], fW1, AX, ALU.add, apply_absolute_value=True).then_inc(once["wsum"], 1)
            dve.tensor_reduce(wsc[:, 1:2], fW2, AX, ALU.add, apply_absolute_value=True).then_inc(once["wsum"], 1)
            low_stage(6)
            high_stage(rows_c, 1, 0, True, False)
            gw = gwf[:, :].rearrange("p (k n) -> p k n", k=KD)
            then(dve.tensor_scalar(gateW[:, 0], gw, WS, None, ALU.mult))
            then(dve.scalar_tensor_tensor(gateW[:, 1], gw, WS, gateW[:, 0], ALU.mult, ALU.subtract))
            for n in ("B0q", "D2q", "E3q"):
                then(dve.tensor_scalar(BC[:, bc[n]:bc[n] + 2], BC[:, bc[n]:bc[n] + 2], 0.25, None, ALU.mult))
            then(dve.tensor_scalar(big[:], ident[:], BIG, None, ALU.mult))
            then(dve.tensor_scalar(small[:], ident[:], 1.0 / WS, None, ALU.mult))
            dve.wait_ge(once["act"], 3)
            then(dve.tensor_tensor(lamt[:, 4:5], lamt[:, 3:4], lamt[:, 2:3], ALU.subtract))
            then(dve.tensor_scalar(lamt[:, 5:6], lamt[:, 4:5], -LAM0, None, ALU.add))

            dve.wait_ge(once["pe"], 1)
            then(dve.tensor_scalar(wsc[:, 2:4], SLOT["S0"][:, 0:2], 1.0 / (HID * D), EPS, ALU.mult, ALU.max))
            then(dve.reciprocal(wsc[:, 4:6], wsc[:, 2:4]))
            for i, (f, w) in enumerate(((fW1, Wq1[:, :, :].rearrange("p k n -> p (k n)")), (fW2, Wq2[:, :, :].rearrange("p k n -> p (k n)")))):
                then(dve.tensor_scalar(f, f, wsc[:, 4 + i:5 + i], MAGIC, ALU.mult, ALU.add))
                then(dve.tensor_scalar(f, f, -MAGIC, 1.0, ALU.add, ALU.min))
                then(dve.tensor_scalar(w, f, -1.0, None, ALU.max))
            dve.tensor_scalar(wsc[:, 2:4], wsc[:, 2:4], 1.0 / QB, None, ALU.mult).then_inc(once["ternary"], 1)
            dve.wait_ge(once["act"], 4)
            dve.memset(rt[0:1, 95:96], 0.0).then_inc(once["high"], 1)
            n_high += 1
            for s in range(HIGH):
                high_stage(rows_e, 0, s, False, False)
            dve.wait_ge(once["high"], n_high)
            then(dve.tensor_tensor(upb[:], rows_e[:, :, D], BC[:, BC_UP:BC_UP + NM], ALU.add))
            dve.wait_ge(once["pe"], 4)
            then(dve.tensor_copy(Wexp[:].rearrange("p k n -> p (k n)"), flat[:, 2 * HID:4 * HID]))
            batch_end(dve, "dve")

            with dve.Fori(0, NB):
                def step(*key):
                    return did("dve", *key)

                begun = set()

                def statistics(N, src, t, written):
                    begun.add(N)
                    if t >= 0:
                        dve.wait_ge(*of("dve", *written, t))
                        if N:
                            dve.bn_stats(stats[:, t], src[:, t]).then_inc(*step(N, "bn", t))

                def norm(N, src, dst):
                    if N not in begun:
                        for t in range(NT):
                            dve.bn_stats(stats[:, t], src[:, t]).then_inc(*step(N, "bn", t))
                    for t in range(NT):
                        dve.wait_ge(*of("dve", N, "bn", t))
                        dve.bn_aggr(mv[:, t], stats[:, t]).then_inc(*(step(N, "mv") if t == NT - 1 else step(N, "ag", t)))
                    dve.wait_ge(*of("act", N, "sd"))
                    dve.reciprocal(rstd[:], sd[:]).then_inc(*step(N, "rstd"))
                    dve.wait_ge(*of("dve", N, "rstd"))
                    for t in range(NT):
                        dve.tensor_scalar(dst[:, t], src[:, t], mv[:, t, 0:1], rstd[:, t:t + 1], ALU.subtract, ALU.mult).then_inc(*step(N, "xn", t))

                def both(slot_):
                    return slot_.rearrange("p (k c) -> p k c", k=KD)

                def x_lo(N):
                    for c in range(2):
                        dve.wait_ge(*of("act", N, "xhi", c))
                        if N == "F":
                            dve.tensor_reduce(xmean[:, c], both(slot("T", N, c)), AX, ALU.add).then_inc(*step(N, "xmean", c))
                        half = slice(c * CH, (c + 1) * CH)
                        dve.tensor_tensor(XT[:, 1, :, half], both(slot("T", N, c)), XT[:, 0, :, half], ALU.subtract).then_inc(*step(N, "xlo", c))
                        led.freed[("T", N, c)] = ("dve", (N, "xlo", c))

                def halves(src, hi, lo, ready, key):
                    dve.wait_ge(*ready)
                    dve.tensor_copy(hi, src).then_inc(*step(*key, "hi"))
                    dve.wait_ge(*of("dve", *key, "hi"))
                    dve.tensor_tensor(lo, src, hi, ALU.subtract).then_inc(*step(*key))

                def x_affine(N):
                    for c in range(2):
                        half = slice(c * CH, (c + 1) * CH)
                        halves(both(tmp), XT[:, 0, :, half], XT[:, 1, :, half], of("act", "free", "T", N, c), (N, "xlo", c))

                dve.tensor_scalar(maskb[:, :, 0:TC], maskr[:, 0:TC].unsqueeze(1).broadcast_to([1, NH, TC]), 0.0, -BIG, ALU.is_gt, ALU.mult).then_inc(*step("mask"))
                norm("A", H, XN["A"])
                dve.wait_ge(*of("act", "cthi"))
                dve.tensor_tensor(CT[:, 1, :, 0:TC], CTf[:], CT[:, 0, :, 0:TC], ALU.subtract).then_inc(*step("ctlo"))
                x_lo("A")
                dve.wait_ge(*of("act", "kp0hi"))
                dve.scalar_tensor_tensor(KP0[:, 1, 0:TC], slot("K0")[:, 0:TC], 1.0 / WS, KP0[:, 0, 0:TC], ALU.mult, ALU.subtract).then_inc(*step("A", "kp0"))
                led.freed[("K0",)] = ("dve", ("A", "kp0"))
                dve.wait_ge(*of("act", "vp0hi"))
                dve.scalar_tensor_tensor(VP0[0:TC, 1], slot("V0")[0:TC, 0:D], 1.0 / WS, VP0[0:TC, 0], ALU.mult, ALU.subtract).then_inc(*step("A", "vp0"))
                led.freed[("V0",)] = ("dve", ("A", "vp0"))
                dve.wait_ge(*of("act", "free", "KX", len(XL) - 1, KD - 1))
                for s in range(2):
                    if s:
                        dve.wait_ge(*of("dve", "kxhi"))
                        dve.tensor_tensor(kxs[:, 1, :, :, 0:TC], kxf[:, :, :, 0:TC], kxs[:, 0, :, :, 0:TC], ALU.subtract).then_inc(*step("kxs"))
                    else:
                        dve.tensor_copy(kxs[:, 0, :, :, 0:TC], kxf[:, :, :, 0:TC]).then_inc(*step("kxhi"))

                for h in range(2):
                    dve.wait_ge(*of("act", "A", "qhi", h))
                    dve.scalar_tensor_tensor(q0[:, 1, h], slot("A", "Q", h), float(P) ** -0.5 / WS, q0[:, 0, h], ALU.mult,
                                             ALU.subtract).then_inc(*step("A", "qlo", h))
                    led.freed[("A", "Q", h)] = ("dve", ("A", "qlo", h))
                for t in range(NT + 1):
                    if t < NT:
                        dve.wait_ge(*of("pe", "A", "S", t))
                        dve.tensor_reduce(sm[:, 2 * t:2 * t + 2], slot("A", "S", t)[:, 0:2 * TC].rearrange("p (h c) -> p h c", h=2), AX, ALU.max,
                                          negate=True).then_inc(*step("A", "m", t))
                    if t:
                        u = t - 1
                        dve.wait_ge(*of("act", "free", "A", "S", u))
                        dve.reciprocal(sm[:, 32 + 2 * u:34 + 2 * u], sm[:, 16 + 2 * u:18 + 2 * u]).then_inc(*step("A", "r", u))
                        dve.wait_ge(*of("dve", "A", "r", u))
                        dve.tensor_tensor(sm[:, 48 + u:49 + u], sm[:, 33 + 2 * u:34 + 2 * u], lamt[:, 5:6], ALU.mult).then_inc(*step("A", "r1", u))
                        dve.wait_ge(*of("dve", "A", "r1", u))
                        dve.tensor_scalar(A0[:, u], E0[:, u % 2, 1], sm[:, 48 + u:49 + u], None, ALU.mult).then_inc(*step("A", "p1", u))
                        dve.wait_ge(*of("dve", "A", "p1", u))
                        dve.scalar_tensor_tensor(A0[:, u], E0[:, u % 2, 0], sm[:, 32 + 2 * u:33 + 2 * u], A0[:, u], ALU.mult,
                                                 ALU.add).then_inc(*step("A", "p", u))
                dve.wait_ge(*of("act", "A", "pthi"))
                dve.tensor_tensor(AT0[0:TC, 1], slot("A", "PT")[0:TC], AT0[0:TC, 0], ALU.subtract).then_inc(*step("A", "ptlo"))
                led.freed[("A", "PT")] = ("dve", ("A", "ptlo"))
                for m in range(KD):
                    dve.wait_ge(*of("act", "A", "ohi", m))
                    dve.tensor_tensor(AO0[:, 1, m], slot("A", "O", m), AO0[:, 0, m], ALU.subtract).then_inc(*step("A", "olo", m))
                    led.freed[("A", "O", m)] = ("dve", ("A", "olo", m))
                dve.wait_ge(*of("act", "A", "rms"))
                dve.reciprocal(sm[:, 120:128], sm[:, 72:80]).then_inc(*step("A", "rr"))
                dve.wait_ge(*of("dve", "A", "rr"))
                dve.tensor_scalar(sm[:, 128:136], sm[:, 120:128], (1.0 - LAM0) / WS, None, ALU.mult).then_inc(*step("A", "rw"))
                dve.wait_ge(*of("dve", "A", "rw"))
                for t in range(NT):
                    dve.wait_ge(*of("pe", "A", "W", t))
                    dve.scalar_tensor_tensor(X[:, t], slot("A", "W", t)[:, 0:D], sm[:, 128 + t:129 + t], H[:, t], ALU.mult,
                                             ALU.add).then_inc(*step("A", "x", t))
                    led.freed[("A", "W", t)] = ("dve", ("A", "x", t))
                    statistics("B1", X, t - 1, ("A", "x"))
                statistics("B1", X, NT - 1, ("A", "x"))

                def maxima(L, own, step_):
                    g, t = step_[1:3]
                    last = None
                    if own:
                        j = step_[3]
                        for c in range(((t + 1) * P + CH - 1) // CH):
                            n = min(CH, (t + 1) * P - c * CH)
                            dve.wait_ge(*of("pe", L, "S", g, t, j, c))
                            dve.tensor_reduce(mpart[:, j * NT + t, c:c + 1], slot(L, "S", g, t, j, c)[:, 0:n], AX,
                                              ALU.max).then_inc(*frees("dve", L, "S", g, t, j, c))
                            last = (L, "S", g, t, j, c)
                    else:
                        dve.wait_ge(*of("pe", L, "S", g, t))
                        mine = negp[g // 2][:, (g % 2) * GH * NT:(g % 2 + 1) * GH * NT]
                        dve.tensor_reduce(mine.rearrange("p (j t) -> p j t", t=NT)[:, :, t],
                                          slot(L, "S", g, t)[:, 0:GH * TX].rearrange("p (j c) -> p j c", c=TX), AX, ALU.max,
                                          negate=True).then_inc(*frees("dve", L, "S", g, t))
                        last = (L, "S", g, t)
                    return last

                def minus_max_rows(L, g, last, n):
                    if n:
                        dve.wait_ge(*of("dve", "free", *last))
                        dve.tensor_reduce(negm[:, g % 2, 0:n], mpart[:, 0:n], AX, ALU.max, negate=True).then_inc(*step(L, "negm", g))

                def minus_max_parts(L, g, n):
                    dve.wait_ge(*of("pe", L, "MT", g))
                    if g >= 2:
                        dve.wait_ge(*of(f"ld_m{g % 2}", L, g - 2, 1))
                    dve.tensor_copy(mrow[0:n, g % 2, 0], slot(L, "MT", g)[0:n, 0:P]).then_inc(*step(L, "mhi", g))
                    dve.wait_ge(*of("dve", L, "mhi", g))
                    dve.tensor_tensor(mrow[0:n, g % 2, 1], slot(L, "MT", g)[0:n, 0:P], mrow[0:n, g % 2, 0], ALU.subtract).then_inc(*step(L, "mrow", g))
                    led.freed[(L, "MT", g)] = ("dve", (L, "mrow", g))

                def inverse_sums(L, g, w):
                    dve.wait_ge(*of(f"ld_s{g}", L))
                    dve.reciprocal(rinv[:, g, 0:w], rsum[:, g, 0:w]).then_inc(*step(L, "rinv", g))

                def normalised(L, own, g):
                    dve.wait_ge(*of("pe", L, "NB", g))
                    dve.tensor_tensor(tmp, OT[own][g], slot(L, "NB", g), ALU.mult).then_inc(*step(L, "onf", g))
                    led.freed[(L, "NB", g)] = ("dve", (L, "onf", g))
                    halves(tmp, ON[:, 0, g], ON[:, 1, g], of("dve", L, "onf", g), (L, "onlo", g))
                    dve.wait_ge(*of("dve", L, "onlo", g))

                def attention(L, own, dst, follows):
                    if own:
                        dve.memset(VP[:, :, :, DH:QUARTER], 1.0).then_inc(*step(L, "ones"))
                    for m in range(KD):
                        halves(tmp, qhl[:, 0, m], qhl[:, 1, m], of("act", "free", L, "q", m), (L, "qlo", m))
                        if own:
                            halves(tmp, khl[:, 0, m], khl[:, 1, m], of("act", "free", L, "k", m), (L, "klo", m))
                    steps = attention_steps(own)
                    last = None
                    for i, s in enumerate(steps):
                        if s[0] == "S":
                            last = maxima(L, own, s)
                        elif s[0] == "MT":
                            minus_max_rows(L, s[1], last, GH * NT if own else 0)
                            minus_max_parts(L, s[1], GH * NT)
                        elif s[0] == "NB":
                            normalised(L, own, s[1])
                        elif s[0] == "RINV":
                            inverse_sums(L, s[1], QUARTER)
                    residual(L, dst, follows)

                def residual(L, dst, follows):
                    begun.add(follows)

                    def pair_statistics(p):
                        dve.wait_ge(*of("dve", L, "x", p))
                        for t in (2 * p, 2 * p + 1):
                            if follows:
                                dve.bn_stats(stats[:, t], dst[:, t]).then_inc(*step(follows, "bn", t))

                    for p in range(NT // 2):
                        dve.wait_ge(*of("pe", L, "W", p))
                        pair = dst[:, 2 * p:2 * p + 2].rearrange("p t d -> p (t d)")
                        dve.scalar_tensor_tensor(pair, slot(L, "W", p), 1.0 / WS, pair, ALU.mult, ALU.add).then_inc(*step(L, "x", p))
                        led.freed[(L, "W", p)] = ("dve", (L, "x", p))
                        if p:
                            pair_statistics(p - 1)
                    pair_statistics(NT // 2 - 1)

                dve.wait_ge(*of("ld_kx", "mask"))
                norm("B1", X, H)
                dve.wait_ge(*of("dve", "B1", "xn", NT - 1))
                norm("B", H, XN["B"])
                x_affine("B")
                attention("B0", True, H, "M")

                norm("M", H, XN["M"])

                def weights_lo(e, w):
                    dve.wait_ge(*of("act", "M", "whi", e, w))
                    dve.scalar_tensor_tensor(Wm[e % 2][:, w, 1], WSt[:, w], WS, Wm[e % 2][:, w, 0], ALU.mult, ALU.subtract).then_inc(*step("M", "wlo", e, w))

                weights_lo(0, 0)
                x_affine("M")
                weights_lo(0, 1)
                lg = sm[:, 0:64].rearrange("p (t e) -> p t e", e=NE)

                def best_two():
                    dve.wait_ge(*of("pe", "M", "gate"))
                    dve.scalar_tensor_tensor(lg, slot("M", "gate")[:, 0:NT * NE].rearrange("p (t e) -> p t e", e=NE), 1.0 / WS,
                                             gateb[:].unsqueeze(1).broadcast_to([P, NT, NE]), ALU.mult, ALU.add).then_inc(*frees("dve", "M", "gate"))
                    dve.wait_ge(*of("dve", "free", "M", "gate"))
                    for t in range(NT):
                        dve.max(maxv[:, t], lg[:, t]).then_inc(*step("M", "top", t))
                    for t in range(NT):
                        dve.wait_ge(*of("dve", "M", "top", t))
                        dve.max_index(maxi[:, t], maxv[:, t], lg[:, t]).then_inc(*step("M", "idx", t))
                    dve.tensor_tensor(sm[:, 80:88], maxv[:, :, 1], maxv[:, :, 0], ALU.subtract).then_inc(*step("M", "d"))

                def gate_weights():
                    dve.wait_ge(*of("act", "M", "e"))
                    dve.tensor_scalar(sm[:, 96:104], sm[:, 88:96], WS, WS, ALU.mult, ALU.add).then_inc(*step("M", "den"))
                    dve.wait_ge(*of("dve", "M", "den"))
                    dve.reciprocal(sm[:, 104:112], sm[:, 96:104]).then_inc(*step("M", "w1"))
                    dve.wait_ge(*of("dve", "M", "w1"))
                    dve.tensor_tensor(sm[:, 112:120], sm[:, 88:96], sm[:, 104:112], ALU.mult).then_inc(*step("M", "w2"))
                    dve.tensor_copy(sm[:, 64:80].rearrange("p (t i) -> p t i", i=2), maxi[:, :, 0:2]).then_inc(*step("M", "idxf"))
                    dve.wait_ge(*of("dve", "M", "idxf"))
                    io = iota[:].unsqueeze(1).broadcast_to([P, NT, NE])
                    ix = sm[:, 64:80].rearrange("p (t i) -> p t i", i=2)
                    for i, dst in enumerate((wfull[:], lg)):
                        dve.tensor_tensor(dst, io, ix[:, :, i:i + 1].broadcast_to([P, NT, NE]), ALU.is_equal).then_inc(*step("M", "eq", i))
                        dve.wait_ge(*of("dve", "M", "eq", i))
                        dve.tensor_tensor(dst, dst, sm[:, 104 + 8 * i:112 + 8 * i].unsqueeze(2).broadcast_to([P, NT, NE]), ALU.mult).then_inc(*step("M", "wm", i))
                        dve.wait_ge(*of("dve", "M", "wm", i))
                    dve.tensor_tensor(wfull[:], wfull[:], lg, ALU.add).then_inc(*step("M", "wfull"))
                    dve.wait_ge(*of("dve", "M", "wfull"))

                def expert_out(e, c):
                    for i in range(4):
                        dve.wait_ge(*of("pe", "M", "D", e, c, NM - 1))
                        t = 4 * c + i
                        last = e == NE - 1
                        if e:
                            dve.wait_ge(*of("dve", "M", *(("xh", t) if last else ("h", e - 1, t))))
                        key = ("M", "x", t) if last else ("M", "h", e, t)
                        sum_ = (X if last else H)[:, t]
                        dve.scalar_tensor_tensor(sum_, slot("M", "D", e, c, i // 2)[:, (i % 2) * D:(i % 2 + 1) * D], wfull[:, t, e:e + 1],
                                                 sum_, ALU.mult, ALU.add).then_inc(*step(*key))
                        if i % 2:
                            led.freed[("M", "D", e, c, i // 2)] = ("dve", key)
                    if e == NE - 1:
                        for i in range(4):
                            statistics("C", X, 4 * c + i, ("M", "x"))

                n = 0
                for e in range(NE):
                    for c in range(2):
                        for m in range(NM):
                            if n >= 4:
                                dve.wait_ge(*of("pe", "M", "D", *back(e, c, m, 4)))
                            halves(midf[:, n % 3], mid[:, n % 4, 0], mid[:, n % 4, 1], of("act", "free", "M", "U", e, c, m), ("M", "midlo", e, c, m))
                            n += 1
                            if e + 1 < NE and (c, m) in ((0, 5), (1, 1)):
                                weights_lo(e + 1, c)
                            if (e, c, m) == (0, 0, 3):
                                best_two()
                            if (e, c, m) == (0, 0, 6):
                                gate_weights()
                            if m == 3 and (e, c) != (0, 0):
                                expert_out(*back(e, c, 0, 1)[:2])
                            if (e, c, m) == (NE - 1, 0, 5):
                                for t in range(NT):
                                    dve.wait_ge(*of("dve", "M", "h", NE - 2, t))
                                    dve.tensor_tensor(X[:, t], X[:, t], H[:, t], ALU.add).then_inc(*step("M", "xh", t))
                expert_out(NE - 1, 1)

                norm("C", X, XN["C"])
                x_lo("C")
                attention("C1", False, X, "L1")

                norm("L1", X, XN["L1"])
                dve.wait_ge(*of("dve", "L1", "xn", NT - 1))
                dve.tensor_reduce(sm[:, 0:8], XN["L1"], AX, ALU.max, apply_absolute_value=True).then_inc(*step("L1", "amax"))
                dve.wait_ge(*of("dve", "L1", "amax"))
                dve.tensor_scalar(sm[:, 0:8], sm[:, 0:8], EPS, None, ALU.max).then_inc(*step("L1", "xs"))
                dve.wait_ge(*of("dve", "L1", "xs"))
                dve.reciprocal(sm[:, 8:16], sm[:, 0:8]).then_inc(*step("L1", "xr"))
                dve.wait_ge(*of("dve", "L1", "xr"))
                dve.tensor_scalar(sm[:, 16:24], sm[:, 8:16], QB, None, ALU.mult).then_inc(*step("L1", "xm"))
                dve.tensor_scalar(sm[:, 24:32], sm[:, 0:8], wsc[:, 2:3], None, ALU.mult).then_inc(*step("L1", "xsc"))
                dve.wait_ge(*of("dve", "L1", "xsc"))
                for t in range(NT):
                    dve.tensor_scalar(XN["L1"][:, t], XN["L1"][:, t], sm[:, 16 + t:17 + t], MAGIC, ALU.mult, ALU.add).then_inc(*step("L1", "xr1", t))
                for t in range(NT):
                    dve.wait_ge(*of("dve", "L1", "xr1", t))
                    dve.tensor_scalar(XN["L1"][:, t], XN["L1"][:, t], -MAGIC, QB, ALU.add, ALU.min).then_inc(*step("L1", "xr2", t))
                for t in range(NT):
                    dve.wait_ge(*of("dve", "L1", "xr2", t))
                    dve.tensor_scalar(xq[:, t], XN["L1"][:, t], -QB - 1.0, None, ALU.max).then_inc(*step("L1", "xq", t))
                dve.wait_ge(*of("ld_b12", 1))

                def hidden(t):
                    dve.wait_ge(*of("pe", "L1", "H1", t))
                    if t >= 3:
                        dve.wait_ge(*of("dve", "L1", "hr1", t - 3))
                    dve.scalar_tensor_tensor(hb[:, t % 3], slot("L1", "H1", t), sm[:, 24 + t:25 + t], b1b, ALU.mult, ALU.add).then_inc(*step("L1", "h", t))
                    led.freed[("L1", "H1", t)] = ("dve", ("L1", "h", t))

                def quantise(t):
                    a, b_, c_ = 32 + t, 40 + t, 48 + t
                    dve.wait_ge(*of("act", "L1", "gelu", t))
                    dve.tensor_reduce(sm[:, a:a + 1], hb[:, t % 3], AX, ALU.max, apply_absolute_value=True).then_inc(*step("L1", "ha", t))
                    dve.wait_ge(*of("dve", "L1", "ha", t))
                    dve.tensor_scalar(sm[:, a:a + 1], sm[:, a:a + 1], EPS, None, ALU.max).then_inc(*step("L1", "hs", t))
                    dve.wait_ge(*of("dve", "L1", "hs", t))
                    dve.reciprocal(sm[:, b_:b_ + 1], sm[:, a:a + 1]).then_inc(*step("L1", "hrc", t))
                    dve.tensor_scalar(sm[:, c_:c_ + 1], sm[:, a:a + 1], wsc[:, 3:4], None, ALU.mult).then_inc(*step("L1", "hsc", t))
                    dve.wait_ge(*of("dve", "L1", "hrc", t))
                    dve.tensor_scalar(sm[:, 56 + t:57 + t], sm[:, b_:b_ + 1], QB, None, ALU.mult).then_inc(*step("L1", "hm", t))
                    dve.wait_ge(*of("dve", "L1", "hm", t))
                    if t >= 2:
                        dve.wait_ge(*of("act", "L1", "hq", t - 2))
                    dve.tensor_scalar(hr[:, t % 2], hb[:, t % 3], sm[:, 56 + t:57 + t], MAGIC, ALU.mult, ALU.add).then_inc(*step("L1", "hr1", t))
                    dve.wait_ge(*of("dve", "L1", "hr1", t))
                    dve.tensor_scalar(hr[:, t % 2], hr[:, t % 2], MAGIC - QB - 1.0, MAGIC + QB, ALU.max, ALU.min).then_inc(*step("L1", "hr2", t))

                def ternary_out(t):
                    dve.wait_ge(*of("pe", "L1", "H2", t))
                    dve.scalar_tensor_tensor(X[:, t], slot("L1", "H2", t)[:, 0:D], sm[:, 48 + t:49 + t], X[:, t], ALU.mult, ALU.add).then_inc(*step("L1", "x1", t))
                    led.freed[("L1", "H2", t)] = ("dve", ("L1", "x1", t))
                    dve.wait_ge(*of("dve", "L1", "x1", t))
                    dve.tensor_tensor(X[:, t], X[:, t], b2b, ALU.add).then_inc(*step("L1", "x", t))
                    statistics("D", X, t, ("L1", "x"))

                hidden(0)
                for t in range(NT):
                    if t + 1 < NT:
                        hidden(t + 1)
                    quantise(t)
                    if t:
                        ternary_out(t - 1)
                ternary_out(NT - 1)

                norm("D", X, XN["D"])
                x_lo("D")
                attention("D2", False, X, "L2")

                norm("L2", X, XN["L2"])
                for t in range(NT):
                    dve.wait_ge(*of("pe", "L2", "Y", t))
                    dve.tensor_tensor(X[:, t], X[:, t], slot("L2", "Y", t)[:, 0:D], ALU.add).then_inc(*step("L2", "x", t))
                    led.freed[("L2", "Y", t)] = ("dve", ("L2", "x", t))
                    statistics("E", X, t - 1, ("L2", "x"))
                statistics("E", X, NT - 1, ("L2", "x"))

                norm("E", X, XN["E"])
                x_lo("E")
                attention("E3", False, X, "F")

                norm("F", X, XN["F"])
                x_lo("F")

                def small_step(key, ins):
                    ins.then_inc(*step("F", key))
                    dve.wait_ge(*of("dve", "F", key))

                dve.wait_ge(*of("pe", "F", "R"))
                small_step("lg", dve.scalar_tensor_tensor(rt[0:1, 0:NH], slot("F", "R")[0:1, 0:NH], 1.0 / T, F3br[:], ALU.mult, ALU.add))
                led.freed[("F", "R")] = ("dve", ("F", "lg"))
                small_step("l8", dve.max(rt[0:1, 16:24], rt[0:1, 0:NH]))
                small_step("lmax", dve.tensor_scalar(rt[0:1, 24:25], rt[0:1, 16:17], -1.0, None, ALU.mult))
                dve.wait_ge(*of("act", "F", "e1"))
                small_step("r1", dve.reciprocal(rt[0:1, 26:27], rt[0:1, 25:26]))
                small_step("dist", dve.tensor_scalar(rt[0:1, 64:80], rt[0:1, 0:NH], rt[0:1, 26:27], None, ALU.mult))
                small_step("top", dve.max(rt[0:1, 28:36], rt[0:1, 64:80]))
                small_step("neg", dve.tensor_scalar(rt[0:1, 36:37], rt[0:1, 28:29], -1.0, None, ALU.mult))
                small_step("index", dve.max_index(rti[:], rt[0:1, 28:36], rt[0:1, 64:80]))
                dve.wait_ge(*of("act", "F", "e3"))
                small_step("den", dve.scalar_tensor_tensor(rt[0:1, 46:47], rt[0:1, 45:46], float(NH - HS), rt[0:1, 44:45], ALU.mult, ALU.add))
                small_step("rden", dve.reciprocal(rt[0:1, 47:48], rt[0:1, 46:47]))
                small_step("gates", dve.tensor_scalar(rt[0:1, 48:52], rt[0:1, 40:44], rt[0:1, 47:48], None, ALU.mult))
                dve.wait_ge(*of("pe", "F", "G"))
                small_step("gcol", dve.tensor_copy(gcol[:, 0:4], slot("F", "G")[:, 0:4]))
                led.freed[("F", "G")] = ("dve", ("F", "gcol"))
                for m in range(KD):
                    for i in range(2):
                        r = slice(DS * i, DS * (i + 1))
                        g_ = gcol[r, 2 * m + i:2 * m + i + 1]
                        small_step(("gq", m, i), dve.tensor_scalar(gcol[r, 4 + 2 * m:5 + 2 * m], g_, float(DS) ** -0.5 / WS, None, ALU.mult))
                        small_step(("gk", m, i), dve.tensor_scalar(gcol[r, 5 + 2 * m:6 + 2 * m], g_, 1.0 / WS, None, ALU.mult))
                dve.wait_ge(*of("ld_sel", HS - 1, "bv"))
                for w in range(3):
                    dve.wait_ge(*of("act", "F", "wsel_hi", w))
                    dve.scalar_tensor_tensor(Wsel[:, w, 1], Wst[:, w], WS, Wsel[:, w, 0], ALU.mult, ALU.subtract).then_inc(*step("F", "wsel_lo", w))
                small_step("bs", dve.tensor_scalar(bsel[:], bsel[:], WS, None, ALU.mult))
                small_step("qkscale", dve.tensor_tensor(bsel[:], bsel[:], gcol[:, 4:8], ALU.mult))
                small_step("bv_hi", dve.tensor_scalar(bvh[:, 0], bvr[:], WS, None, ALU.mult))
                small_step("bv_lo", dve.scalar_tensor_tensor(bvh[:, 1], bvr[:], WS, bvh[:, 0], ALU.mult, ALU.subtract))
                dve.memset(VP4[:, :, :, DS:TV], 1.0).then_inc(*step("F3", "ones"))
                for m in range(KD):
                    for n, hl in (("q", qhl), ("k", khl)):
                        halves(tmp, hl[:, 0, m], hl[:, 1, m], of("act", "free", "F3", n, m), ("F3", n + "lo", m))
                for s in last_attention_steps():
                    if s[0] == "S":
                        _, h, t, c = s
                        dve.wait_ge(*of("pe", "F3", "S", h, t, c))
                        dve.tensor_reduce(mpart[:, t, c:c + 1], slot("F3", "S", h, t, c), AX, ALU.max).then_inc(*frees("dve", "F3", "S", h, t, c))
                    elif s[0] == "MT":
                        h = s[1]
                        minus_max_rows("F3", h, ("F3", "S", h, NT - 1, 1), NT)
                        minus_max_parts("F3", h, NT)
                    elif s[0] == "RINV":
                        inverse_sums("F3", s[1], NT)
                    elif s[0] == "NB":
                        h = s[1]
                        dve.wait_ge(*of("pe", "F3", "NB", h))
                        dve.scalar_tensor_tensor(tmp[0:TV], OT4[h % 2], gcol[0:TV, h:h + 1], slot("F3", "NB", h)[0:TV], ALU.mult,
                                                 ALU.mult).then_inc(*step("F3", "onf", h))
                        led.freed[("F3", "NB", h)] = ("dve", ("F3", "onf", h))
                        halves(tmp[0:TV], ON4[:, 0, h], ON4[:, 1, h], of("dve", "F3", "onf", h), ("F3", "onlo", h))
                        dve.wait_ge(*of("dve", "F3", "onlo", h))
                dve.memset(mpart[:], -3.0e38).then_inc(*step("F3", "mpart"))
                residual("F3", X, None)
                dve.memset(rt[0:1, 95:96], 0.0).then_inc(*step("final"))
                batch_end(dve, "dve")
        return led


def halves_of(w):
    return w.reshape(KD, P, -1).transpose(1, 0, 2).reshape(P, -1)


def by_heads(w, heads, width, tall, groups):
    out = np.zeros((heads, tall, w.shape[1]), np.float32)
    out[:, :width] = w.reshape(heads, width, -1)
    return out.reshape(groups, -1, w.shape[1])


def with_next(a):
    return np.concatenate([a, a[:1]])


def layouts(i):
    f = {k: np.asarray(v) for k, v in i.items()}
    z = np.zeros
    pad_k = z((D, D), np.float32)
    pad_k[:, :P] = f["L0_xattn_Wk"].T
    mats = {"A0q": f["L0_xattn_Wq"].T, "A0o": f["L0_xattn_Wo"].T, "A0k": pad_k, "A0v": f["L0_xattn_Wv"].T,
            "B0q": f["L0_ffn_Wq"], "B0k": f["L0_ffn_Wk"], "B0v": f["L0_ffn_Wv"],
            "C1q": f["L1_xattn_Wq"].T, "C1k": f["L1_xattn_Wk"].T, "C1v": f["L1_xattn_Wv"].T,
            "D2q": f["L2_xattn_Wq"].T, "D2k": f["L2_xattn_Wk"].T, "D2v": f["L2_xattn_Wv"].T,
            "E3q": f["L3_xattn_q_w"].T, "E3k": f["L3_xattn_k_w"].T, "E3v": f["L3_xattn_v_w"].T}
    padded = {"B0p": f["L0_ffn_Wp"], "C1o": f["L1_xattn_Wo"].T, "D2o": f["L2_xattn_Wo"].T, "E3id": np.eye(D, dtype=np.float32)}
    pads = [by_heads(padded[n], NH, DH, QUARTER, NG) for n in PADDED[:-1]]
    pads.append(by_heads(f["L3_ffn_Wo"], HS, DS, P, HS))
    rows = {"B0v": f["L0_ffn_bv"], "B0p": f["L0_ffn_bp"], "C1o": f["L1_xattn_bo"], "D2v": f["L2_xattn_bv"], "D2o": f["L2_xattn_bo"],
            "E3v": f["L3_xattn_v_b"], "F3o": f["L3_ffn_bo"], "L2con": f["L2_ffn_b_con"], "L2down": f["L2_ffn_down_bias"]}
    rows.update({f"e{e}": f["L0_ffn_exp_b2"][e] for e in range(NE)})
    cols = {"B0q": f["L0_ffn_bq"], "B0k": f["L0_ffn_bk"], "D2q": f["L2_xattn_bq"], "D2k": f["L2_xattn_bk"], "E3q": f["L3_xattn_q_b"],
            "E3k": f["L3_xattn_k_b"], "ln1_g": f["L0_ffn_ln1_g"], "ln1_b": f["L0_ffn_ln1_b"], "ln2_g": f["L0_ffn_ln2_g"], "ln2_b": f["L0_ffn_ln2_b"]}
    w_exp = z((P, NM, D + 1), np.float32)
    w_exp[:, :, :D] = f["L2_ffn_W_exp"].T.reshape(NM, P, D).transpose(1, 0, 2)
    w_exp[:, :, D] = f["L2_ffn_b_exp"].reshape(NM, P).T
    up, down = f["L2_ffn_up_weights"].reshape(LOW + HIGH, -1), f["L2_ffn_down_weights"].reshape(LOW + HIGH, -1)
    low = z((MROW + 2, 2 * HID), np.float32)
    low[:2 * LOW] = np.concatenate([up[:LOW], down[:LOW][::-1]])
    high = [w[LOW:].reshape(HIGH, NM // 2, P, 4).transpose(2, 0, 1, 3).reshape(P, -1) for w in (up, down)]
    eye = np.eye(P, dtype=np.float32)
    k_, q_ = np.arange(P)[:, None], np.arange(P)[None, :]
    causal = np.stack([np.where(q_ > k_, -BIG, 0.0), np.where(k_ > q_, -BIG, 0.0)], 1).astype(np.float16)
    e4 = z((P, P), np.float32)
    for j in range(GH):
        e4[QUARTER * j + DH, QUARTER * j:QUARTER * (j + 1)] = 1.0
    e64 = z((TV, TV), np.float32)
    e64[DS] = 1.0
    kx = z((MROW + 2, len(XL), NH, TX), np.float16)
    kx[48, :, :, TC:] = -BIG
    kx[MROW:] = 1.0
    qs = z((MROW - 48, 2, GH, T), np.float16)
    qs[0] = BIG
    ks = z((MROW + 2 - 48, 2, GH, T), np.float16)
    ks[MROW - 48:] = 1.0
    eps = z((P, 3), np.float32)
    eps[:, 0] = EPS
    eps[:, 2] = -MAGIC
    a = {
        "x": with_next(f["x"]), "ctxT": with_next(f["ctx_1024"].transpose(0, 2, 1)), "mask": with_next(f["mask_BxS2_ik0"]),
        "wflat": np.concatenate([halves_of(mats[n]) for n in FLAT + CTXW], 1),
        "wpad": np.concatenate([p.transpose(1, 0, 2).reshape(P, -1) for p in pads], 1),
        "bcol": np.concatenate([cols[n].reshape(KD, P).T for n in BCOL] + [f["L2_ffn_up_bias"].reshape(NM, P).T,
                               f["L0_ffn_exp_b1"].reshape(NE * NM, P).T], 1),
        "brow": np.stack([rows[n] for n in BROW]),
        "gate_W": halves_of(f["L0_ffn_gate_W"]), "gate_b": f["L0_ffn_gate_b"].reshape(1, NE),
        "lam": np.concatenate([f["L0_xattn_lambda_" + n] for n in ("q1", "k1", "q2", "k2")]).reshape(1, -1),
        "exp_W1": f["L0_ffn_exp_W1"].reshape(NE, KD, P, HID).transpose(0, 2, 1, 3).reshape(NE, P, -1),
        "exp_W2": f["L0_ffn_exp_W2"].reshape(NE, NM, P, D).transpose(0, 2, 1, 3).reshape(NE, P, -1),
        "L1_W1": halves_of(f["L1_ffn_W1"].T), "L1_W2": f["L1_ffn_W2"].T.reshape(NM, P, D).transpose(1, 0, 2).reshape(P, -1),
        "L1_b1": f["L1_ffn_b1"].reshape(1, -1), "L1_b2": f["L1_ffn_b2"].reshape(1, -1),
        "W_exp": w_exp, "W_con": f["L2_ffn_W_con"].reshape(NM, P, D).transpose(1, 0, 2),
        "low_w": low, "high_w": np.concatenate(high, 1),
        "F3_W": np.concatenate([f["L3_ffn_" + n].reshape(KD, P, HID) for n in ("Wq", "Wk", "Wv")]).transpose(1, 0, 2),
        "F3_bqk": np.stack([f["L3_ffn_bq"], f["L3_ffn_bk"]], 1), "F3_bv": f["L3_ffn_bv"].reshape(1, -1),
        "F3_Wr": f["L3_ffn_Wr"].reshape(KD, P, NH).transpose(1, 0, 2), "F3_br": f["L3_ffn_br"].reshape(1, -1),
        "c_ident": eye, "c_ident16": eye.astype(np.float16), "c_causal": causal, "c_E4": e4, "c_E64": e64,
        "c_iota": np.tile(np.arange(NE, dtype=np.float32), (P, 1)), "c_eps": eps, "c_kx": kx, "c_qs": qs, "c_ks": ks,
    }
    return {k: np.ascontiguousarray(v) for k, v in a.items()}


def program(nc, arrays, known):
    args = {k: nc.dram_tensor(f"in_{k}", v.shape, mybir.dt.from_np(v.dtype), kind="ExternalInput").ap() for k, v in arrays.items()}
    out = nc.dram_tensor("out_0", (NB, T, D), F32, kind="ExternalOutput").ap()
    return build(nc, args, out, known)


def kernel(**inputs):
    import concourse.bacc as _bacc
    from concourse.bass_utils import run_bass_kernel_spmd as _run

    arrays = layouts(inputs)
    counted = program(_bacc.Bacc("TRN2", target_bir_lowering=False, num_devices=1), arrays, None)
    nc = _bacc.Bacc("TRN2", target_bir_lowering=False, num_devices=1)
    program(nc, arrays, counted)
    r = _run(nc, [{f"in_{k}": v for k, v in arrays.items()}], core_ids=[0])
    return r.results[0]["out_0"]
```
